# Optimizing a Trainium2 kernel written in Bass

```python
import numpy as np
import jax
import jax.numpy as jnp

def _softmax(x, axis=-1):
    return jax.nn.softmax(x, axis=axis)

def _gelu(x):
    return jax.nn.gelu(x, approximate=True)

def _silu(x):
    return jax.nn.silu(x)

def _sigmoid(x):
    return jax.nn.sigmoid(x)

def _layernorm(x, axis=-1, eps=1e-05):
    m = jnp.mean(x, axis=axis, keepdims=True)
    v = jnp.var(x, axis=axis, keepdims=True)
    return (x - m) / jnp.sqrt(v + eps)

def _scatter_add(tgt, idx, src, axis=0):
    return tgt.at[idx].add(src)

def _segment_sum(src, seg, n):
    return jax.ops.segment_sum(src, seg, n)
kernel_name = 'mk_early_fusion_d1_tok_img512_r4_073b1d'

def setup_inputs(seed: int=0):
    np.random.seed(seed)
    _w = jnp.asarray

    def _rec_inputs():
        import jax
        import jax.numpy as jnp
        _rk = jax.random.key(seed)
        x = -0.000178447 + 0.99995 * jax.random.normal(jax.random.fold_in(_rk, 1), (16, 3, 176, 208), jnp.float32)
        txt = -0.051393 + 1.14128 * jax.random.normal(jax.random.fold_in(_rk, 2), (16, 128, 128), jnp.float32)
        return (x, txt)
    x, txt = _rec_inputs()

    def _L0_tok_setup():
        import jax, jax.numpy as jnp
        import numpy as np
        P1, P2, C = (16, 16, 3)
        PW, PH = (176 // P1, 208 // P2)
        key = jax.random.key(seed)
        k1, k2, k3, k4, k5 = jax.random.split(key, 5)
        B, D = (64, 128)
        patch_dim = P1 * P2 * C
        return {'x': jax.random.normal(k1, (B, C, PW * P1, PH * P2), dtype=jnp.float32), 'W': jax.random.normal(k2, (D, patch_dim), dtype=jnp.float32) * 0.02, 'b': jax.random.normal(k3, (D,), dtype=jnp.float32) * 0.02, 'cls_token': jax.random.uniform(k4, (1, 1, D), dtype=jnp.float32), 'pos_emb': jax.random.normal(k5, (1, PW * PH + 1, 1), dtype=jnp.float32)}
    _L0_tok_all = _L0_tok_setup()
    _L0_tok_in = {k: v for k, v in _L0_tok_all.items() if k in ('W', 'b', 'cls_token', 'pos_emb')}
    del _L0_tok_all

    def _L0_attn_setup():
        import jax, jax.numpy as jnp
        import numpy as np
        B, T, DM = (2, 256, 128)
        DS, K = (16, 4)
        DI = DM * 2

        def _pscan(a, b):
            s = jnp.exp(jnp.cumsum(jnp.log(jnp.clip(a, 1e-06)), axis=1))
            return s * jnp.cumsum(b / (s + 1e-08), axis=1)

        def _forward(x, in_w, in_b, conv_w, conv_b, xp_w, xp_b, dt_w, dt_b, A_log, D_skip, out_w, out_b, ln_g, ln_b):
            res = x
            xz = x @ in_w.T + in_b
            x_, z = (xz[..., :DI], xz[..., DI:])
            xc = jax.lax.conv_general_dilated(x_.transpose(0, 2, 1), conv_w, window_strides=(1,), padding=[(K - 1, 0)], feature_group_count=DI, dimension_numbers=('NCH', 'OIH', 'NCH'))
            x_ = (xc + conv_b[None, :, None]).transpose(0, 2, 1)
            x_ = x_ * jax.nn.sigmoid(x_)
            bcd = x_ @ xp_w.T + xp_b
            B_s = bcd[..., :DS]
            C_s = bcd[..., DS:2 * DS]
            dt = jax.nn.softplus(bcd[..., 2 * DS:] @ dt_w.T + dt_b)
            A = -jnp.exp(A_log)
            dA = jnp.exp(dt[..., None] * A)
            dB = dt[..., None] * B_s[:, :, None, :]
            h = _pscan(dA, dB * x_[..., None])
            y = jnp.sum(h * C_s[:, :, None, :], axis=-1) + D_skip * x_
            o = y * (z * jax.nn.sigmoid(z)) @ out_w.T + out_b + res
            mu = jnp.mean(o, axis=-1, keepdims=True)
            var = jnp.mean(jnp.square(o - mu), axis=-1, keepdims=True)
            return (o - mu) / jnp.sqrt(var + 1e-05) * ln_g + ln_b
        key = jax.random.key(seed)
        ks = jax.random.split(key, 16)
        s = 0.02
        inp = {'x': jax.random.normal(ks[0], (B, T, DM), jnp.float32), 'in_w': jax.random.normal(ks[1], (2 * DI, DM), jnp.float32) * s, 'in_b': jnp.zeros((2 * DI,), jnp.float32), 'conv_w': jax.random.normal(ks[2], (DI, 1, K), jnp.float32) * s, 'conv_b': jnp.zeros((DI,), jnp.float32), 'xp_w': jax.random.normal(ks[3], (2 * DS + DI, DI), jnp.float32) * s, 'xp_b': jnp.zeros((2 * DS + DI,), jnp.float32), 'dt_w': jax.random.normal(ks[4], (DI, DI), jnp.float32) * s, 'dt_b': jnp.zeros((DI,), jnp.float32), 'A_log': jnp.log(jnp.broadcast_to(jnp.arange(1, DS + 1, dtype=jnp.float32)[None, :], (DI, DS))), 'D_skip': jnp.ones((DI,), jnp.float32), 'out_w': jax.random.normal(ks[5], (DM, DI), jnp.float32) * s, 'out_b': jnp.zeros((DM,), jnp.float32), 'ln_g': jnp.ones((DM,), jnp.float32), 'ln_b': jnp.zeros((DM,), jnp.float32)}
        return inp
    _L0_attn_all = _L0_attn_setup()
    _L0_attn_in = {k: v for k, v in _L0_attn_all.items() if k in ('in_w', 'in_b', 'conv_w', 'conv_b', 'xp_w', 'xp_b', 'dt_w', 'dt_b', 'A_log', 'D_skip', 'out_w', 'out_b', 'ln_g', 'ln_b')}
    del _L0_attn_all

    def _L0_ffn_setup():
        import jax, jax.numpy as jnp
        import numpy as np
        B, T, D = (4, 2048, 128)
        E, F, CAP = (8, 512, 1024)
        key = jax.random.key(seed)
        ks = jax.random.split(key, 6)
        s = 0.02
        return {'x': jax.random.normal(ks[0], (B, T, D), dtype=jnp.float32), 'Wr': jax.random.normal(ks[1], (D, E), dtype=jnp.float32) * s, 'W1': jax.random.normal(ks[2], (E, D, F), dtype=jnp.float32) * s, 'b1': jax.random.normal(ks[3], (E, F), dtype=jnp.float32) * s, 'W2': jax.random.normal(ks[4], (E, F, D), dtype=jnp.float32) * s, 'b2': jax.random.normal(ks[5], (E, D), dtype=jnp.float32) * s}
    _L0_ffn_all = _L0_ffn_setup()
    _L0_ffn_in = {k: v for k, v in _L0_ffn_all.items() if k in ('Wr', 'W1', 'b1', 'W2', 'b2')}
    del _L0_ffn_all
    return {'x': x, 'txt': txt, 'L0_tok_W': _L0_tok_in['W'], 'L0_tok_b': _L0_tok_in['b'], 'L0_tok_cls_token': _L0_tok_in['cls_token'], 'L0_tok_pos_emb': _L0_tok_in['pos_emb'], 'L0_attn_in_w': _L0_attn_in['in_w'], 'L0_attn_in_b': _L0_attn_in['in_b'], 'L0_attn_conv_w': _L0_attn_in['conv_w'], 'L0_attn_conv_b': _L0_attn_in['conv_b'], 'L0_attn_xp_w': _L0_attn_in['xp_w'], 'L0_attn_xp_b': _L0_attn_in['xp_b'], 'L0_attn_dt_w': _L0_attn_in['dt_w'], 'L0_attn_dt_b': _L0_attn_in['dt_b'], 'L0_attn_A_log': _L0_attn_in['A_log'], 'L0_attn_D_skip': _L0_attn_in['D_skip'], 'L0_attn_out_w': _L0_attn_in['out_w'], 'L0_attn_out_b': _L0_attn_in['out_b'], 'L0_attn_ln_g': _L0_attn_in['ln_g'], 'L0_attn_ln_b': _L0_attn_in['ln_b'], 'L0_ffn_Wr': _L0_ffn_in['Wr'], 'L0_ffn_W1': _L0_ffn_in['W1'], 'L0_ffn_b1': _L0_ffn_in['b1'], 'L0_ffn_W2': _L0_ffn_in['W2'], 'L0_ffn_b2': _L0_ffn_in['b2']}

def reference(x, txt, L0_tok_W, L0_tok_b, L0_tok_cls_token, L0_tok_pos_emb, L0_attn_in_w, L0_attn_in_b, L0_attn_conv_w, L0_attn_conv_b, L0_attn_xp_w, L0_attn_xp_b, L0_attn_dt_w, L0_attn_dt_b, L0_attn_A_log, L0_attn_D_skip, L0_attn_out_w, L0_attn_out_b, L0_attn_ln_g, L0_attn_ln_b, L0_ffn_Wr, L0_ffn_W1, L0_ffn_b1, L0_ffn_W2, L0_ffn_b2):
    import jax
    import jax.numpy as jnp

    def _L0_tok_ref(x, W, b, cls_token, pos_emb):
        import jax, jax.numpy as jnp
        import numpy as np
        P1, P2, C = (16, 16, 3)
        PW, PH = (176 // P1, 208 // P2)
        B = x.shape[0]
        patches = x.reshape(B, C, PW, P1, PH, P2)
        patches = patches.transpose(0, 2, 4, 3, 5, 1).reshape(B, PW * PH, P1 * P2 * C)
        proj = jnp.einsum('bnp,dp->bnd', patches, W) + b
        cls = jnp.broadcast_to(cls_token, (B, 1, cls_token.shape[-1]))
        out = jnp.concatenate([cls, proj], axis=1) + pos_emb
        return out

    def _L0_attn_ref(x, in_w, in_b, conv_w, conv_b, xp_w, xp_b, dt_w, dt_b, A_log, D_skip, out_w, out_b, ln_g, ln_b):
        import jax, jax.numpy as jnp
        import numpy as np
        B, T, DM = (2, 256, 128)
        DS, K = (16, 4)
        DI = DM * 2

        def _pscan(a, b):
            s = jnp.exp(jnp.cumsum(jnp.log(jnp.clip(a, 1e-06)), axis=1))
            return s * jnp.cumsum(b / (s + 1e-08), axis=1)

        def _forward(x, in_w, in_b, conv_w, conv_b, xp_w, xp_b, dt_w, dt_b, A_log, D_skip, out_w, out_b, ln_g, ln_b):
            res = x
            xz = x @ in_w.T + in_b
            x_, z = (xz[..., :DI], xz[..., DI:])
            xc = jax.lax.conv_general_dilated(x_.transpose(0, 2, 1), conv_w, window_strides=(1,), padding=[(K - 1, 0)], feature_group_count=DI, dimension_numbers=('NCH', 'OIH', 'NCH'))
            x_ = (xc + conv_b[None, :, None]).transpose(0, 2, 1)
            x_ = x_ * jax.nn.sigmoid(x_)
            bcd = x_ @ xp_w.T + xp_b
            B_s = bcd[..., :DS]
            C_s = bcd[..., DS:2 * DS]
            dt = jax.nn.softplus(bcd[..., 2 * DS:] @ dt_w.T + dt_b)
            A = -jnp.exp(A_log)
            dA = jnp.exp(dt[..., None] * A)
            dB = dt[..., None] * B_s[:, :, None, :]
            h = _pscan(dA, dB * x_[..., None])
            y = jnp.sum(h * C_s[:, :, None, :], axis=-1) + D_skip * x_
            o = y * (z * jax.nn.sigmoid(z)) @ out_w.T + out_b + res
            mu = jnp.mean(o, axis=-1, keepdims=True)
            var = jnp.mean(jnp.square(o - mu), axis=-1, keepdims=True)
            return (o - mu) / jnp.sqrt(var + 1e-05) * ln_g + ln_b
        return _forward(x, in_w, in_b, conv_w, conv_b, xp_w, xp_b, dt_w, dt_b, A_log, D_skip, out_w, out_b, ln_g, ln_b)

    def _L0_ffn_ref(x, Wr, W1, b1, W2, b2):
        import jax, jax.numpy as jnp
        import numpy as np
        B, T, D = (4, 2048, 128)
        E, F, CAP = (8, 512, 1024)
        Bb, Tt, Dd = x.shape
        N = Bb * Tt
        C = min(CAP, N)
        x_flat = x.reshape(N, Dd)
        logits = x_flat @ Wr
        probs = jax.nn.softmax(logits, axis=0)
        vals, idx = jax.lax.top_k(probs.T, C)
        selected = x_flat[idx]
        h = jax.nn.gelu(jnp.einsum('ecd,edf->ecf', selected, W1) + b1[:, None, :], approximate=False)
        out_e = jnp.einsum('ecf,efd->ecd', h, W2) + b2[:, None, :]
        weighted = vals[..., None] * out_e
        output = jnp.zeros_like(x_flat).at[idx.reshape(-1)].add(weighted.reshape(-1, Dd))
        return output.reshape(Bb, Tt, Dd)
    h = _L0_tok_ref(x, L0_tok_W, L0_tok_b, L0_tok_cls_token, L0_tok_pos_emb)
    h = jnp.concatenate([h, txt], axis=1)
    h = h + _L0_attn_ref(_layernorm(h, axis=-1), L0_attn_in_w, L0_attn_in_b, L0_attn_conv_w, L0_attn_conv_b, L0_attn_xp_w, L0_attn_xp_b, L0_attn_dt_w, L0_attn_dt_b, L0_attn_A_log, L0_attn_D_skip, L0_attn_out_w, L0_attn_out_b, L0_attn_ln_g, L0_attn_ln_b)
    h = h + _L0_ffn_ref(_layernorm(h, axis=-1), L0_ffn_Wr, L0_ffn_W1, L0_ffn_b1, L0_ffn_W2, L0_ffn_b2)
    return h

_drawn_inputs = setup_inputs


def setup_inputs(seed=0):
    import zlib

    import numpy as np

    out = dict(_drawn_inputs(seed))
    spreads = {'L0_attn_in_b': (0.0, 0.8),
     'L0_attn_conv_b': (0.0, 0.8),
     'L0_attn_xp_b': (0.0, 0.8),
     'L0_attn_dt_b': (0.0, 0.8),
     'L0_attn_D_skip': (1.0, 0.6),
     'L0_attn_out_b': (0.0, 0.497),
     'L0_attn_ln_g': (1.0, 0.2),
     'L0_attn_ln_b': (0.0, 0.1)}
    factors = {'L0_tok_b': 2.779,
     'L0_attn_in_w': 8.0,
     'L0_attn_conv_w': 8.0,
     'L0_attn_xp_w': 8.0,
     'L0_attn_dt_w': 8.0,
     'L0_attn_A_log': 8.0,
     'L0_attn_out_w': 8.0,
     'L0_ffn_Wr': 64.0,
     'L0_ffn_W1': 64.0,
     'L0_ffn_b1': 64.0,
     'L0_ffn_W2': 61.273,
     'L0_ffn_b2': 64.0}
    for name, (base, spread) in spreads.items():
        noise = np.random.default_rng([zlib.crc32(name.encode()), seed]).standard_normal(out[name].shape)
        drawn = base * np.exp(spread * noise) if base else spread * noise
        out[name] = jnp.asarray(drawn.astype(out[name].dtype))
    for name, factor in factors.items():
        out[name] = (out[name] * factor).astype(out[name].dtype)
    return out
```

```python
from contextlib import ExitStack

import concourse.bass as bass
from concourse import mybir

ALU = mybir.AluOpType
ACT = mybir.ActivationFunctionType
AX = mybir.AxisListType
F32 = mybir.dt.float32
BF16 = mybir.dt.bfloat16
I32 = mybir.dt.int32

P = 128
B = 16
NPATCH = 143
TI = NPATCH + 1
T = TI + 128
KT = 6
NH = 2
NS = 16
KC = 4
E = 8
FT = 4
CAP = 1024
CHUNK = 512
LOG_FLOOR = -13.815510557964274
LOG_EPS_HALF = 9.210340371976184
SERIES_BELOW = 1.0 / 128
NBITS = 30

S_GONE = -104.0

RANGES = [(0, 16, 16), (16, 48, 8), (64, T - 64, 2)]

V_INB, V_CB, V_DTIN, V_DTB, V_D, V_OUTB, V_LNG, V_LNB, V_EPS, V_LE, V_B1 = 0, 4, 6, 8, 10, 12, 13, 14, 15, 16, 17
V_B2 = V_B1 + E * FT
NV = V_B2 + E


def each_batch(eng, body):
    body(0, 0, True)
    body(1, 1, True)
    with eng.Fori(1, B // 2) as i:
        for s in range(2):
            body(i * 2 + s, s, False)


def skewed(eng, head, tail):
    head(0, 0, True)
    head(1, 1, True)
    tail(0, 0, True)
    head(2, 0, False)
    tail(1, 1, True)
    with eng.Fori(1, B // 2 - 1) as i:
        for s in range(2):
            head(i * 2 + s + 1, 1 - s, False)
            tail(i * 2 + s, s, False)
    head(B - 1, 1, False)
    tail(B - 2, 0, False)
    tail(B - 1, 1, False)


def nothing(*_):
    pass


def build_program(nc, patches, txt, tokw, tok_rows, tok_cols, vecs, inw, convw, xpw, xpb, dtw, alog, outw, wr,
                  w1, w2, ident_c, sel_c, group_c, below_c, mean_c, bits_i, bits_f, out):
    h_save = nc.dram_tensor("h_save", [P, B, T], F32, kind="Internal").ap()
    with ExitStack() as ctx:
        def sb(name, shape, dt=F32):
            return ctx.enter_context(nc.sbuf_tensor(name, shape, dt))

        def sem(name):
            return ctx.enter_context(nc.semaphore(name))

        bank = [ctx.enter_context(nc.psum_tensor(f"bank{i}", [P, 512], F32)) for i in range(8)]

        WORK = 10952
        work = sb("work", [P, WORK])
        xn = sb("xn", [P, B, T])
        xs = sb("xs", [P, B, NH, T])
        dt = sb("dt", [P, B, NH, T])
        dtx = sb("dtx", [P, B, NH, T])
        bc = sb("bc", [96, B, T], BF16)
        vec = sb("vec", [P, NV])
        hvec = sb("hvec", [P, NV])
        ident = sb("ident", [P, P])
        sel = sb("sel", [96, 32, P], BF16)
        meanm = sb("meanm", [P, P])
        diag = sb("diag", [P, NH, KC, P])
        xpb_s = sb("xpb_s", [32, 1])
        inw_s = sb("inw_s", [P, 2 * NH * P])
        xpw_s = sb("xpw_s", [P, NH, 32 + NH * P])
        dtw_s = sb("dtw_s", [P, NH, NH * P])
        outw_s = sb("outw_s", [P, NH, P])
        convw_s = sb("convw_s", [P, NH * KC])
        negA = sb("negA", [P, NH, NS])
        wr_s = sb("wr_s", [P, E])

        def view(arr, off, *shape, rows=P, dtype=F32):
            size = 1
            for d in shape:
                size *= d
            v = arr[0:rows, off:off + (size if dtype != BF16 else size // 2)]
            if dtype != F32:
                v = v.bitcast(dtype)
            names = "abcd"[:len(shape)]
            return v if len(shape) == 1 else v.rearrange(
                f"p ({' '.join(names)}) -> p {' '.join(names)}", **dict(zip(names, shape)))

        hT = view(work, 0, B, T)
        oT = dt[:, :, :, :].rearrange("p b h t -> p (b h t)")[:, 0:B * T].rearrange("p (b t) -> p b t", b=B)

        class Scratch:
            def __init__(self, off=B * T):
                self.off = off

            def take(self, *shape, **kw):
                size = 1
                for d in shape:
                    size *= d
                v = view(work, self.off, *shape, **kw)
                self.off += size if kw.get("dtype") != BF16 else size // 2
                assert self.off <= WORK, self.off
                return v

            def two(self, *shape, **kw):
                return [self.take(*shape, **kw) for _ in range(2)]

        def row(arr, b):
            return arr[:, bass.ds(b, 1), :].rearrange("p o t -> p (o t)")

        def both(arr, b):
            return arr[:, bass.ds(b, 1), :, :].rearrange("p o h t -> p (o h) t")

        stage_done = [sem(f"stage{k}_done") for k in range(9)]

        def fence(eng, k):
            eng.drain().then_inc(stage_done[k], 1)
            eng.wait_ge(stage_done[k], 4)

        passed = sem("passed")

        def apart(eng):
            eng.sem_inc(passed, 1)

        block = ctx.enter_context(nc.Block())

        consts_in, late_in, text_in, tok_mm, tok_ev = (
            sem(n) for n in ("consts_in", "late_in", "text_in", "tok_mm", "tok_ev"))
        pat_in = [sem(f"pat_in{s}") for s in range(2)]
        m = Scratch()
        pat = m.two(KT, TI)
        tokw_s = m.take(KT, P)
        tokr_s = m.take(P, rows=3)
        tokc_s = m.take(TI, rows=3)
        EARLY = [(vec[:, :], vecs), (tokw_s, tokw), (tokr_s, tok_rows), (tokc_s, tok_cols), (meanm[:, :], mean_c)]
        LATE = [(ident[:, :], ident_c), (inw_s[:, :], inw), (convw_s[:, :], convw), (xpw_s[:, :, :], xpw),
                (xpb_s[:, :], xpb), (dtw_s[:, :, :], dtw), (negA[:, :, :], alog), (outw_s[:, :, :], outw),
                (wr_s[:, :], wr), (sel[:, :, :], sel_c)]

        def tok_sync(sp):
            for dst, src in EARLY:
                sp.dma_start(dst, src).then_inc(consts_in, 16)

            def load(b, s, first):
                if not first:
                    sp.wait_ge(tok_mm, b - 1)
                sp.dma_start(pat[s], patches[bass.ds(b, 1)].rearrange("o p k n -> (o p) k n")).then_inc(pat_in[s], 16)
            each_batch(sp, load)

        def tok_pool(pool):
            pool.dma_start(hT[:, :, TI:T], txt).then_inc(text_in, 16)
            for dst, src in LATE:
                pool.dma_start(dst, src).then_inc(late_in, 16)

        def tok_pe(pe):
            pe.wait_ge(consts_in, 16 * len(EARLY))

            def tok(b, s, first):
                if not first:
                    pe.wait_ge(tok_ev, b - 1)
                nc.tensor.matmul(bank[s][:, 0:TI], tokr_s, tokc_s, start=True, stop=False)
                pe.wait_ge(pat_in[s], (b - s) * 8 + 16)
                for k in range(KT):
                    mm = nc.tensor.matmul(bank[s][:, 0:TI], tokw_s[:, k, :], pat[s][:, k, :], start=False,
                                          stop=(k == KT - 1))
                mm.then_inc(tok_mm, 1)
            each_batch(pe, tok)

        def tok_act(act):
            def evict(b, s, first):
                act.wait_ge(tok_mm, b + 1)
                nc.scalar.copy(row(hT, b)[:, 0:TI], bank[s][:, 0:TI]).then_inc(tok_ev, 1)
            each_batch(act, evict)
            act.wait_ge(text_in, 16)

        m = Scratch()
        ln_sq, ln_log, ln_rs = m.two(T), m.two(T), m.two(T)

        class LayerNorm:

            def __init__(self, name, src, dst):
                self.src, self.dst = src, dst
                self.mean, self.cent, self.sq, self.var, self.log, self.rstd, self.out = (
                    sem(f"{name}_{n}") for n in ("mean", "cent", "sq", "var", "log", "rstd", "out"))

            def pe(self, pe):
                def mean(b, s, first):
                    if not first:
                        pe.wait_ge(self.cent, b - 1)
                    nc.tensor.matmul(bank[s][:, 0:T], meanm[:, :], row(self.src, b), start=True,
                                     stop=True).then_inc(self.mean, 1)

                def var(b, s, first):
                    pe.wait_ge(self.sq, b + 1)
                    if not first:
                        pe.wait_ge(self.log, b - 1)
                    nc.tensor.matmul(bank[2 + s][:, 0:T], meanm[:, :], ln_sq[s], start=True,
                                     stop=True).then_inc(self.var, 1)
                skewed(pe, mean, var)

            def act(self, act):
                nc.scalar.preload_act_table_set("natural_log_exp_and_others")

                def square(b, s, first):
                    act.wait_ge(self.cent, b + 1)
                    if not first:
                        act.wait_ge(self.var, b - 1)
                    nc.scalar.activation(ln_sq[s], row(self.dst, b), ACT.Square).then_inc(self.sq, 1)

                def rstd(b, s, first):
                    act.wait_ge(self.var, b + 1)
                    nc.scalar.activation(ln_log[s], bank[2 + s][:, 0:T], ACT.Ln,
                                         bias=vec[:, V_EPS:V_EPS + 1]).then_inc(self.log, 1)
                    act.wait_ge(self.log, b + 1)
                    if not first:
                        act.wait_ge(self.out, b - 1)
                    nc.scalar.activation(ln_rs[s], ln_log[s], ACT.Exp, scale=-0.5).then_inc(self.rstd, 1)
                skewed(act, square, rstd)

            def dve(self, dve, finish=None):
                def center(b, s, first):
                    dve.wait_ge(self.mean, b + 1)
                    nc.vector.tensor_tensor(row(self.dst, b), row(self.src, b), bank[s][:, 0:T],
                                            ALU.subtract).then_inc(self.cent, 1)

                def scale(b, s, first):
                    dve.wait_ge(self.rstd, b + 1)
                    nc.vector.tensor_tensor(row(self.dst, b), row(self.dst, b), ln_rs[s],
                                            ALU.mult).then_inc(self.out, 1)
                    if finish:
                        finish(b, s, first)
                skewed(dve, center, scale)

        ln_in = LayerNorm("ln_in", hT, xn)

        in_mm, in_ev, conv_mm, conv_th, conv_half, conv_out = (
            sem(n) for n in ("in_mm", "in_ev", "conv_mm", "conv_th", "conv_half", "conv_out"))
        negA_exp, setup_ok, h_saved = sem("negA_exp"), sem("setup_ok"), sem("h_saved")
        m = Scratch()
        xpad, cth, chalf = m.two(NH, T + KC - 1), m.two(NH, T), m.two(NH, T)

        def conv_setup_dve(dve):
            dve.wait_ge(late_in, 16 * len(LATE))
            dve.wait_ge(consts_in, 16 * len(EARLY))
            for h in range(NH):
                for k in range(KC):
                    nc.vector.tensor_scalar(diag[:, h, k, :], ident[:, :], convw_s[:, h * KC + k:h * KC + k + 1],
                                            None, ALU.mult).then_inc(setup_ok, 1)
                nc.vector.memset(xpad[h][:, :, 0:KC - 1], 0.0).then_inc(setup_ok, 1)
            nc.vector.tensor_scalar(hvec[:, :], vec[:, :], 0.5, None, ALU.mult).then_inc(setup_ok, 1)
            dve.wait_ge(negA_exp, 1)
            nc.vector.tensor_scalar(negA[:, :, :], negA[:, :, :], -1.0, None, ALU.mult).then_inc(setup_ok, 1)

        SETUP = NH * (KC + 1) + 2

        def conv_pe(pe):
            pe.wait_ge(setup_ok, SETUP)

            def inproj(b, s, first):
                if not first:
                    pe.wait_ge(in_ev, b - 1)
                for h in range(NH):
                    mm = nc.tensor.matmul(bank[4 * s + h][:, 0:T], inw_s[:, h * P:(h + 1) * P], row(xn, b),
                                          start=True, stop=True)
                mm.then_inc(in_mm, 1)

            def conv(b, s, first):
                pe.wait_ge(in_ev, b + 1)
                if not first:
                    pe.wait_ge(conv_half, b - 1)
                for h in range(NH):
                    for k in range(KC):
                        mm = nc.tensor.matmul(bank[4 * s + 2 + h][:, 0:T], diag[:, h, k, :],
                                              xpad[s][:, h, k:k + T], start=(k == 0), stop=(k == KC - 1))
                mm.then_inc(conv_mm, 1)
            skewed(pe, inproj, conv)

        def conv_act(act):
            act.wait_ge(late_in, 16 * len(LATE))
            nc.scalar.activation(negA[:, :, :], negA[:, :, :], ACT.Exp).then_inc(negA_exp, 1)
            act.wait_ge(setup_ok, SETUP)

            def evict(b, s, first):
                act.wait_ge(in_mm, b + 1)
                if not first:
                    act.wait_ge(conv_mm, b - 1)
                for h in range(NH):
                    a = nc.scalar.activation(xpad[s][:, h, KC - 1:], bank[4 * s + h][:, 0:T], ACT.Identity,
                                             bias=vec[:, V_INB + h:V_INB + h + 1])
                a.then_inc(in_ev, 1)

            def gate(b, s, first):
                act.wait_ge(conv_mm, b + 1)
                if not first:
                    act.wait_ge(conv_out, b - 1)
                for h in range(NH):
                    a = nc.scalar.activation(cth[s][:, h, :], bank[4 * s + 2 + h][:, 0:T], ACT.Tanh, scale=0.5,
                                             bias=hvec[:, V_CB + h:V_CB + h + 1])
                a.then_inc(conv_th, 1)
                for h in range(NH):
                    a = nc.scalar.activation(chalf[s][:, h, :], bank[4 * s + 2 + h][:, 0:T], ACT.Identity, scale=0.5,
                                             bias=hvec[:, V_CB + h:V_CB + h + 1])
                a.then_inc(conv_half, 1)
            skewed(act, evict, gate)

        def conv_dve(dve):
            def silu(b, s, first):
                dve.wait_ge(conv_th, b + 1)
                dve.wait_ge(conv_half, b + 1)
                nc.vector.scalar_tensor_tensor(both(xs, b), cth[s], 1.0, chalf[s], ALU.add,
                                               ALU.mult).then_inc(conv_out, 1)
            each_batch(dve, silu)

        (xp_mm, dtin_ev, bcf_ev, dt_mm, dt_abs, dt_exp, dt_log, dt_relu, dt_ser, dt_mask, dt_sel, dt_ok, dtx_ok,
         bc_cp, bc_sub, bz) = (sem(n) for n in (
             "xp_mm", "dtin_ev", "bcf_ev", "dt_mm", "dt_abs", "dt_exp", "dt_log", "dt_relu", "dt_ser", "dt_mask",
             "dt_sel", "dt_ok", "dtx_ok", "bc_cp", "bc_sub", "bz"))
        m = Scratch()
        dtin, dexp, dlog, drel = m.two(NH, T), m.two(NH, T), m.two(NH, T), m.two(NH, T)
        dser, dmask = m.take(NH, T), m.take(NH, T, dtype=I32)
        bcf, bcr = m.two(T, rows=32), m.take(T, rows=32)
        bcq = m.take(T, rows=32, dtype=BF16)

        def steps_pe(pe):
            def xproj(b, s, first):
                if not first:
                    pe.wait_ge(bcf_ev, b - 1)
                    pe.wait_ge(dtin_ev, b - 1)
                for k in range(NH):
                    nc.tensor.matmul(bank[3 * s][0:32, 0:T], xpw_s[:, k, 0:32], both(xs, b)[:, k, :],
                                     start=(k == 0), stop=(k == NH - 1))
                for h in range(NH):
                    for k in range(NH):
                        mm = nc.tensor.matmul(bank[3 * s + 1 + h][:, 0:T], xpw_s[:, k, 32 + h * P:32 + (h + 1) * P],
                                              both(xs, b)[:, k, :], start=(k == 0), stop=(k == NH - 1))
                mm.then_inc(xp_mm, 1)

            def steps(b, s, first):
                pe.wait_ge(dtin_ev, b + 1)
                if not (isinstance(b, int) and b == 0):
                    pe.wait_ge(dt_relu, b)
                for h in range(NH):
                    for k in range(NH):
                        mm = nc.tensor.matmul(bank[6 + h][:, 0:T], dtw_s[:, k, h * P:(h + 1) * P],
                                              dtin[s][:, k, :], start=(k == 0), stop=(k == NH - 1))
                mm.then_inc(dt_mm, 1)
            skewed(pe, xproj, steps)

        def steps_act(act):
            nc.scalar.preload_act_table_set("natural_log_exp_and_others")

            def evict(b, s, first):
                act.wait_ge(xp_mm, b + 1)
                if not first:
                    act.wait_ge(dt_mm, b - 1)
                for h in range(NH):
                    a = nc.scalar.activation(dtin[s][:, h, :], bank[3 * s + 1 + h][:, 0:T], ACT.Identity,
                                             bias=vec[:, V_DTIN + h:V_DTIN + h + 1])
                a.then_inc(dtin_ev, 1)
                if not first:
                    act.wait_ge(bc_sub, 2 * b - 2)
                nc.scalar.activation(bcf[s], bank[3 * s][0:32, 0:T], ACT.Identity, bias=xpb_s[:, :]).then_inc(bcf_ev, 1)

            def softplus(b, s, first):
                act.wait_ge(dt_mm, b + 1)
                if not first:
                    act.wait_ge(dt_sel, b - 1)
                    act.wait_ge(dt_ok, b - 1)
                for h in range(NH):
                    a = nc.scalar.activation(dexp[s][:, h, :], bank[6 + h][:, 0:T], ACT.Abs,
                                             bias=vec[:, V_DTB + h:V_DTB + h + 1])
                a.then_inc(dt_abs, 1)
                act.wait_ge(dt_abs, b + 1)
                nc.scalar.activation(dexp[s], dexp[s], ACT.Exp, scale=-1.0).then_inc(dt_exp, 1)
                act.wait_ge(dt_exp, b + 1)
                nc.scalar.activation(dlog[s], dexp[s], ACT.Ln, bias=1.0).then_inc(dt_log, 1)
            skewed(act, evict, softplus)

        def steps_dve(dve):
            def one(b, s, first):
                dve.wait_ge(dt_abs, b + 1)
                for h in range(NH):
                    a = nc.vector.tensor_scalar(drel[s][:, h, :], bank[6 + h][:, 0:T],
                                                vec[:, V_DTB + h:V_DTB + h + 1], 0.0, ALU.add, ALU.max)
                a.then_inc(dt_relu, 1)
                dve.wait_ge(dt_exp, b + 1)
                nc.vector.tensor_scalar(dser, dexp[s], 1.0 / 3, -0.5, ALU.mult, ALU.add).then_inc(dt_ser, 1)
                nc.vector.tensor_scalar(dmask, dexp[s], SERIES_BELOW, None, ALU.is_lt).then_inc(dt_mask, 1)
                dve.wait_ge(dt_ser, 3 * b + 1)
                nc.vector.tensor_tensor(dser, dser, dexp[s], ALU.mult).then_inc(dt_ser, 1)
                dve.wait_ge(dt_ser, 3 * b + 2)
                nc.vector.scalar_tensor_tensor(dser, dser, 1.0, dexp[s], ALU.add, ALU.mult).then_inc(dt_ser, 1)
                dve.wait_ge(dt_ser, 3 * b + 3)
                dve.wait_ge(dt_mask, b + 1)
                dve.wait_ge(dt_log, b + 1)
                apart(dve)
                nc.vector.copy_predicated(dlog[s], dmask, dser).then_inc(dt_sel, 1)
                dve.wait_ge(dt_sel, b + 1)
                nc.vector.tensor_tensor(both(dt, b), dlog[s], drel[s], ALU.add).then_inc(dt_ok, 1)
            each_batch(dve, one)

        def steps_pool(pool):
            def one(b, s, first):
                pool.wait_ge(bcf_ev, b + 1)
                apart(pool)
                nc.gpsimd.tensor_copy(row(bc, b)[0:32, :], bcf[s]).then_inc(bc_cp, 1)
                pool.wait_ge(bc_cp, 3 * b + 1)
                apart(pool)
                nc.gpsimd.tensor_tensor(bcr, bcf[s], row(bc, b)[0:32, :], ALU.subtract).then_inc(bc_sub, 1)
                pool.wait_ge(bc_sub, 2 * b + 1)
                apart(pool)
                nc.gpsimd.tensor_copy(bcq, bcr).then_inc(bc_cp, 1)
                pool.wait_ge(bc_cp, 3 * b + 2)
                apart(pool)
                nc.gpsimd.tensor_copy(row(bc, b)[32:64, :], bcq).then_inc(bc_cp, 1)
                nc.gpsimd.tensor_tensor(row(bc, b)[64:96, :], bcr, bcq, ALU.subtract).then_inc(bc_sub, 1)
                pool.wait_ge(bc_cp, 3 * b + 3)
                pool.wait_ge(bc_sub, 2 * b + 2)
                pool.wait_ge(dt_ok, b + 1)
                apart(pool)
                nc.gpsimd.tensor_tensor(both(dtx, b), both(dt, b), both(xs, b), ALU.mult).then_inc(dtx_ok, 1)
            each_batch(pool, one)

        TILE = max(NH * g * (1 + tl) for _, tl, g in RANGES)
        m = Scratch(0)
        s_mask, s_u = m.take(TILE), m.take(TILE)
        s_a, s_L, s_w = m.two(TILE), m.two(TILE), m.two(TILE)
        s_c = m.two(512)
        carryL, carryH = m.take(NS, B * NH), m.take(NS, B * NH)
        s_max, s_dead, ones_c = m.take(NS), m.take(NS), m.take(1)
        alive = [m.take(NS, rows=1, dtype=I32) for _ in RANGES]
        alive4 = [m.take(NS // 4, rows=1, dtype=I32) for _ in RANGES]
        S = {n: sem(f"scan_{n}") for n in ("bmm", "cmm", "ccopy", "clip", "logsum", "logtail", "decay", "gate", "src",
                                           "inp", "state", "tail", "out", "added")}
        OF = {"pe": ("bmm", "cmm"), "act": ("ccopy", "decay", "gate"), "pool": ("out", "added"),
              "dve": ("clip", "logsum", "logtail", "src", "inp", "state", "tail")}
        s_zero, s_pads, s_skip, s_flag, s_count = (
            sem(n) for n in ("scan_zero", "scan_pads", "scan_skip", "scan_flag", "scan_count"))
        s_yD = sem("scan_yD")
        LAST = len(RANGES) - 1

        def tiles_before(r):
            return sum(B // gb * NS for _, _, gb in RANGES[:r])

        def scan_starts(eng, who):
            for n in OF[who]:
                eng.sem_inc(S[n], 2)

        def until(eng, name, k):
            eng.wait_ge(S[name], k + 3)

        class Tile:

            def __init__(self, r, n, g, s):
                self.t0, self.tl, self.gb = RANGES[r]
                self.carried, self.carries = r > 0, r < LAST
                self.k = tiles_before(r) + n * (B // self.gb) + g
                self.g, self.n, self.s = g, n, s
                self.segs = self.gb * NH

            def flat(self, buf):
                return buf[:, 0:self.segs * (1 + self.tl)]

            def seg(self, buf):
                return self.flat(buf).rearrange("p (s t) -> p s t", s=self.segs)

            def body(self, buf):
                return self.seg(buf)[:, :, 1:]

            def body_bh(self, buf):
                return self.seg(buf).rearrange("p (b h) t -> p b h t", h=NH)[:, :, :, 1:]

            def array(self, arr):
                return arr[:, bass.ds(self.g * self.gb, self.gb), :, self.t0:self.t0 + self.tl]

            def rows_bc(self):
                return bc[:, bass.ds(self.g * self.gb, self.gb), self.t0:self.t0 + self.tl]

            def per_token(self, ap):
                return ap[:, 0:self.gb * self.tl].rearrange("p (b o t) -> p b o t", b=self.gb, o=1).to_broadcast(
                    [P, self.gb, NH, self.tl])

            def carry(self, arr):
                return arr[:, bass.ds(self.n, 1), bass.ds(self.g * self.segs, self.segs)].rearrange("p o s -> p (o s)")

        def tiles(eng, who, before_range, head, tail):
            def run(r, tile, count):
                head(tile(0, 0))
                if count > 2:
                    with eng.Fori(0, count // 2 - 1) as i:
                        for s in range(2):
                            head(tile(i * 2 + s + 1, 1 - s))
                            tail(tile(i * 2 + s, s))
                head(tile(count - 1, 1))
                tail(tile(count - 2, 0))
                tail(tile(count - 1, 1))

            before_range(0)
            run(0, lambda n, s: Tile(0, n, 0, s), NS)
            for r in range(1, len(RANGES)):
                before_range(r)
                eng.wait_ge(s_flag, 2 * r)
                groups = B // RANGES[r][2]

                def skip(states):
                    eng.drain().then_inc(s_skip, 1)
                    for name in OF[who]:
                        eng.sem_inc(S[name], states * groups)

                with eng.Fori(0, NS // 4) as q:
                    with eng.If(eng.value_load(alive4[r][0:1, bass.ds(q, 1)], min_val=0, max_val=P) != 0):
                        with eng.Fori(0, 4) as j:
                            n = eng.snap(q * 4 + j)
                            with eng.If(eng.value_load(alive[r][0:1, bass.ds(n, 1)], min_val=0, max_val=P) != 0):
                                run(r, lambda g, s: Tile(r, n, g, s), groups)
                            with eng.Else():
                                skip(1)
                    with eng.Else():
                        skip(4)

        def scan_pe(pe):
            scan_starts(pe, "pe")

            def count_dead(r):
                if r:
                    pe.wait_ge(s_count, 2 * r - 1)
                    nc.tensor.matmul(bank[4][0:1, 0:NS], ones_c, s_dead, start=True, stop=True).then_inc(s_count, 1)

            def spread(x):
                n = x.gb * x.tl
                until(pe, "src", x.k - 2)
                nc.tensor.matmul(bank[x.s][:, 0:n], sel[:, bass.ds(x.n, 1), :].rearrange("p o m -> p (o m)"),
                                 x.rows_bc(), start=True, stop=True).then_inc(S["bmm"], 1)
                until(pe, "ccopy", x.k - 2)
                nc.tensor.matmul(bank[2 + x.s][:, 0:n],
                                 sel[:, bass.ds(x.n + NS, 1), :].rearrange("p o m -> p (o m)"),
                                 x.rows_bc(), start=True, stop=True).then_inc(S["cmm"], 1)
            tiles(pe, "pe", count_dead, spread, nothing)

        def scan_act(act):
            scan_starts(act, "act")
            act.wait_ge(h_saved, 16)

            def head(x):
                until(act, "clip", x.k)
                until(act, "state", x.k - 2)
                nc.scalar.activation(x.body(s_a[x.s]), x.body(s_u), ACT.Exp).then_inc(S["decay"], 1)
                until(act, "logtail" if x.carries else "logsum", x.k)
                nc.scalar.activation(x.flat(s_L[x.s]), x.flat(s_L[x.s]), ACT.Tanh, scale=0.5,
                                     bias=vec[:, V_LE:V_LE + 1]).then_inc(S["gate"], 1)
                until(act, "cmm", x.k)
                until(act, "out", x.k - 2)
                nc.scalar.copy(s_c[x.s][:, 0:x.gb * x.tl], bank[2 + x.s][:, 0:x.gb * x.tl]).then_inc(S["ccopy"], 1)
            tiles(act, "act", nothing, head, nothing)

        def scan_dve(dve):
            scan_starts(dve, "dve")
            dve.wait_ge(h_saved, 16)

            def before_range(r):
                t = Tile(r, 0, 0, 0)
                if r:
                    until(dve, "added", t.k - 1)
                    nc.vector.tensor_reduce(s_max, carryL, AX.X, ALU.max).then_inc(s_zero, 1)
                    dve.wait_ge(s_zero, 8 * r + 1)
                    nc.vector.tensor_scalar(s_dead, s_max, S_GONE, None, ALU.is_le).then_inc(s_count, 1)
                    dve.wait_ge(s_count, 2 * r)
                    nc.vector.tensor_scalar(alive[r], bank[4][0:1, 0:NS], -1.0, float(P), ALU.mult,
                                            ALU.add).then_inc(s_flag, 1)
                    dve.wait_ge(s_flag, 2 * r - 1)
                    nc.vector.tensor_reduce(alive4[r], alive[r].rearrange("p (q j) -> p q j", j=4), AX.X,
                                            ALU.max).then_inc(s_flag, 1)
                nc.vector.memset(t.flat(s_mask), 1.0).then_inc(s_zero, 1)
                dve.wait_ge(s_zero, 8 * r + (2 if r else 1))
                for buf in (s_mask, *s_a, s_u, *s_w):
                    nc.vector.memset(t.seg(buf)[:, :, 0:1], 0.0).then_inc(s_zero, 1)
                if not r:
                    nc.vector.memset(ones_c, 1.0).then_inc(s_zero, 1)
                    for h in range(NH):
                        a = nc.vector.tensor_scalar(xs[:, :, h, :], xs[:, :, h, :], vec[:, V_D + h:V_D + h + 1], None,
                                                    ALU.mult)
                    a.then_inc(s_yD, 1)
                dve.wait_ge(s_zero, 8 * r + 8)

            def head(x):
                until(dve, "decay", x.k - 1)
                until(dve, "logsum", x.k - 1)
                if x.carried:
                    nc.vector.tensor_scalar(x.seg(s_u)[:, :, 0:1], x.carry(carryL).rearrange(
                        "p (s o) -> p s o", o=1), 1.0, None, ALU.mult).then_inc(s_pads, 1)
                for h in range(NH):
                    a = nc.vector.tensor_scalar(x.body_bh(s_u)[:, :, h, :], x.array(dt)[:, :, h, :],
                                                negA[:, h, bass.ds(x.n, 1)], LOG_FLOOR, ALU.mult, ALU.max)
                a.then_inc(S["clip"], 1)
                until(dve, "clip", x.k)
                until(dve, "inp", x.k - 2)
                nc.vector.tensor_tensor_scan(x.flat(s_L[x.s]), x.flat(s_mask), x.flat(s_u), 0.0, ALU.mult,
                                             ALU.add).then_inc(S["logsum"], 1)
                if x.carries:
                    until(dve, "logsum", x.k)
                    nc.vector.tensor_scalar(x.carry(carryL), x.seg(s_L[x.s])[:, :, x.tl:].rearrange(
                        "p s o -> p (s o)"), 1.0, None, ALU.mult).then_inc(S["logtail"], 1)

            def tail(x):
                until(dve, "bmm", x.k)
                until(dve, "added", x.k - 2)
                nc.vector.tensor_tensor(x.body_bh(s_w[x.s]), x.array(dtx), x.per_token(bank[x.s]),
                                        ALU.mult).then_inc(S["src"], 1)
                if x.carried:
                    nc.vector.tensor_scalar(x.seg(s_w[x.s])[:, :, 0:1], x.carry(carryH).rearrange(
                        "p (s o) -> p s o", o=1), 1.0, None, ALU.mult).then_inc(s_pads, 1)
                until(dve, "gate", x.k)
                until(dve, "src", x.k)
                nc.vector.scalar_tensor_tensor(x.body(s_w[x.s]), x.body(s_L[x.s]), 1.0, x.body(s_w[x.s]), ALU.add,
                                               ALU.mult).then_inc(S["inp"], 1)
                until(dve, "decay", x.k)
                until(dve, "inp", x.k)
                nc.vector.tensor_tensor_scan(x.flat(s_w[x.s]), x.flat(s_a[x.s]), x.flat(s_w[x.s]), 0.0, ALU.mult,
                                             ALU.add).then_inc(S["state"], 1)
                if x.carries:
                    until(dve, "state", x.k)
                    nc.vector.tensor_scalar(x.carry(carryH), x.seg(s_w[x.s])[:, :, x.tl:].rearrange(
                        "p s o -> p (s o)"), 1.0, None, ALU.mult).then_inc(S["tail"], 1)
            tiles(dve, "dve", before_range, head, tail)

        def scan_pool(pool):
            scan_starts(pool, "pool")
            pool.wait_ge(s_yD, 1)

            def sum_up(x):
                until(pool, "tail" if x.carries else "state", x.k)
                until(pool, "ccopy", x.k)
                apart(pool)
                nc.gpsimd.tensor_tensor(x.body_bh(s_w[x.s]), x.body_bh(s_w[x.s]), x.per_token(s_c[x.s]),
                                        ALU.mult).then_inc(S["out"], 1)
                until(pool, "out", x.k)
                until(pool, "added", x.k - 1)
                apart(pool)
                nc.gpsimd.tensor_tensor(x.array(xs), x.array(xs), x.body_bh(s_w[x.s]), ALU.add).then_inc(S["added"], 1)
            tiles(pool, "pool", nothing, nothing, sum_up)

        z_mm, z_th, z_half, z_silu, yz_ok, o_mm, o_ok, h_back = (
            sem(n) for n in ("z_mm", "z_th", "z_half", "z_silu", "yz_ok", "o_mm", "o_ok", "h_back"))
        m = Scratch()
        zth, zhalf = m.two(NH, T), m.two(NH, T)

        def gate_pe(pe):
            def z(b, s, first):
                if not first:
                    pe.wait_ge(z_half, b - 1)
                for h in range(NH):
                    mm = nc.tensor.matmul(bank[2 * s + h][:, 0:T], inw_s[:, (NH + h) * P:(NH + h + 1) * P],
                                          row(xn, b), start=True, stop=True)
                mm.then_inc(z_mm, 1)

            def outproj(b, s, first):
                pe.wait_ge(yz_ok, b + 1)
                if not first:
                    pe.wait_ge(o_ok, b - 1)
                for k in range(NH):
                    mm = nc.tensor.matmul(bank[4 + s][:, 0:T], outw_s[:, k, :], both(dtx, b)[:, k, :],
                                          start=(k == 0), stop=(k == NH - 1))
                mm.then_inc(o_mm, 1)
            skewed(pe, z, outproj)

        def gate_act(act):
            def one(b, s, first):
                act.wait_ge(z_mm, b + 1)
                if not first:
                    act.wait_ge(z_silu, b - 1)
                for h in range(NH):
                    a = nc.scalar.activation(zth[s][:, h, :], bank[2 * s + h][:, 0:T], ACT.Tanh, scale=0.5,
                                             bias=hvec[:, V_INB + NH + h:V_INB + NH + h + 1])
                a.then_inc(z_th, 1)
                for h in range(NH):
                    a = nc.scalar.activation(zhalf[s][:, h, :], bank[2 * s + h][:, 0:T], ACT.Identity, scale=0.5,
                                             bias=hvec[:, V_INB + NH + h:V_INB + NH + h + 1])
                a.then_inc(z_half, 1)
            each_batch(act, one)

        def gate_dve(dve):
            def silu(b, s, first):
                dve.wait_ge(z_th, b + 1)
                dve.wait_ge(z_half, b + 1)
                nc.vector.scalar_tensor_tensor(both(dtx, b), zth[s], 1.0, zhalf[s], ALU.add,
                                               ALU.mult).then_inc(z_silu, 1)
                dve.wait_ge(z_silu, b + 1)
                nc.vector.tensor_tensor(both(dtx, b), both(dtx, b), both(xs, b), ALU.mult).then_inc(yz_ok, 1)

            def residual(b, s, first):
                dve.wait_ge(o_mm, b + 1)
                nc.vector.scalar_tensor_tensor(row(oT, b), bank[4 + s][:, 0:T], vec[:, V_OUTB:V_OUTB + 1],
                                               row(xn, b), ALU.add, ALU.add).then_inc(o_ok, 1)
            skewed(dve, silu, residual)

        ln_blk = LayerNorm("ln_blk", oT, oT)
        aff_ok, h2_ok = sem("aff_ok"), sem("h2_ok")

        def block_dve(dve):
            def add(b, s, first):
                dve.wait_ge(ln_blk.out, b + 1)
                nc.vector.tensor_scalar(row(oT, b), row(oT, b), vec[:, V_LNG:V_LNG + 1], vec[:, V_LNB:V_LNB + 1],
                                        ALU.mult, ALU.add).then_inc(aff_ok, 1)
                dve.wait_ge(aff_ok, b + 1)
                nc.vector.tensor_tensor(row(hT, b), row(hT, b), row(oT, b), ALU.add).then_inc(h2_ok, 1)
            dve.wait_ge(h_back, 16)
            ln_blk.dve(dve, finish=add)

        ln_moe = LayerNorm("ln_moe", hT, xn)

        bigx = xs[:, :, :, :].rearrange("p b h t -> p (b h t)")
        bigd = dt[:, :, :, :].rearrange("p b h t -> p (b h t)")
        bigy = dtx[:, :, :, :].rearrange("p b h t -> p (b h t)")
        lg_mm, lg_ev, lg_moved, rt_in, rt_pe, rt_dve, rt_act, rt_cand, wt_moved, w_in = (
            sem(n) for n in ("lg_mm", "lg_ev", "lg_moved", "rt_in", "rt_pe", "rt_dve", "rt_act", "rt_cand", "wt_moved",
                             "w_in"))
        lg = view(bigy, 0, B, T, rows=E)
        wrow = view(bigy, 0, B * T, rows=32)
        wq = view(bigy, B * T, B * T, rows=32, dtype=BF16)
        wsp = bc[:, :, :].rearrange("p b t -> p (b t)")
        lgr = view(bigx, 0, T)
        prob, flag, pick, ones_t = (view(bigx, T * i, T) for i in (1, 2, 3, 4))
        group, below = view(bigx, T * 5, P), view(bigx, T * 5 + P, P)
        bitI, bitF = view(bigx, T * 5 + 2 * P, NBITS, dtype=I32), view(bigx, T * 5 + 2 * P + 32, NBITS)
        sm = view(bigx, T * 5 + 2 * P + 64, 32)
        smi = sm.bitcast(I32)
        rowv = view(bigx, T * 5 + 2 * P + 96, P, rows=1)
        rowe = view(bigx, T * 5 + 3 * P + 96, E, rows=1)
        rowx = view(bigx, T * 5 + 3 * P + 96 + E, P, rows=1)
        C_MAX, C_NEG, C_SUM, C_INV, C_THR, C_CNT, C_ADD, C_CAND, C_GT, C_EQ, C_PRI, C_NEED = range(12)

        def col(c):
            return sm[:, c:c + 1]

        def coli(c):
            return smi[:, c:c + 1]

        def logits_pe(pe):
            def one(b, s, first):
                if not first:
                    pe.wait_ge(lg_ev, b - 1)
                nc.tensor.matmul(bank[s][0:E, 0:T], wr_s[:, :], row(xn, b), start=True, stop=True).then_inc(lg_mm, 1)
            each_batch(pe, one)

        def logits_act(act):
            def one(b, s, first):
                act.wait_ge(lg_mm, b + 1)
                nc.scalar.copy(row(lg, b), bank[s][0:E, 0:T]).then_inc(lg_ev, 1)
            each_batch(act, one)

        def route_sync(sp):
            sp.wait_ge(lg_ev, B)
            for e in range(E):
                sp.dma_start(lgr[e * B:(e + 1) * B, :], lg[e:e + 1, :, :]).then_inc(lg_moved, 16)
            sp.wait_ge(rt_dve, R_WEIGHTS)
            for e in range(E):
                sp.dma_start(wrow[NS + e:NS + e + 1, :].rearrange("e (b t) -> e b t", b=B),
                             pick[e * B:(e + 1) * B, :]).then_inc(wt_moved, 16)

        R_BITS = 8
        R_WEIGHTS = R_BITS + 3 * NBITS + 11

        def route_pe(pe):
            n = [0]

            def mm(out_, lhsT, rhs, ve, ac=0):
                pe.wait_ge(rt_dve, ve)
                if ac:
                    pe.wait_ge(rt_act, ac)
                n[0] += 1
                nc.tensor.matmul(out_, lhsT, rhs, start=True, stop=True).then_inc(rt_pe, 1)
            pe.wait_ge(rt_in, 16 * 4)
            pe.wait_ge(rt_dve, 2)
            nc.tensor.transpose(bank[4][0:1, 0:P], col(C_MAX), ident[:, :]).then_inc(rt_pe, 1)
            mm(bank[5][:, 0:1], rowx[:, :], ident[0:1, 0:1], 4)
            mm(bank[6][:, 0:1], group, col(C_SUM), 5, 1)
            with pe.Fori(0, NBITS) as i:
                pe.wait_ge(rt_dve, i * 3 + (R_BITS + 1))
                nc.tensor.matmul(bank[7][:, 0:1], group, col(C_CNT), start=True, stop=True).then_inc(rt_pe, 1)
            base = R_BITS + 3 * NBITS
            mm(bank[4][:, 0:1], group, col(C_GT), base + 2)
            mm(bank[5][:, 0:1], below, col(C_EQ), base + 4)

        def route_act(act):
            act.wait_ge(rt_dve, 5)
            nc.scalar.activation(prob, lgr, ACT.Exp, bias=col(C_NEG), accum_out=col(C_SUM)).then_inc(rt_act, 1)

        def route_dve(dve):
            n = [0]

            def did(ins):
                n[0] += 1
                ins.then_inc(rt_dve, 1)
                dve.wait_ge(rt_dve, n[0])
            dve.wait_ge(rt_in, 16 * 4)
            did(nc.vector.memset(ones_t, 1.0))
            dve.wait_ge(lg_moved, 16 * E)
            did(nc.vector.tensor_reduce(col(C_MAX), lgr, AX.X, ALU.max))
            dve.wait_ge(rt_pe, 1)
            did(nc.vector.tensor_reduce(rowe, bank[4][0:1, 0:P].rearrange("p (e b) -> p e b", e=E), AX.X,
                                        ALU.max))
            did(nc.vector.tensor_copy(rowx.rearrange("p (e b) -> p e b", e=E),
                                      rowe.rearrange("p (e o) -> p e o", o=1).to_broadcast([1, E, B])))
            dve.wait_ge(rt_pe, 2)
            did(nc.vector.tensor_scalar(col(C_NEG), bank[5][:, 0:1], -1.0, None, ALU.mult))
            dve.wait_ge(rt_pe, 3)
            did(nc.vector.reciprocal(col(C_INV), bank[6][:, 0:1]))
            did(nc.vector.tensor_scalar(prob, prob, col(C_INV), None, ALU.mult))
            did(nc.vector.memset(coli(C_THR), 0))
            assert n[0] == R_BITS
            with dve.Fori(0, NBITS) as i:
                nc.vector.tensor_tensor(coli(C_CAND), coli(C_THR), bitI[:, bass.ds(i, 1)],
                                        ALU.bitwise_or).then_inc(rt_cand, 1)
                dve.wait_ge(rt_cand, i + 1)
                nc.vector.tensor_scalar(flag, prob, col(C_CAND), None, ALU.is_ge, ALU.add,
                                        accum_out=col(C_CNT)).then_inc(rt_dve, 1)
                dve.wait_ge(rt_pe, i + 4)
                nc.vector.tensor_scalar(coli(C_ADD), bank[7][:, 0:1], float(CAP), bitF[:, bass.ds(i, 1)], ALU.is_ge,
                                        ALU.mult).then_inc(rt_dve, 1)
                dve.wait_ge(rt_dve, i * 3 + (R_BITS + 2))
                nc.vector.tensor_tensor(coli(C_THR), coli(C_THR), coli(C_ADD), ALU.bitwise_or).then_inc(rt_dve, 1)
                dve.wait_ge(rt_dve, i * 3 + (R_BITS + 3))
            n[0] += 3 * NBITS
            did(nc.vector.tensor_scalar(flag, prob, col(C_THR), None, ALU.is_gt))
            did(nc.vector.tensor_reduce(col(C_GT), flag, AX.X, ALU.add))
            did(nc.vector.tensor_scalar(lgr, prob, col(C_THR), None, ALU.is_equal))
            did(nc.vector.tensor_reduce(col(C_EQ), lgr, AX.X, ALU.add))
            did(nc.vector.tensor_tensor_scan(pick, ones_t, lgr, 0.0, ALU.mult, ALU.add))
            dve.wait_ge(rt_pe, 3 + NBITS + 2)
            did(nc.vector.tensor_scalar(pick, pick, bank[5][:, 0:1], bank[4][:, 0:1], ALU.add, ALU.add))
            did(nc.vector.tensor_scalar(pick, pick, float(CAP), None, ALU.is_le))
            did(nc.vector.tensor_tensor(pick, pick, lgr, ALU.mult))
            did(nc.vector.tensor_tensor(pick, pick, flag, ALU.add))
            did(nc.vector.tensor_tensor(pick, pick, prob, ALU.mult))
            did(nc.vector.memset(wrow, 0.0))
            assert n[0] == R_WEIGHTS
            dve.wait_ge(wt_moved, 16 * E)
            did(nc.vector.tensor_copy(wsp[0:32, :], wrow))
            did(nc.vector.tensor_tensor(wrow, wrow, wsp[0:32, :], ALU.subtract))
            did(nc.vector.tensor_copy(wq, wrow))
            did(nc.vector.tensor_copy(wsp[32:64, :], wq))
            did(nc.vector.tensor_tensor(wsp[64:96, :], wrow, wq, ALU.subtract))

        hid = [view(bigx, 2600 + i * FT * CHUNK, FT, CHUNK) for i in range(2)]
        w1_s = view(bigd, 0, E, FT * P)
        w2_s = view(bigd, E * FT * P, E, FT * P)
        part = [view(bigx, 2600 + 2 * FT * CHUNK + s * CHUNK, CHUNK) for s in range(2)]
        M = {n: sem(f"moe_{n}") for n in ("hid", "gelu", "out", "wmm", "oev", "scaled", "added")}
        stored = sem("stored")
        hflat = work[:, 0:B * T]
        xflat = xn[:, :, :].rearrange("p b t -> p (b t)")

        def experts(eng, before, head, tail, after):
            def chunk(c, n):
                before(c, n)
                head(c, n, 0, 0)
                for e in range(E):
                    if e + 1 < E:
                        head(c, n, e + 1, (e + 1) % 2)
                    tail(c, n, e, e % 2)
                after(c, n)
            with eng.Fori(0, B * T // CHUNK) as c:
                chunk(c, CHUNK)
            chunk(B * T // CHUNK, B * T % CHUNK)

        def tokens(arr, c, n):
            return arr[:, bass.ds(c * CHUNK, n)]

        def moe_pe(pe):
            pe.wait_ge(w_in, 32)

            def hidden(c, n, e, s):
                k = c * E + e
                for f in range(FT):
                    pe.wait_ge(M["gelu"], k * FT + (f + 1))
                    nc.tensor.matmul(bank[f][:, 0:n], w1_s[:, bass.ds(e, 1), f * P:(f + 1) * P].rearrange(
                        "p o m -> p (o m)"), tokens(xflat, c, n), start=True, stop=True).then_inc(M["hid"], 1)

            def outputs(c, n, e, s):
                k = c * E + e
                pe.wait_ge(M["scaled"], k + 1)
                nc.tensor.matmul(bank[6 + s][:, 0:n], sel[:, bass.ds(e + NS, 1), :].rearrange("p o m -> p (o m)"),
                                 tokens(wsp, c, n), start=True, stop=True).then_inc(M["wmm"], 1)
                pe.wait_ge(M["oev"], k + 1)
                for f in range(FT):
                    pe.wait_ge(M["gelu"], k * FT + (f + 1 + FT))
                    mm = nc.tensor.matmul(bank[4 + s][:, 0:n], w2_s[:, bass.ds(e, 1), f * P:(f + 1) * P].rearrange(
                        "p o m -> p (o m)"), hid[s][:, f, 0:n], start=(f == 0), stop=(f == FT - 1))
                mm.then_inc(M["out"], 1)
            pe.sem_inc(M["out"], 2)
            experts(pe, nothing, hidden, outputs, nothing)

        def moe_act(act):
            act.sem_inc(M["gelu"], FT)
            act.sem_inc(M["oev"], 2)

            def gelu(c, n, e, s):
                k = c * E + e
                act.wait_ge(M["out"], k + 1)
                for f in range(FT):
                    act.wait_ge(M["hid"], k * FT + (f + 1))
                    nc.scalar.activation(hid[s][:, f, 0:n], bank[f][:, 0:n], ACT.Gelu,
                                         bias=vec[:, bass.ds(e * FT + (V_B1 + f), 1)]).then_inc(M["gelu"], 1)

            def evict(c, n, e, s):
                k = c * E + e
                act.wait_ge(M["out"], k + 3)
                act.wait_ge(M["added"], k + 1)
                nc.scalar.activation(part[s][:, 0:n], bank[4 + s][:, 0:n], ACT.Identity,
                                     bias=vec[:, bass.ds(e + V_B2, 1)]).then_inc(M["oev"], 1)
            experts(act, nothing, gelu, evict, nothing)

        def moe_dve(dve):
            dve.sem_inc(M["scaled"], 2)
            dve.sem_inc(M["added"], 2)

            def add(c, n, e, s):
                k = c * E + e
                dve.wait_ge(M["oev"], k + 3)
                dve.wait_ge(M["wmm"], k + 1)
                nc.vector.tensor_tensor(part[s][:, 0:n], part[s][:, 0:n], bank[6 + s][:, 0:n],
                                        ALU.mult).then_inc(M["scaled"], 1)
                dve.wait_ge(M["scaled"], k + 3)
                dve.wait_ge(M["added"], k + 2)
                nc.vector.tensor_tensor(tokens(hflat, c, n), tokens(hflat, c, n), part[s][:, 0:n],
                                        ALU.add).then_inc(M["added"], 1)
            experts(dve, nothing, nothing, add, nothing)

        def moe_sync(sp):
            def store(c, n):
                sp.wait_ge(M["added"], c * E + (E + 2))
                sp.dma_start(out[:, bass.ds(c * CHUNK, n)], tokens(hflat, c, n)).then_inc(stored, 16)
            with sp.Fori(0, B * T // CHUNK) as c:
                store(c, CHUNK)
            store(B * T // CHUNK, B * T % CHUNK)
            sp.wait_ge(stored, 16 * (B * T // CHUNK + 1))

        @block.sync
        def _(sp):
            tok_sync(sp)
            sp.wait_ge(stage_done[1], 4)
            sp.dma_start(h_save, hT).then_inc(h_saved, 16)
            sp.wait_ge(stage_done[4], 4)
            sp.dma_start(hT, h_save).then_inc(h_back, 16)
            sp.wait_ge(stage_done[7], 4)
            for dst, src in ((group, group_c), (below, below_c), (bitI, bits_i), (bitF, bits_f)):
                sp.dma_start(dst, src).then_inc(rt_in, 16)
            sp.dma_start(w1_s, w1).then_inc(w_in, 16)
            sp.dma_start(w2_s, w2).then_inc(w_in, 16)
            route_sync(sp)
            moe_sync(sp)

        @block.tensor
        def _(pe):
            for k, stage in enumerate((tok_pe, ln_in.pe, conv_pe, steps_pe, scan_pe, gate_pe, ln_blk.pe, ln_moe.pe)):
                stage(pe)
                fence(pe, k)
            logits_pe(pe)
            route_pe(pe)
            fence(pe, 8)
            moe_pe(pe)

        @block.scalar
        def _(act):
            for k, stage in enumerate((tok_act, ln_in.act, conv_act, steps_act, scan_act, gate_act, ln_blk.act,
                                       ln_moe.act)):
                stage(act)
                fence(act, k)
            logits_act(act)
            route_act(act)
            fence(act, 8)
            moe_act(act)

        @block.vector
        def _(dve):
            for k, stage in enumerate((nothing, ln_in.dve, lambda e: (conv_setup_dve(e), conv_dve(e)), steps_dve,
                                       scan_dve, gate_dve, block_dve, ln_moe.dve)):
                stage(dve)
                fence(dve, k)
            route_dve(dve)
            fence(dve, 8)
            moe_dve(dve)

        @block.gpsimd
        def _(pool):
            for k, stage in enumerate((tok_pool, nothing, nothing, steps_pool, lambda e: (e.wait_ge(h_saved, 16), scan_pool(e)),
                                       nothing, nothing, nothing, nothing)):
                stage(pool)
                fence(pool, k)


def kernel(x, txt, L0_tok_W, L0_tok_b, L0_tok_cls_token, L0_tok_pos_emb, L0_attn_in_w, L0_attn_in_b, L0_attn_conv_w,
           L0_attn_conv_b, L0_attn_xp_w, L0_attn_xp_b, L0_attn_dt_w, L0_attn_dt_b, L0_attn_A_log, L0_attn_D_skip,
           L0_attn_out_w, L0_attn_out_b, L0_attn_ln_g, L0_attn_ln_b, L0_ffn_Wr, L0_ffn_W1, L0_ffn_b1, L0_ffn_W2,
           L0_ffn_b2):
    import ml_dtypes
    import numpy as np
    import concourse.bacc as bacc
    from concourse.bass_utils import run_bass_kernel_spmd

    f32 = np.float32

    def cols(v):
        return np.asarray(v).reshape(-1, P).T

    def halves(w):
        w = np.asarray(w)
        return w.reshape(-1, P, w.shape[1]).transpose(1, 0, 2)

    def const(v):
        return np.full((P, 1), v, f32)

    patches = np.asarray(x).reshape(B, 3, 11, 16, 13, 16).transpose(0, 3, 5, 1, 2, 4).reshape(B, KT, P, NPATCH)
    patches = np.pad(patches, ((0, 0), (0, 0), (0, 0), (1, 0)))
    tok_cols = np.zeros((3, TI), f32)
    tok_cols[0] = np.asarray(L0_tok_pos_emb).reshape(-1)
    tok_cols[1, 0] = 1
    tok_cols[2, 1:] = 1
    xpb = np.asarray(L0_attn_xp_b)
    sel = np.zeros((3, 32, 32, P), f32)
    for j in range(32):
        sel[:, j, j] = 0.5 if j < NS else 1
    q = np.arange(P)
    same = q[:, None] // B == q[None] // B
    bits = (1 << np.arange(NBITS - 1, -1, -1)).astype(np.int32)
    arrays = {
        "patches": patches.transpose(0, 2, 1, 3),
        "txt": np.asarray(txt).transpose(2, 0, 1),
        "tokw": halves(np.asarray(L0_tok_W).T),
        "tok_rows": np.stack([np.ones(P, f32), np.asarray(L0_tok_cls_token).reshape(-1), np.asarray(L0_tok_b)]),
        "tok_cols": tok_cols,
        "vecs": np.concatenate([
            cols(L0_attn_in_b), cols(L0_attn_conv_b), cols(xpb[2 * NS:]), cols(L0_attn_dt_b), cols(L0_attn_D_skip),
            cols(L0_attn_out_b), cols(L0_attn_ln_g), cols(L0_attn_ln_b), const(1e-5), const(LOG_EPS_HALF),
            cols(L0_ffn_b1), cols(L0_ffn_b2)], axis=1),
        "inw": np.asarray(L0_attn_in_w).T,
        "convw": np.asarray(L0_attn_conv_w).reshape(NH, P, KC).transpose(1, 0, 2).reshape(P, NH * KC),
        "xpw": halves(np.asarray(L0_attn_xp_w).T),
        "xpb": xpb[:2 * NS].reshape(-1, 1),
        "dtw": halves(np.asarray(L0_attn_dt_w).T),
        "alog": halves(L0_attn_A_log),
        "outw": halves(np.asarray(L0_attn_out_w).T),
        "wr": np.asarray(L0_ffn_Wr),
        "w1": np.asarray(L0_ffn_W1).transpose(1, 0, 2),
        "w2": np.asarray(L0_ffn_W2).reshape(E, FT, P, P).transpose(2, 0, 1, 3).reshape(P, E, FT * P),
        "ident_c": np.eye(P, dtype=f32),
        "sel_c": sel.reshape(96, 32, P).astype(ml_dtypes.bfloat16),
        "group_c": same.astype(f32),
        "below_c": (same & (q[:, None] < q[None])).astype(f32),
        "mean_c": np.full((P, P), 1 / P, f32),
        "bits_i": np.tile(bits, (P, 1)),
        "bits_f": np.tile(bits.astype(f32), (P, 1)),
    }
    nc = bacc.Bacc("TRN2", target_bir_lowering=False, num_devices=1)
    ins, aps = {}, {}
    for name, a in arrays.items():
        ins[name + "_in"] = np.ascontiguousarray(a)
        aps[name] = nc.dram_tensor(name + "_in", a.shape, mybir.dt.from_np(a.dtype), kind="ExternalInput").ap()
    out = nc.dram_tensor("out", (P, B * T), F32, kind="ExternalOutput").ap()
    build_program(nc, **aps, out=out)
    r = run_bass_kernel_spmd(nc, [ins], core_ids=[0])
    return r.results[0]["out"].reshape(P, B, T).transpose(1, 2, 0)
```

```python
from contextlib import ExitStack

import concourse.bass as bass
from concourse import mybir

ALU = mybir.AluOpType
ACT = mybir.ActivationFunctionType
AX = mybir.AxisListType
F32 = mybir.dt.float32
BF16 = mybir.dt.bfloat16
I32 = mybir.dt.int32

P = 128
B = 16
NPATCH = 143
TI = NPATCH + 1
T = TI + 128
KT = 6
NH = 2
NS = 16
KC = 4
E = 8
FT = 4
CAP = 1024
UNIT = 512
UNITS = E * CAP // UNIT
TPU = UNIT // P
NG = B * T // UNIT
SETS = 6
LOG_FLOOR = -13.815510557964274
LOG_EPS_HALF = 9.210340371976184
SERIES_BELOW = 1.0 / 128
KB = -(-T // P)
NBITS = 30

S_GONE = -104.0

RANGES = [(0, 16, 16), (16, 48, 8), (64, T - 64, 2)]

V_INB, V_CB, V_DTIN, V_DTB, V_D, V_OUTB, V_LNG, V_LNB, V_EPS, V_LE, V_B1 = 0, 4, 6, 8, 10, 12, 13, 14, 15, 16, 17
NV = V_B1 + E * FT


def each_batch(eng, body):
    body(0, 0, True)
    body(1, 1, True)
    with eng.Fori(1, B // 2) as i:
        for s in range(2):
            body(i * 2 + s, s, False)


def skewed(eng, head, tail):
    head(0, 0, True)
    head(1, 1, True)
    tail(0, 0, True)
    head(2, 0, False)
    tail(1, 1, True)
    with eng.Fori(1, B // 2 - 1) as i:
        for s in range(2):
            head(i * 2 + s + 1, 1 - s, False)
            tail(i * 2 + s, s, False)
    head(B - 1, 1, False)
    tail(B - 2, 0, False)
    tail(B - 1, 1, False)


def nothing(*_):
    pass


def build_program(nc, patches, txt, tokw, tok_rows, tok_cols, vecs, inw, convw, xpw, xpb, dtw, alog, outw, wr,
                  w1, w2, b2, ident_c, sel_c, group_c, below_c, mean_c, bits_i, bits_f, iota_c, place_c, out):
    h_save = nc.dram_tensor("h_save", [P, B, T], F32, kind="Internal").ap()
    x_rows = nc.dram_tensor("x_rows", [B * T, P], F32, kind="Internal").ap()
    with ExitStack() as ctx:
        def sb(name, shape, dt=F32):
            return ctx.enter_context(nc.sbuf_tensor(name, shape, dt))

        def sem(name):
            return ctx.enter_context(nc.semaphore(name))

        bank = [ctx.enter_context(nc.psum_tensor(f"bank{i}", [P, 512], F32)) for i in range(8)]

        WORK = 10952
        work = sb("work", [P, WORK])
        xn = sb("xn", [P, B, T])
        xs = sb("xs", [P, B, NH, T])
        dt = sb("dt", [P, B, NH, T])
        dtx = sb("dtx", [P, B, NH, T])
        bc = sb("bc", [96, B, T], BF16)
        vec = sb("vec", [P, NV])
        hvec = sb("hvec", [P, NV])
        ident = sb("ident", [P, P])
        sel = sb("sel", [96, 32, P], BF16)
        meanm = sb("meanm", [P, P])
        diag = sb("diag", [P, NH, KC, P])
        xpb_s = sb("xpb_s", [32, 1])
        inw_s = sb("inw_s", [P, 2 * NH * P])
        xpw_s = sb("xpw_s", [P, NH, 32 + NH * P])
        dtw_s = sb("dtw_s", [P, NH, NH * P])
        outw_s = sb("outw_s", [P, NH, P])
        convw_s = sb("convw_s", [P, NH * KC])
        negA = sb("negA", [P, NH, NS])
        wr_s = sb("wr_s", [P, E])

        def view(arr, off, *shape, rows=P, dtype=F32):
            size = 1
            for d in shape:
                size *= d
            v = arr[0:rows, off:off + (size if dtype != BF16 else size // 2)]
            if dtype != F32:
                v = v.bitcast(dtype)
            names = "abcd"[:len(shape)]
            return v if len(shape) == 1 else v.rearrange(
                f"p ({' '.join(names)}) -> p {' '.join(names)}", **dict(zip(names, shape)))

        hT = view(work, 0, B, T)
        oT = dt[:, :, :, :].rearrange("p b h t -> p (b h t)")[:, 0:B * T].rearrange("p (b t) -> p b t", b=B)

        class Scratch:
            def __init__(self, off=B * T):
                self.off = off

            def take(self, *shape, **kw):
                size = 1
                for d in shape:
                    size *= d
                v = view(work, self.off, *shape, **kw)
                self.off += size if kw.get("dtype") != BF16 else size // 2
                assert self.off <= WORK, self.off
                return v

            def two(self, *shape, **kw):
                return [self.take(*shape, **kw) for _ in range(2)]

        def row(arr, b):
            return arr[:, bass.ds(b, 1), :].rearrange("p o t -> p (o t)")

        def both(arr, b):
            return arr[:, bass.ds(b, 1), :, :].rearrange("p o h t -> p (o h) t")

        stage_done = [sem(f"stage{k}_done") for k in range(9)]

        def fence(eng, k):
            eng.drain().then_inc(stage_done[k], 1)
            eng.wait_ge(stage_done[k], 4)

        passed = sem("passed")

        def apart(eng):
            eng.sem_inc(passed, 1)

        block = ctx.enter_context(nc.Block())

        consts_in, late_in, text_in, tok_mm, tok_ev = (
            sem(n) for n in ("consts_in", "late_in", "text_in", "tok_mm", "tok_ev"))
        pat_in = [sem(f"pat_in{s}") for s in range(2)]
        m = Scratch()
        pat = m.two(KT, TI)
        tokw_s = m.take(KT, P)
        tokr_s = m.take(P, rows=3)
        tokc_s = m.take(TI, rows=3)
        EARLY = [(vec[:, :], vecs), (tokw_s, tokw), (tokr_s, tok_rows), (tokc_s, tok_cols), (meanm[:, :], mean_c)]
        LATE = [(ident[:, :], ident_c), (inw_s[:, :], inw), (convw_s[:, :], convw), (xpw_s[:, :, :], xpw),
                (xpb_s[:, :], xpb), (dtw_s[:, :, :], dtw), (negA[:, :, :], alog), (outw_s[:, :, :], outw),
                (wr_s[:, :], wr), (sel[:, :, :], sel_c)]

        def tok_sync(sp):
            for dst, src in EARLY:
                sp.dma_start(dst, src).then_inc(consts_in, 16)

            def load(b, s, first):
                if not first:
                    sp.wait_ge(tok_mm, b - 1)
                sp.dma_start(pat[s], patches[bass.ds(b, 1)].rearrange("o p k n -> (o p) k n")).then_inc(pat_in[s], 16)
            each_batch(sp, load)

        def tok_pool(pool):
            pool.dma_start(hT[:, :, TI:T], txt).then_inc(text_in, 16)
            for dst, src in LATE:
                pool.dma_start(dst, src).then_inc(late_in, 16)

        def tok_pe(pe):
            pe.wait_ge(consts_in, 16 * len(EARLY))

            def tok(b, s, first):
                if not first:
                    pe.wait_ge(tok_ev, b - 1)
                nc.tensor.matmul(bank[s][:, 0:TI], tokr_s, tokc_s, start=True, stop=False)
                pe.wait_ge(pat_in[s], (b - s) * 8 + 16)
                for k in range(KT):
                    mm = nc.tensor.matmul(bank[s][:, 0:TI], tokw_s[:, k, :], pat[s][:, k, :], start=False,
                                          stop=(k == KT - 1))
                mm.then_inc(tok_mm, 1)
            each_batch(pe, tok)

        def tok_act(act):
            def evict(b, s, first):
                act.wait_ge(tok_mm, b + 1)
                nc.scalar.copy(row(hT, b)[:, 0:TI], bank[s][:, 0:TI]).then_inc(tok_ev, 1)
            each_batch(act, evict)
            act.wait_ge(text_in, 16)

        m = Scratch()
        ln_sq, ln_log, ln_rs = m.two(T), m.two(T), m.two(T)

        class LayerNorm:

            def __init__(self, name, src, dst):
                self.src, self.dst = src, dst
                self.mean, self.cent, self.sq, self.var, self.log, self.rstd, self.out = (
                    sem(f"{name}_{n}") for n in ("mean", "cent", "sq", "var", "log", "rstd", "out"))

            def pe(self, pe):
                def mean(b, s, first):
                    if not first:
                        pe.wait_ge(self.cent, b - 1)
                    nc.tensor.matmul(bank[s][:, 0:T], meanm[:, :], row(self.src, b), start=True,
                                     stop=True).then_inc(self.mean, 1)

                def var(b, s, first):
                    pe.wait_ge(self.sq, b + 1)
                    if not first:
                        pe.wait_ge(self.log, b - 1)
                    nc.tensor.matmul(bank[2 + s][:, 0:T], meanm[:, :], ln_sq[s], start=True,
                                     stop=True).then_inc(self.var, 1)
                skewed(pe, mean, var)

            def act(self, act):
                nc.scalar.preload_act_table_set("natural_log_exp_and_others")

                def square(b, s, first):
                    act.wait_ge(self.cent, b + 1)
                    if not first:
                        act.wait_ge(self.var, b - 1)
                    nc.scalar.activation(ln_sq[s], row(self.dst, b), ACT.Square).then_inc(self.sq, 1)

                def rstd(b, s, first):
                    act.wait_ge(self.var, b + 1)
                    nc.scalar.activation(ln_log[s], bank[2 + s][:, 0:T], ACT.Ln,
                                         bias=vec[:, V_EPS:V_EPS + 1]).then_inc(self.log, 1)
                    act.wait_ge(self.log, b + 1)
                    if not first:
                        act.wait_ge(self.out, b - 1)
                    nc.scalar.activation(ln_rs[s], ln_log[s], ACT.Exp, scale=-0.5).then_inc(self.rstd, 1)
                skewed(act, square, rstd)

            def dve(self, dve, finish=None):
                def center(b, s, first):
                    dve.wait_ge(self.mean, b + 1)
                    nc.vector.tensor_tensor(row(self.dst, b), row(self.src, b), bank[s][:, 0:T],
                                            ALU.subtract).then_inc(self.cent, 1)

                def scale(b, s, first):
                    dve.wait_ge(self.rstd, b + 1)
                    nc.vector.tensor_tensor(row(self.dst, b), row(self.dst, b), ln_rs[s],
                                            ALU.mult).then_inc(self.out, 1)
                    if finish:
                        finish(b, s, first)
                skewed(dve, center, scale)

        ln_in = LayerNorm("ln_in", hT, xn)

        in_mm, in_ev, conv_mm, conv_th, conv_half, conv_out = (
            sem(n) for n in ("in_mm", "in_ev", "conv_mm", "conv_th", "conv_half", "conv_out"))
        negA_exp, setup_ok, h_saved = sem("negA_exp"), sem("setup_ok"), sem("h_saved")
        m = Scratch()
        xpad, cth, chalf = m.two(NH, T + KC - 1), m.two(NH, T), m.two(NH, T)

        def conv_setup_dve(dve):
            dve.wait_ge(late_in, 16 * len(LATE))
            dve.wait_ge(consts_in, 16 * len(EARLY))
            for h in range(NH):
                for k in range(KC):
                    nc.vector.tensor_scalar(diag[:, h, k, :], ident[:, :], convw_s[:, h * KC + k:h * KC + k + 1],
                                            None, ALU.mult).then_inc(setup_ok, 1)
                nc.vector.memset(xpad[h][:, :, 0:KC - 1], 0.0).then_inc(setup_ok, 1)
            nc.vector.tensor_scalar(hvec[:, :], vec[:, :], 0.5, None, ALU.mult).then_inc(setup_ok, 1)
            dve.wait_ge(negA_exp, 1)
            nc.vector.tensor_scalar(negA[:, :, :], negA[:, :, :], -1.0, None, ALU.mult).then_inc(setup_ok, 1)

        SETUP = NH * (KC + 1) + 2

        def conv_pe(pe):
            pe.wait_ge(setup_ok, SETUP)

            def inproj(b, s, first):
                if not first:
                    pe.wait_ge(in_ev, b - 1)
                for h in range(NH):
                    mm = nc.tensor.matmul(bank[4 * s + h][:, 0:T], inw_s[:, h * P:(h + 1) * P], row(xn, b),
                                          start=True, stop=True)
                mm.then_inc(in_mm, 1)

            def conv(b, s, first):
                pe.wait_ge(in_ev, b + 1)
                if not first:
                    pe.wait_ge(conv_half, b - 1)
                for h in range(NH):
                    for k in range(KC):
                        mm = nc.tensor.matmul(bank[4 * s + 2 + h][:, 0:T], diag[:, h, k, :],
                                              xpad[s][:, h, k:k + T], start=(k == 0), stop=(k == KC - 1))
                mm.then_inc(conv_mm, 1)
            skewed(pe, inproj, conv)

        def conv_act(act):
            act.wait_ge(late_in, 16 * len(LATE))
            nc.scalar.activation(negA[:, :, :], negA[:, :, :], ACT.Exp).then_inc(negA_exp, 1)
            act.wait_ge(setup_ok, SETUP)

            def evict(b, s, first):
                act.wait_ge(in_mm, b + 1)
                if not first:
                    act.wait_ge(conv_mm, b - 1)
                for h in range(NH):
                    a = nc.scalar.activation(xpad[s][:, h, KC - 1:], bank[4 * s + h][:, 0:T], ACT.Identity,
                                             bias=vec[:, V_INB + h:V_INB + h + 1])
                a.then_inc(in_ev, 1)

            def gate(b, s, first):
                act.wait_ge(conv_mm, b + 1)
                if not first:
                    act.wait_ge(conv_out, b - 1)
                for h in range(NH):
                    a = nc.scalar.activation(cth[s][:, h, :], bank[4 * s + 2 + h][:, 0:T], ACT.Tanh, scale=0.5,
                                             bias=hvec[:, V_CB + h:V_CB + h + 1])
                a.then_inc(conv_th, 1)
                for h in range(NH):
                    a = nc.scalar.activation(chalf[s][:, h, :], bank[4 * s + 2 + h][:, 0:T], ACT.Identity, scale=0.5,
                                             bias=hvec[:, V_CB + h:V_CB + h + 1])
                a.then_inc(conv_half, 1)
            skewed(act, evict, gate)

        def conv_dve(dve):
            def silu(b, s, first):
                dve.wait_ge(conv_th, b + 1)
                dve.wait_ge(conv_half, b + 1)
                nc.vector.scalar_tensor_tensor(both(xs, b), cth[s], 1.0, chalf[s], ALU.add,
                                               ALU.mult).then_inc(conv_out, 1)
            each_batch(dve, silu)

        (xp_mm, dtin_ev, bcf_ev, dt_mm, dt_abs, dt_exp, dt_log, dt_relu, dt_ser, dt_mask, dt_sel, dt_ok, dtx_ok,
         bc_cp, bc_sub, bz) = (sem(n) for n in (
             "xp_mm", "dtin_ev", "bcf_ev", "dt_mm", "dt_abs", "dt_exp", "dt_log", "dt_relu", "dt_ser", "dt_mask",
             "dt_sel", "dt_ok", "dtx_ok", "bc_cp", "bc_sub", "bz"))
        m = Scratch()
        dtin, dexp, dlog, drel = m.two(NH, T), m.two(NH, T), m.two(NH, T), m.two(NH, T)
        dser, dmask = m.take(NH, T), m.take(NH, T, dtype=I32)
        bcf, bcr = m.two(T, rows=32), m.take(T, rows=32)
        bcq = m.take(T, rows=32, dtype=BF16)

        def steps_pe(pe):
            def xproj(b, s, first):
                if not first:
                    pe.wait_ge(bcf_ev, b - 1)
                    pe.wait_ge(dtin_ev, b - 1)
                for k in range(NH):
                    nc.tensor.matmul(bank[3 * s][0:32, 0:T], xpw_s[:, k, 0:32], both(xs, b)[:, k, :],
                                     start=(k == 0), stop=(k == NH - 1))
                for h in range(NH):
                    for k in range(NH):
                        mm = nc.tensor.matmul(bank[3 * s + 1 + h][:, 0:T], xpw_s[:, k, 32 + h * P:32 + (h + 1) * P],
                                              both(xs, b)[:, k, :], start=(k == 0), stop=(k == NH - 1))
                mm.then_inc(xp_mm, 1)

            def steps(b, s, first):
                pe.wait_ge(dtin_ev, b + 1)
                if not (isinstance(b, int) and b == 0):
                    pe.wait_ge(dt_relu, b)
                for h in range(NH):
                    for k in range(NH):
                        mm = nc.tensor.matmul(bank[6 + h][:, 0:T], dtw_s[:, k, h * P:(h + 1) * P],
                                              dtin[s][:, k, :], start=(k == 0), stop=(k == NH - 1))
                mm.then_inc(dt_mm, 1)
            skewed(pe, xproj, steps)

        def steps_act(act):
            nc.scalar.preload_act_table_set("natural_log_exp_and_others")

            def evict(b, s, first):
                act.wait_ge(xp_mm, b + 1)
                if not first:
                    act.wait_ge(dt_mm, b - 1)
                for h in range(NH):
                    a = nc.scalar.activation(dtin[s][:, h, :], bank[3 * s + 1 + h][:, 0:T], ACT.Identity,
                                             bias=vec[:, V_DTIN + h:V_DTIN + h + 1])
                a.then_inc(dtin_ev, 1)
                if not first:
                    act.wait_ge(bc_sub, 2 * b - 2)
                nc.scalar.activation(bcf[s], bank[3 * s][0:32, 0:T], ACT.Identity, bias=xpb_s[:, :]).then_inc(bcf_ev, 1)

            def softplus(b, s, first):
                act.wait_ge(dt_mm, b + 1)
                if not first:
                    act.wait_ge(dt_sel, b - 1)
                    act.wait_ge(dt_ok, b - 1)
                for h in range(NH):
                    a = nc.scalar.activation(dexp[s][:, h, :], bank[6 + h][:, 0:T], ACT.Abs,
                                             bias=vec[:, V_DTB + h:V_DTB + h + 1])
                a.then_inc(dt_abs, 1)
                act.wait_ge(dt_abs, b + 1)
                nc.scalar.activation(dexp[s], dexp[s], ACT.Exp, scale=-1.0).then_inc(dt_exp, 1)
                act.wait_ge(dt_exp, b + 1)
                nc.scalar.activation(dlog[s], dexp[s], ACT.Ln, bias=1.0).then_inc(dt_log, 1)
            skewed(act, evict, softplus)

        def steps_dve(dve):
            def one(b, s, first):
                dve.wait_ge(dt_abs, b + 1)
                for h in range(NH):
                    a = nc.vector.tensor_scalar(drel[s][:, h, :], bank[6 + h][:, 0:T],
                                                vec[:, V_DTB + h:V_DTB + h + 1], 0.0, ALU.add, ALU.max)
                a.then_inc(dt_relu, 1)
                dve.wait_ge(dt_exp, b + 1)
                nc.vector.tensor_scalar(dser, dexp[s], 1.0 / 3, -0.5, ALU.mult, ALU.add).then_inc(dt_ser, 1)
                nc.vector.tensor_scalar(dmask, dexp[s], SERIES_BELOW, None, ALU.is_lt).then_inc(dt_mask, 1)
                dve.wait_ge(dt_ser, 3 * b + 1)
                nc.vector.tensor_tensor(dser, dser, dexp[s], ALU.mult).then_inc(dt_ser, 1)
                dve.wait_ge(dt_ser, 3 * b + 2)
                nc.vector.scalar_tensor_tensor(dser, dser, 1.0, dexp[s], ALU.add, ALU.mult).then_inc(dt_ser, 1)
                dve.wait_ge(dt_ser, 3 * b + 3)
                dve.wait_ge(dt_mask, b + 1)
                dve.wait_ge(dt_log, b + 1)
                apart(dve)
                nc.vector.copy_predicated(dlog[s], dmask, dser).then_inc(dt_sel, 1)
                dve.wait_ge(dt_sel, b + 1)
                nc.vector.tensor_tensor(both(dt, b), dlog[s], drel[s], ALU.add).then_inc(dt_ok, 1)
            each_batch(dve, one)

        def steps_pool(pool):
            def one(b, s, first):
                pool.wait_ge(bcf_ev, b + 1)
                apart(pool)
                nc.gpsimd.tensor_copy(row(bc, b)[0:32, :], bcf[s]).then_inc(bc_cp, 1)
                pool.wait_ge(bc_cp, 3 * b + 1)
                apart(pool)
                nc.gpsimd.tensor_tensor(bcr, bcf[s], row(bc, b)[0:32, :], ALU.subtract).then_inc(bc_sub, 1)
                pool.wait_ge(bc_sub, 2 * b + 1)
                apart(pool)
                nc.gpsimd.tensor_copy(bcq, bcr).then_inc(bc_cp, 1)
                pool.wait_ge(bc_cp, 3 * b + 2)
                apart(pool)
                nc.gpsimd.tensor_copy(row(bc, b)[32:64, :], bcq).then_inc(bc_cp, 1)
                nc.gpsimd.tensor_tensor(row(bc, b)[64:96, :], bcr, bcq, ALU.subtract).then_inc(bc_sub, 1)
                pool.wait_ge(bc_cp, 3 * b + 3)
                pool.wait_ge(bc_sub, 2 * b + 2)
                pool.wait_ge(dt_ok, b + 1)
                apart(pool)
                nc.gpsimd.tensor_tensor(both(dtx, b), both(dt, b), both(xs, b), ALU.mult).then_inc(dtx_ok, 1)
            each_batch(pool, one)

        TILE = max(NH * g * (1 + tl) for _, tl, g in RANGES)
        m = Scratch(0)
        s_mask, s_u = m.take(TILE), m.take(TILE)
        s_a, s_L, s_w = m.two(TILE), m.two(TILE), m.two(TILE)
        s_c = m.two(512)
        carryL, carryH = m.take(NS, B * NH), m.take(NS, B * NH)
        s_max, s_dead, ones_c = m.take(NS), m.take(NS), m.take(1)
        alive = [m.take(NS, rows=1, dtype=I32) for _ in RANGES]
        alive4 = [m.take(NS // 4, rows=1, dtype=I32) for _ in RANGES]
        S = {n: sem(f"scan_{n}") for n in ("bmm", "cmm", "ccopy", "clip", "logsum", "logtail", "decay", "gate", "src",
                                           "inp", "state", "tail", "out", "added")}
        OF = {"pe": ("bmm", "cmm"), "act": ("ccopy", "decay", "gate"), "pool": ("out", "added"),
              "dve": ("clip", "logsum", "logtail", "src", "inp", "state", "tail")}
        s_zero, s_pads, s_skip, s_flag, s_count = (
            sem(n) for n in ("scan_zero", "scan_pads", "scan_skip", "scan_flag", "scan_count"))
        s_yD = sem("scan_yD")
        LAST = len(RANGES) - 1

        def tiles_before(r):
            return sum(B // gb * NS for _, _, gb in RANGES[:r])

        def scan_starts(eng, who):
            for n in OF[who]:
                eng.sem_inc(S[n], 2)

        def until(eng, name, k):
            eng.wait_ge(S[name], k + 3)

        class Tile:

            def __init__(self, r, n, g, s):
                self.t0, self.tl, self.gb = RANGES[r]
                self.carried, self.carries = r > 0, r < LAST
                self.k = tiles_before(r) + n * (B // self.gb) + g
                self.g, self.n, self.s = g, n, s
                self.segs = self.gb * NH

            def flat(self, buf):
                return buf[:, 0:self.segs * (1 + self.tl)]

            def seg(self, buf):
                return self.flat(buf).rearrange("p (s t) -> p s t", s=self.segs)

            def body(self, buf):
                return self.seg(buf)[:, :, 1:]

            def body_bh(self, buf):
                return self.seg(buf).rearrange("p (b h) t -> p b h t", h=NH)[:, :, :, 1:]

            def array(self, arr):
                return arr[:, bass.ds(self.g * self.gb, self.gb), :, self.t0:self.t0 + self.tl]

            def rows_bc(self):
                return bc[:, bass.ds(self.g * self.gb, self.gb), self.t0:self.t0 + self.tl]

            def per_token(self, ap):
                return ap[:, 0:self.gb * self.tl].rearrange("p (b o t) -> p b o t", b=self.gb, o=1).to_broadcast(
                    [P, self.gb, NH, self.tl])

            def carry(self, arr):
                return arr[:, bass.ds(self.n, 1), bass.ds(self.g * self.segs, self.segs)].rearrange("p o s -> p (o s)")

        def tiles(eng, who, before_range, head, tail):
            def run(r, tile, count):
                head(tile(0, 0))
                if count > 2:
                    with eng.Fori(0, count // 2 - 1) as i:
                        for s in range(2):
                            head(tile(i * 2 + s + 1, 1 - s))
                            tail(tile(i * 2 + s, s))
                head(tile(count - 1, 1))
                tail(tile(count - 2, 0))
                tail(tile(count - 1, 1))

            before_range(0)
            run(0, lambda n, s: Tile(0, n, 0, s), NS)
            for r in range(1, len(RANGES)):
                before_range(r)
                eng.wait_ge(s_flag, 2 * r)
                groups = B // RANGES[r][2]

                def skip(states):
                    eng.drain().then_inc(s_skip, 1)
                    for name in OF[who]:
                        eng.sem_inc(S[name], states * groups)

                with eng.Fori(0, NS // 4) as q:
                    with eng.If(eng.value_load(alive4[r][0:1, bass.ds(q, 1)], min_val=0, max_val=P) != 0):
                        with eng.Fori(0, 4) as j:
                            n = eng.snap(q * 4 + j)
                            with eng.If(eng.value_load(alive[r][0:1, bass.ds(n, 1)], min_val=0, max_val=P) != 0):
                                run(r, lambda g, s: Tile(r, n, g, s), groups)
                            with eng.Else():
                                skip(1)
                    with eng.Else():
                        skip(4)

        def scan_pe(pe):
            scan_starts(pe, "pe")

            def count_dead(r):
                if r:
                    pe.wait_ge(s_count, 2 * r - 1)
                    nc.tensor.matmul(bank[4][0:1, 0:NS], ones_c, s_dead, start=True, stop=True).then_inc(s_count, 1)

            def spread(x):
                n = x.gb * x.tl
                until(pe, "src", x.k - 2)
                nc.tensor.matmul(bank[x.s][:, 0:n], sel[:, bass.ds(x.n, 1), :].rearrange("p o m -> p (o m)"),
                                 x.rows_bc(), start=True, stop=True).then_inc(S["bmm"], 1)
                until(pe, "ccopy", x.k - 2)
                nc.tensor.matmul(bank[2 + x.s][:, 0:n],
                                 sel[:, bass.ds(x.n + NS, 1), :].rearrange("p o m -> p (o m)"),
                                 x.rows_bc(), start=True, stop=True).then_inc(S["cmm"], 1)
            tiles(pe, "pe", count_dead, spread, nothing)

        def scan_act(act):
            scan_starts(act, "act")
            act.wait_ge(h_saved, 16)

            def head(x):
                until(act, "clip", x.k)
                until(act, "state", x.k - 2)
                nc.scalar.activation(x.body(s_a[x.s]), x.body(s_u), ACT.Exp).then_inc(S["decay"], 1)
                until(act, "logtail" if x.carries else "logsum", x.k)
                nc.scalar.activation(x.flat(s_L[x.s]), x.flat(s_L[x.s]), ACT.Tanh, scale=0.5,
                                     bias=vec[:, V_LE:V_LE + 1]).then_inc(S["gate"], 1)
                until(act, "cmm", x.k)
                until(act, "out", x.k - 2)
                nc.scalar.copy(s_c[x.s][:, 0:x.gb * x.tl], bank[2 + x.s][:, 0:x.gb * x.tl]).then_inc(S["ccopy"], 1)
            tiles(act, "act", nothing, head, nothing)

        def scan_dve(dve):
            scan_starts(dve, "dve")
            dve.wait_ge(h_saved, 16)

            def before_range(r):
                t = Tile(r, 0, 0, 0)
                if r:
                    until(dve, "added", t.k - 1)
                    nc.vector.tensor_reduce(s_max, carryL, AX.X, ALU.max).then_inc(s_zero, 1)
                    dve.wait_ge(s_zero, 8 * r + 1)
                    nc.vector.tensor_scalar(s_dead, s_max, S_GONE, None, ALU.is_le).then_inc(s_count, 1)
                    dve.wait_ge(s_count, 2 * r)
                    nc.vector.tensor_scalar(alive[r], bank[4][0:1, 0:NS], -1.0, float(P), ALU.mult,
                                            ALU.add).then_inc(s_flag, 1)
                    dve.wait_ge(s_flag, 2 * r - 1)
                    nc.vector.tensor_reduce(alive4[r], alive[r].rearrange("p (q j) -> p q j", j=4), AX.X,
                                            ALU.max).then_inc(s_flag, 1)
                nc.vector.memset(t.flat(s_mask), 1.0).then_inc(s_zero, 1)
                dve.wait_ge(s_zero, 8 * r + (2 if r else 1))
                for buf in (s_mask, *s_a, s_u, *s_w):
                    nc.vector.memset(t.seg(buf)[:, :, 0:1], 0.0).then_inc(s_zero, 1)
                if not r:
                    nc.vector.memset(ones_c, 1.0).then_inc(s_zero, 1)
                    for h in range(NH):
                        a = nc.vector.tensor_scalar(xs[:, :, h, :], xs[:, :, h, :], vec[:, V_D + h:V_D + h + 1], None,
                                                    ALU.mult)
                    a.then_inc(s_yD, 1)
                dve.wait_ge(s_zero, 8 * r + 8)

            def head(x):
                until(dve, "decay", x.k - 1)
                until(dve, "logsum", x.k - 1)
                if x.carried:
                    nc.vector.tensor_scalar(x.seg(s_u)[:, :, 0:1], x.carry(carryL).rearrange(
                        "p (s o) -> p s o", o=1), 1.0, None, ALU.mult).then_inc(s_pads, 1)
                for h in range(NH):
                    a = nc.vector.tensor_scalar(x.body_bh(s_u)[:, :, h, :], x.array(dt)[:, :, h, :],
                                                negA[:, h, bass.ds(x.n, 1)], LOG_FLOOR, ALU.mult, ALU.max)
                a.then_inc(S["clip"], 1)
                until(dve, "clip", x.k)
                until(dve, "inp", x.k - 2)
                nc.vector.tensor_tensor_scan(x.flat(s_L[x.s]), x.flat(s_mask), x.flat(s_u), 0.0, ALU.mult,
                                             ALU.add).then_inc(S["logsum"], 1)
                if x.carries:
                    until(dve, "logsum", x.k)
                    nc.vector.tensor_scalar(x.carry(carryL), x.seg(s_L[x.s])[:, :, x.tl:].rearrange(
                        "p s o -> p (s o)"), 1.0, None, ALU.mult).then_inc(S["logtail"], 1)

            def tail(x):
                until(dve, "bmm", x.k)
                until(dve, "added", x.k - 2)
                nc.vector.tensor_tensor(x.body_bh(s_w[x.s]), x.array(dtx), x.per_token(bank[x.s]),
                                        ALU.mult).then_inc(S["src"], 1)
                if x.carried:
                    nc.vector.tensor_scalar(x.seg(s_w[x.s])[:, :, 0:1], x.carry(carryH).rearrange(
                        "p (s o) -> p s o", o=1), 1.0, None, ALU.mult).then_inc(s_pads, 1)
                until(dve, "gate", x.k)
                until(dve, "src", x.k)
                nc.vector.scalar_tensor_tensor(x.body(s_w[x.s]), x.body(s_L[x.s]), 1.0, x.body(s_w[x.s]), ALU.add,
                                               ALU.mult).then_inc(S["inp"], 1)
                until(dve, "decay", x.k)
                until(dve, "inp", x.k)
                nc.vector.tensor_tensor_scan(x.flat(s_w[x.s]), x.flat(s_a[x.s]), x.flat(s_w[x.s]), 0.0, ALU.mult,
                                             ALU.add).then_inc(S["state"], 1)
                if x.carries:
                    until(dve, "state", x.k)
                    nc.vector.tensor_scalar(x.carry(carryH), x.seg(s_w[x.s])[:, :, x.tl:].rearrange(
                        "p s o -> p (s o)"), 1.0, None, ALU.mult).then_inc(S["tail"], 1)
            tiles(dve, "dve", before_range, head, tail)

        def scan_pool(pool):
            scan_starts(pool, "pool")
            pool.wait_ge(s_yD, 1)

            def sum_up(x):
                until(pool, "tail" if x.carries else "state", x.k)
                until(pool, "ccopy", x.k)
                apart(pool)
                nc.gpsimd.tensor_tensor(x.body_bh(s_w[x.s]), x.body_bh(s_w[x.s]), x.per_token(s_c[x.s]),
                                        ALU.mult).then_inc(S["out"], 1)
                until(pool, "out", x.k)
                until(pool, "added", x.k - 1)
                apart(pool)
                nc.gpsimd.tensor_tensor(x.array(xs), x.array(xs), x.body_bh(s_w[x.s]), ALU.add).then_inc(S["added"], 1)
            tiles(pool, "pool", nothing, nothing, sum_up)

        z_mm, z_th, z_half, z_silu, yz_ok, o_mm, o_ok, h_back = (
            sem(n) for n in ("z_mm", "z_th", "z_half", "z_silu", "yz_ok", "o_mm", "o_ok", "h_back"))
        m = Scratch()
        zth, zhalf = m.two(NH, T), m.two(NH, T)

        def gate_pe(pe):
            def z(b, s, first):
                if not first:
                    pe.wait_ge(z_half, b - 1)
                for h in range(NH):
                    mm = nc.tensor.matmul(bank[2 * s + h][:, 0:T], inw_s[:, (NH + h) * P:(NH + h + 1) * P],
                                          row(xn, b), start=True, stop=True)
                mm.then_inc(z_mm, 1)

            def outproj(b, s, first):
                pe.wait_ge(yz_ok, b + 1)
                if not first:
                    pe.wait_ge(o_ok, b - 1)
                for k in range(NH):
                    mm = nc.tensor.matmul(bank[4 + s][:, 0:T], outw_s[:, k, :], both(dtx, b)[:, k, :],
                                          start=(k == 0), stop=(k == NH - 1))
                mm.then_inc(o_mm, 1)
            skewed(pe, z, outproj)

        def gate_act(act):
            def one(b, s, first):
                act.wait_ge(z_mm, b + 1)
                if not first:
                    act.wait_ge(z_silu, b - 1)
                for h in range(NH):
                    a = nc.scalar.activation(zth[s][:, h, :], bank[2 * s + h][:, 0:T], ACT.Tanh, scale=0.5,
                                             bias=hvec[:, V_INB + NH + h:V_INB + NH + h + 1])
                a.then_inc(z_th, 1)
                for h in range(NH):
                    a = nc.scalar.activation(zhalf[s][:, h, :], bank[2 * s + h][:, 0:T], ACT.Identity, scale=0.5,
                                             bias=hvec[:, V_INB + NH + h:V_INB + NH + h + 1])
                a.then_inc(z_half, 1)
            each_batch(act, one)

        def gate_dve(dve):
            def silu(b, s, first):
                dve.wait_ge(z_th, b + 1)
                dve.wait_ge(z_half, b + 1)
                nc.vector.scalar_tensor_tensor(both(dtx, b), zth[s], 1.0, zhalf[s], ALU.add,
                                               ALU.mult).then_inc(z_silu, 1)
                dve.wait_ge(z_silu, b + 1)
                nc.vector.tensor_tensor(both(dtx, b), both(dtx, b), both(xs, b), ALU.mult).then_inc(yz_ok, 1)

            def residual(b, s, first):
                dve.wait_ge(o_mm, b + 1)
                nc.vector.scalar_tensor_tensor(row(oT, b), bank[4 + s][:, 0:T], vec[:, V_OUTB:V_OUTB + 1],
                                               row(xn, b), ALU.add, ALU.add).then_inc(o_ok, 1)
            skewed(dve, silu, residual)

        ln_blk = LayerNorm("ln_blk", oT, oT)
        aff_ok, h2_ok = sem("aff_ok"), sem("h2_ok")

        def block_dve(dve):
            def add(b, s, first):
                dve.wait_ge(ln_blk.out, b + 1)
                nc.vector.tensor_scalar(row(oT, b), row(oT, b), vec[:, V_LNG:V_LNG + 1], vec[:, V_LNB:V_LNB + 1],
                                        ALU.mult, ALU.add).then_inc(aff_ok, 1)
                dve.wait_ge(aff_ok, b + 1)
                nc.vector.tensor_tensor(row(hT, b), row(hT, b), row(oT, b), ALU.add).then_inc(h2_ok, 1)
            dve.wait_ge(h_back, 16)
            ln_blk.dve(dve, finish=add)

        ln_moe = LayerNorm("ln_moe", hT, xn)

        bigx = xs[:, :, :, :].rearrange("p b h t -> p (b h t)")
        bigd = dt[:, :, :, :].rearrange("p b h t -> p (b h t)")
        bigy = dtx[:, :, :, :].rearrange("p b h t -> p (b h t)")
        lg_mm, lg_ev, lg_moved, rt_in, rt_pe, rt_dve, rt_act, rt_cand, place_in, b2_in, w_in = (
            sem(n) for n in ("lg_mm", "lg_ev", "lg_moved", "rt_in", "rt_pe", "rt_dve", "rt_act", "rt_cand",
                             "place_in", "b2_in", "w_in"))
        lg = view(bigy, 0, B, T, rows=E)
        lgr = view(bigx, 0, T)
        prob, flag, pick, ones_t = (view(bigx, T * i, T) for i in (1, 2, 3, 4))
        slotI = view(bigx, T * 5, T, dtype=I32)
        group, below = view(bigx, T * 6, P), view(bigx, T * 6 + P, P)
        bitI, bitF = view(bigx, T * 6 + 2 * P, NBITS, dtype=I32), view(bigx, T * 6 + 2 * P + 32, NBITS)
        sm = view(bigx, T * 6 + 2 * P + 64, 32)
        smi = sm.bitcast(I32)
        rowe = view(bigx, T * 6 + 2 * P + 96, E, rows=1)
        rowx = view(bigx, T * 6 + 2 * P + 96 + E, P, rows=1)
        C_MAX, C_NEG, C_SUM, C_INV, C_THR, C_CNT, C_ADD, C_CAND, C_GT, C_EQ = range(10)

        m = Scratch()
        tin = {"x": m.take(UNIT), "h": m.take(UNIT)}
        trow = {"x": m.take(TPU, P), "h": m.take(TPU, P)}
        gath = [m.take(TPU, P), *trow.values()]
        xe = m.two(UNIT)
        place = m.take(E, KB * B, SETS, dtype=BF16)
        tokT = {n: m.take(KB, P) for n in ("lo", "hi", "w")}
        lowx = m.take(P, dtype=BF16)
        hot_hi = m.take(KB * B, E, dtype=BF16)
        found = m.take(P, rows=SETS * E)
        chosen = m.take(2, CAP // P)
        idx = m.take(E, CAP // P, dtype=I32)
        hot_lo = [view(bigy, i * KB * B * P // 2, KB * B, P, dtype=BF16) for i in range(2)]
        told = [view(bigy, KB * B * P + i * KB * B * SETS * 4, KB * B, SETS, 8, dtype=BF16) for i in range(2)]
        hid = [view(bigx, 2600 + i * FT * UNIT, FT, UNIT) for i in range(2)]
        oute = [view(bigx, 2600 + (2 * FT + i) * UNIT, TPU, P) for i in range(2)]
        weight = view(bigx, 2600 + (2 * FT + 2) * UNIT, E, CAP // P)
        b2_s = view(xn[:, :, :].rearrange("p b t -> p (b t)"), 0, E, P)
        w1_s = view(bigd, 0, E, FT * P)
        w2_s = view(bigd, E * FT * P, E, FT * P)
        assert CAP // P == 8 and B * T % UNIT == 256

        def col(c):
            return sm[:, c:c + 1]

        def coli(c):
            return smi[:, c:c + 1]

        def logits_pe(pe):
            def one(b, s, first):
                if not first:
                    pe.wait_ge(lg_ev, b - 1)
                nc.tensor.matmul(bank[s][0:E, 0:T], wr_s[:, :], row(xn, b), start=True, stop=True).then_inc(lg_mm, 1)
            each_batch(pe, one)

        def logits_act(act):
            def one(b, s, first):
                act.wait_ge(lg_mm, b + 1)
                nc.scalar.copy(row(lg, b), bank[s][0:E, 0:T]).then_inc(lg_ev, 1)
            each_batch(act, one)

        def route_sync(sp):
            sp.wait_ge(lg_ev, B)
            for e in range(E):
                sp.dma_start(lgr[e * B:(e + 1) * B, :], lg[e:e + 1, :, :]).then_inc(lg_moved, 16)

        NGA = NG + 1
        EARLY_G = 1
        t_cp, t_mm, t_ev, t_st = ({n: sem(f"rows_{w}_{n}") for n in "xh"} for w in ("cp", "mm", "ev", "st"))
        source = {"x": xn[:, :, :].rearrange("p b t -> p (b t)"), "h": work[:, 0:B * T]}
        target = {"x": x_rows, "h": out}

        def group_cp(pool, i, n=UNIT):
            for a in "xh":
                if not (isinstance(i, int) and i == 0):
                    pool.wait_ge(t_mm[a], i)
                    apart(pool)
                nc.gpsimd.tensor_copy(tin[a][:, 0:n], source[a][:, bass.ds(i * UNIT, n)]).then_inc(t_cp[a], 1)

        def group_mm(pe, a, i, n=UNIT):
            pe.wait_ge(t_cp[a], i + 1)
            if not (isinstance(i, int) and i == 0):
                pe.wait_ge(t_ev[a], i)
            bk = bank[2 if a == "x" else 3]
            for j in range(n // P):
                t = nc.tensor.transpose(bk[:, j * P:(j + 1) * P], tin[a][:, j * P:(j + 1) * P], ident[:, :])
            t.then_inc(t_mm[a], 1)

        def group_ev(act, i, n=UNIT):
            for a in "xh":
                act.wait_ge(t_mm[a], i + 1)
                if not (isinstance(i, int) and i == 0):
                    act.wait_ge(t_st[a], 16 * i)
                bk = bank[2 if a == "x" else 3]
                nc.scalar.copy(trow[a][:, 0:n // P, :], bk[:, 0:n].rearrange("p (j c) -> p j c", c=P)).then_inc(
                    t_ev[a], 1)

        def group_store(sp, i, n=UNIT):
            for a in "xh":
                sp.wait_ge(t_ev[a], i + 1)
                sp.dma_start(target[a][bass.ds(i * UNIT, n), :].rearrange("(j p) c -> p j c", p=P),
                             trow[a][:, 0:n // P, :]).then_inc(t_st[a], 16)

        def rows_pool(pool):
            with pool.Fori(0, NG) as i:
                group_cp(pool, i)
            group_cp(pool, NG, B * T - NG * UNIT)

        def rows_sync(sp):
            with sp.Fori(0, NG) as i:
                group_store(sp, i)
            group_store(sp, NG, B * T - NG * UNIT)

        R_BITS = 8
        R_END = R_BITS + 3 * NBITS

        def route_pe(pe):
            n = [0]

            def mm(out_, lhsT, rhs, ve, ac=0):
                pe.wait_ge(rt_dve, ve)
                if ac:
                    pe.wait_ge(rt_act, ac)
                n[0] += 1
                nc.tensor.matmul(out_, lhsT, rhs, start=True, stop=True).then_inc(rt_pe, 1)
            for i in range(EARLY_G):
                for a in "xh":
                    group_mm(pe, a, i)
            pe.wait_ge(rt_in, 16 * 5)
            pe.wait_ge(rt_dve, 2)
            nc.tensor.transpose(bank[4][0:1, 0:P], col(C_MAX), ident[:, :]).then_inc(rt_pe, 1)
            mm(bank[5][:, 0:1], rowx[:, :], ident[0:1, 0:1], 4)
            mm(bank[6][:, 0:1], group, col(C_SUM), 5, 1)

            def bit(i):
                pe.wait_ge(rt_dve, i * 3 + (R_BITS + 1))
                nc.tensor.matmul(bank[7][:, 0:1], group, col(C_CNT), start=True, stop=True).then_inc(rt_pe, 1)
            pairs = NG - EARLY_G
            with pe.Fori(0, pairs) as i:
                bit(i * 2)
                group_mm(pe, "x", i + EARLY_G)
                bit(i * 2 + 1)
                group_mm(pe, "h", i + EARLY_G)
            bit(pairs * 2)
            group_mm(pe, "x", NG, B * T - NG * UNIT)
            bit(pairs * 2 + 1)
            group_mm(pe, "h", NG, B * T - NG * UNIT)
            with pe.Fori(pairs * 2 + 2, NBITS) as i:
                bit(i)
            mm(bank[4][:, 0:1], group, col(C_GT), R_END + 2)
            mm(bank[5][:, 0:1], below, col(C_EQ), R_END + 4)
            mm(bank[6][:, 0:1], below, col(C_CNT), R_END + 10)
            pe.wait_ge(t_ev["x"], NGA)
            pe.wait_ge(t_ev["h"], NGA)
            for j, (src, ve) in enumerate(((prob, R_END + 10), (pick, R_END + 15), (flag, R_END + 17))):
                pe.wait_ge(rt_dve, ve)
                for k in range(KB):
                    w = min(P, T - k * P)
                    t = nc.tensor.transpose(bank[j][0:w, k * P:(k + 1) * P], src[:, k * P:k * P + w], ident[:, :])
                t.then_inc(rt_pe, 1)

        RT_SLOTS = 3 + NBITS + 3

        def route_act(act):
            for i in range(EARLY_G):
                group_ev(act, i)
            act.wait_ge(rt_dve, 5)
            nc.scalar.activation(prob, lgr, ACT.Exp, bias=col(C_NEG), accum_out=col(C_SUM)).then_inc(rt_act, 1)
            with act.Fori(EARLY_G, NG) as i:
                group_ev(act, i)
            group_ev(act, NG, B * T - NG * UNIT)

        def route_dve(dve):
            n = [0]

            def did(ins):
                n[0] += 1
                ins.then_inc(rt_dve, 1)
                dve.wait_ge(rt_dve, n[0])
            dve.wait_ge(rt_in, 16 * 5)
            did(nc.vector.memset(ones_t, 1.0))
            dve.wait_ge(lg_moved, 16 * E)
            did(nc.vector.tensor_reduce(col(C_MAX), lgr, AX.X, ALU.max))
            dve.wait_ge(rt_pe, 1)
            did(nc.vector.tensor_reduce(rowe, bank[4][0:1, 0:P].rearrange("p (e b) -> p e b", e=E), AX.X,
                                        ALU.max))
            did(nc.vector.tensor_copy(rowx.rearrange("p (e b) -> p e b", e=E),
                                      rowe.rearrange("p (e o) -> p e o", o=1).to_broadcast([1, E, B])))
            dve.wait_ge(rt_pe, 2)
            did(nc.vector.tensor_scalar(col(C_NEG), bank[5][:, 0:1], -1.0, None, ALU.mult))
            dve.wait_ge(rt_pe, 3)
            did(nc.vector.reciprocal(col(C_INV), bank[6][:, 0:1]))
            did(nc.vector.tensor_scalar(prob, prob, col(C_INV), None, ALU.mult))
            did(nc.vector.memset(coli(C_THR), 0))
            assert n[0] == R_BITS
            with dve.Fori(0, NBITS) as i:
                nc.vector.tensor_tensor(coli(C_CAND), coli(C_THR), bitI[:, bass.ds(i, 1)],
                                        ALU.bitwise_or).then_inc(rt_cand, 1)
                dve.wait_ge(rt_cand, i + 1)
                nc.vector.tensor_scalar(flag, prob, col(C_CAND), None, ALU.is_ge, ALU.add,
                                        accum_out=col(C_CNT)).then_inc(rt_dve, 1)
                dve.wait_ge(rt_pe, i + 4)
                nc.vector.tensor_scalar(coli(C_ADD), bank[7][:, 0:1], float(CAP), bitF[:, bass.ds(i, 1)], ALU.is_ge,
                                        ALU.mult).then_inc(rt_dve, 1)
                dve.wait_ge(rt_dve, i * 3 + (R_BITS + 2))
                nc.vector.tensor_tensor(coli(C_THR), coli(C_THR), coli(C_ADD), ALU.bitwise_or).then_inc(rt_dve, 1)
                dve.wait_ge(rt_dve, i * 3 + (R_BITS + 3))
            n[0] += 3 * NBITS
            did(nc.vector.tensor_scalar(flag, prob, col(C_THR), None, ALU.is_gt))
            did(nc.vector.tensor_reduce(col(C_GT), flag, AX.X, ALU.add))
            did(nc.vector.tensor_scalar(lgr, prob, col(C_THR), None, ALU.is_equal))
            did(nc.vector.tensor_reduce(col(C_EQ), lgr, AX.X, ALU.add))
            did(nc.vector.tensor_tensor_scan(pick, ones_t, lgr, 0.0, ALU.mult, ALU.add))
            dve.wait_ge(rt_pe, 3 + NBITS + 2)
            did(nc.vector.tensor_scalar(pick, pick, bank[5][:, 0:1], bank[4][:, 0:1], ALU.add, ALU.add))
            did(nc.vector.tensor_scalar(pick, pick, float(CAP), None, ALU.is_le))
            did(nc.vector.tensor_tensor(pick, pick, lgr, ALU.mult))
            did(nc.vector.tensor_tensor(pick, pick, flag, ALU.add))
            did(nc.vector.tensor_reduce(col(C_CNT), pick, AX.X, ALU.add))
            did(nc.vector.tensor_tensor_scan(flag, ones_t, pick, 0.0, ALU.mult, ALU.add))
            did(nc.vector.scalar_tensor_tensor(flag, pick, -2.0 * CAP, flag, ALU.mult, ALU.add))
            dve.wait_ge(rt_pe, RT_SLOTS)
            did(nc.vector.tensor_scalar(slotI, flag, bank[6][:, 0:1], 2.0 * CAP - 1, ALU.add, ALU.add))
            did(nc.vector.tensor_scalar(lgr.bitcast(I32), slotI, P - 1, None, ALU.bitwise_and))
            did(nc.vector.tensor_copy(pick, lgr.bitcast(I32)))
            did(nc.vector.tensor_scalar(slotI, slotI, 7, None, ALU.logical_shift_right))
            did(nc.vector.tensor_copy(flag, slotI))
            assert n[0] == R_END + 17
            for name, a in tokT.items():
                did(nc.vector.memset(a[:, KB - 1, :], 2.0 * CAP / P if name == "hi" else 0.0))
            w = T - (KB - 1) * P
            for j, a in enumerate((tokT["w"], tokT["lo"], tokT["hi"])):
                dve.wait_ge(rt_pe, RT_SLOTS + 1 + j)
                did(nc.vector.tensor_copy(a[:, 0:KB - 1, :], bank[j][:, 0:(KB - 1) * P].rearrange(
                    "p (k c) -> p k c", c=P)))
                did(nc.vector.tensor_copy(a[0:w, KB - 1, :], bank[j][0:w, (KB - 1) * P:KB * P]))
            dve.wait_ge(place_in, 16)
            wT = tokT["w"]
            for i in range(3):
                for k in range(KB):
                    ins = nc.vector.tensor_copy(
                        place[:, :, k * B:(k + 1) * B, 3 + i:4 + i].rearrange("p e b o -> p e (b o)"),
                        wT[:, k, :].rearrange("p (e b) -> p e b", e=E))
                did(ins)
                if i < 2:
                    for k in range(KB):
                        part = place[:, :, k * B:(k + 1) * B, 3 + i:4 + i].rearrange("p e b o -> p e (b o)")
                        ins = nc.vector.tensor_tensor(wT[:, k, :].rearrange("p (e b) -> p e b", e=E),
                                                      wT[:, k, :].rearrange("p (e b) -> p e b", e=E), part,
                                                      ALU.subtract)
                    did(ins)

        C = {n: sem(f"slot_{n}") for n in ("hi", "lo", "told", "mm", "cp", "tr", "sum", "idx")}
        M = {n: sem(f"moe_{n}") for n in ("tr", "xe", "hid", "gelu", "out", "bias", "scaled")}
        gathered = [sem(f"gathered{i}") for i in range(3)]
        scattered = [sem(f"scattered{i}") for i in range(2)]

        def hot_dve(dve, e):
            s = e % 2
            if e >= 2:
                dve.wait_ge(C["mm"], e - 1)
            if e:
                dve.wait_ge(C["told"], e)

            def per_tile(a, w):
                return a[:, :, e * B:(e + 1) * B].rearrange("p k (b o) -> p k b o", o=1).to_broadcast([P, KB, B, w])

            def over_tiles(w):
                return lowx[:, 0:w].rearrange("p (k b w) -> p k b w", k=1, b=1).to_broadcast([P, KB, B, w])
            nc.vector.tensor_tensor(hot_hi.rearrange("p (k b) w -> p k b w", k=KB), per_tile(tokT["hi"], 8),
                                    over_tiles(8), ALU.is_equal).then_inc(C["hi"], 1)
            nc.vector.tensor_tensor(hot_lo[s].rearrange("p (k b) w -> p k b w", k=KB), per_tile(tokT["lo"], P),
                                    over_tiles(P), ALU.is_equal).then_inc(C["lo"], 1)
            dve.wait_ge(C["hi"], e + 1)
            nc.vector.tensor_tensor(
                told[s],
                hot_hi.rearrange("p t (o w) -> p t o w", o=1).to_broadcast([P, KB * B, SETS, 8]),
                place[:, e, :, :].rearrange("p t (s o) -> p t s o", o=1).to_broadcast([P, KB * B, SETS, 8]),
                ALU.mult).then_inc(C["told"], 1)

        def slots_pe(pe, e):
            s = e % 2
            pe.wait_ge(C["lo"], e + 1)
            pe.wait_ge(C["told"], e + 1)
            if e:
                pe.wait_ge(C["sum"], e)
            for t in range(KB * B):
                mm = nc.tensor.matmul(bank[7][0:SETS * 8, 0:P], told[s][:, t, :, :].rearrange("p s w -> p (s w)"),
                                      hot_lo[s][:, t, :], start=(t == 0), stop=(t == KB * B - 1))
            mm.then_inc(C["mm"], 1)

        def slots_tr(pe, e):
            pe.wait_ge(C["cp"], e + 1)
            nc.tensor.transpose(bank[7][:, P:P + SETS * 8], found, ident[0:SETS * 8, 0:SETS * 8]).then_inc(C["tr"], 1)

        def slots_act(act, e):
            act.wait_ge(C["mm"], e + 1)
            if e:
                act.wait_ge(C["tr"], e)
            nc.scalar.copy(found, bank[7][0:SETS * 8, 0:P]).then_inc(C["cp"], 1)

        def slots_dve(dve, e):
            dve.wait_ge(C["tr"], e + 1)
            parts = bank[7][:, P:P + SETS * 8].rearrange("p (v s w) -> p v w s", v=2, s=3)
            nc.vector.tensor_reduce(chosen, parts, AX.X, ALU.add).then_inc(C["sum"], 1)
            dve.wait_ge(C["sum"], e + 1)
            nc.vector.tensor_copy(idx[:, e, :], chosen[:, 0, :]).then_inc(C["idx"], 1)
            nc.vector.tensor_copy(weight[:, e, :], chosen[:, 1, :]).then_inc(C["idx"], 1)
            dve.wait_ge(C["idx"], 2 * e + 2)

        def tile_of(u, j):
            return u // 2, u % 2 * TPU + j

        def moe_pool(pool):
            def gather(u):
                if u % 2 == 0:
                    pool.wait_ge(C["idx"], u + 2)
                if u >= 3:
                    pool.wait_ge(M["tr"], u - 2)
                for j in range(TPU):
                    e, g = tile_of(u, j)
                    pool.indirect_dma_start(gath[u % 3][:, j, :], None, x_rows, bass.IndirectOffsetOnAxis(
                        ap=idx[:, e, g:g + 1], axis=0)).then_inc(gathered[u % 3], 16)

            def scatter(u):
                pool.wait_ge(M["scaled"], u + 1)
                if u % 2 == 0 and u:
                    for i in range(2):
                        pool.wait_ge(scattered[i], 16 * TPU * (u // 2))
                for j in range(TPU):
                    e, g = tile_of(u, j)
                    pool.indirect_dma_start(out, bass.IndirectOffsetOnAxis(ap=idx[:, e, g:g + 1], axis=0),
                                            oute[u % 2][:, j, :], None, compute_op=ALU.add).then_inc(
                                                scattered[u % 2], 16)
            pool.wait_ge(t_st["x"], 16 * NGA)
            pool.wait_ge(t_st["h"], 16 * NGA)
            gather(0)
            gather(1)
            for u in range(UNITS):
                if u + 2 < UNITS:
                    gather(u + 2)
                scatter(u)
            for i in range(2):
                pool.wait_ge(scattered[i], 16 * TPU * (UNITS // 2))

        def moe_pe(pe):
            def rows_to_channels(u):
                pe.wait_ge(gathered[u % 3], 16 * TPU * (u // 3 + 1))
                if u:
                    pe.wait_ge(M["xe"], u)
                for j in range(TPU):
                    t = nc.tensor.transpose(bank[4][:, j * P:(j + 1) * P], gath[u % 3][:, j, :], ident[:, :])
                t.then_inc(M["tr"], 1)

            def hidden(u):
                pe.wait_ge(M["xe"], u + 1)
                for f in range(FT):
                    if u:
                        pe.wait_ge(M["gelu"], FT * (u - 1) + f + 1)
                    nc.tensor.matmul(bank[f][:, 0:UNIT], w1_s[:, u // 2, f * P:(f + 1) * P], xe[u % 2], start=True,
                                     stop=True).then_inc(M["hid"], 1)

            def outputs(u):
                if u >= 2:
                    pe.wait_ge(M["bias"], u - 1)
                for j in range(TPU):
                    for f in range(FT):
                        if j == 0:
                            pe.wait_ge(M["gelu"], FT * u + f + 1)
                        mm = nc.tensor.matmul(bank[5 + u % 2][:, j * P:(j + 1) * P],
                                              hid[u % 2][:, f, j * P:(j + 1) * P],
                                              w2_s[:, u // 2, f * P:(f + 1) * P], start=(f == 0), stop=(f == FT - 1))
                mm.then_inc(M["out"], 1)
            slots_pe(pe, 0)
            slots_tr(pe, 0)
            pe.wait_ge(w_in, 32)
            rows_to_channels(0)
            for u in range(UNITS):
                e = (u + 3) // 2
                finds = (u % 2 == 1 or u == 0) and e < E
                hidden(u)
                if u + 1 < UNITS:
                    rows_to_channels(u + 1)
                if finds:
                    slots_pe(pe, e)
                    if u == 0:
                        slots_tr(pe, e)
                outputs(u)
                if finds and u:
                    slots_tr(pe, e)

        def moe_act(act):
            def channels(u):
                act.wait_ge(M["tr"], u + 1)
                if u >= 2:
                    act.wait_ge(M["hid"], FT * (u - 1))
                nc.scalar.copy(xe[u % 2], bank[4][:, 0:UNIT]).then_inc(M["xe"], 1)

            def gelu(u):
                if u >= 2:
                    act.wait_ge(M["out"], u - 1)
                for f in range(FT):
                    act.wait_ge(M["hid"], FT * u + f + 1)
                    nc.scalar.activation(hid[u % 2][:, f, :], bank[f][:, 0:UNIT], ACT.Gelu,
                                         bias=vec[:, V_B1 + u // 2 * FT + f:V_B1 + u // 2 * FT + f + 1]).then_inc(
                                             M["gelu"], 1)
            slots_act(act, 0)
            channels(0)
            for u in range(UNITS):
                e = (u + 3) // 2
                gelu(u)
                if u + 1 < UNITS:
                    channels(u + 1)
                if (u % 2 == 1 or u == 0) and e < E:
                    slots_act(act, e)

        def moe_dve(dve):
            def weigh(u):
                dve.wait_ge(M["out"], u + 1)
                if u >= 2:
                    dve.wait_ge(scattered[u % 2], 16 * TPU * (u // 2))
                nc.vector.tensor_tensor(
                    oute[u % 2], bank[5 + u % 2][:, 0:UNIT].rearrange("p (j c) -> p j c", c=P),
                    b2_s[:, u // 2:u // 2 + 1, :].to_broadcast([P, TPU, P]), ALU.add).then_inc(M["bias"], 1)
                dve.wait_ge(M["bias"], u + 1)
                for j in range(TPU):
                    e, g = tile_of(u, j)
                    ins = nc.vector.tensor_scalar(oute[u % 2][:, j, :], oute[u % 2][:, j, :],
                                                  weight[:, e, g:g + 1], None, ALU.mult)
                ins.then_inc(M["scaled"], 1)
            hot_dve(dve, 0)
            slots_dve(dve, 0)
            hot_dve(dve, 1)
            slots_dve(dve, 1)
            hot_dve(dve, 2)
            dve.wait_ge(b2_in, 16)
            for u in range(UNITS):
                if u % 2 == 0 and u and u // 2 + 2 < E:
                    hot_dve(dve, u // 2 + 2)
                weigh(u)
                if u % 2 == 1 and (u + 3) // 2 < E:
                    slots_dve(dve, (u + 3) // 2)

        @block.sync
        def _(sp):
            tok_sync(sp)
            sp.wait_ge(stage_done[1], 4)
            sp.dma_start(h_save, hT).then_inc(h_saved, 16)
            sp.wait_ge(stage_done[4], 4)
            sp.dma_start(hT, h_save).then_inc(h_back, 16)
            sp.wait_ge(stage_done[6], 4)
            for dst, src in ((group, group_c), (below, below_c), (bitI, bits_i), (bitF, bits_f)):
                sp.dma_start(dst, src).then_inc(rt_in, 16)
            sp.dma_start(w1_s, w1).then_inc(w_in, 16)
            sp.dma_start(w2_s, w2).then_inc(w_in, 16)
            sp.wait_ge(stage_done[7], 4)
            sp.dma_start(lowx, iota_c).then_inc(rt_in, 16)
            sp.dma_start(place.rearrange("p e t s -> p (e t s)"), place_c).then_inc(place_in, 16)
            route_sync(sp)
            rows_sync(sp)
            sp.wait_ge(t_cp["x"], NGA)
            sp.dma_start(b2_s.rearrange("p e c -> p (e c)"), b2).then_inc(b2_in, 16)

        @block.tensor
        def _(pe):
            for k, stage in enumerate((tok_pe, ln_in.pe, conv_pe, steps_pe, scan_pe, gate_pe, ln_blk.pe, ln_moe.pe)):
                stage(pe)
                fence(pe, k)
            logits_pe(pe)
            route_pe(pe)
            moe_pe(pe)

        @block.scalar
        def _(act):
            for k, stage in enumerate((tok_act, ln_in.act, conv_act, steps_act, scan_act, gate_act, ln_blk.act,
                                       ln_moe.act)):
                stage(act)
                fence(act, k)
            logits_act(act)
            route_act(act)
            moe_act(act)

        @block.vector
        def _(dve):
            for k, stage in enumerate((nothing, ln_in.dve, lambda e: (conv_setup_dve(e), conv_dve(e)), steps_dve,
                                       scan_dve, gate_dve, block_dve, ln_moe.dve)):
                stage(dve)
                fence(dve, k)
            route_dve(dve)
            moe_dve(dve)

        @block.gpsimd
        def _(pool):
            for k, stage in enumerate((tok_pool, nothing, nothing, steps_pool, lambda e: (e.wait_ge(h_saved, 16), scan_pool(e)),
                                       nothing, nothing, nothing)):
                stage(pool)
                fence(pool, k)
            rows_pool(pool)
            moe_pool(pool)


def kernel(x, txt, L0_tok_W, L0_tok_b, L0_tok_cls_token, L0_tok_pos_emb, L0_attn_in_w, L0_attn_in_b, L0_attn_conv_w,
           L0_attn_conv_b, L0_attn_xp_w, L0_attn_xp_b, L0_attn_dt_w, L0_attn_dt_b, L0_attn_A_log, L0_attn_D_skip,
           L0_attn_out_w, L0_attn_out_b, L0_attn_ln_g, L0_attn_ln_b, L0_ffn_Wr, L0_ffn_W1, L0_ffn_b1, L0_ffn_W2,
           L0_ffn_b2):
    import ml_dtypes
    import numpy as np
    import concourse.bacc as bacc
    from concourse.bass_utils import run_bass_kernel_spmd

    f32 = np.float32

    def cols(v):
        return np.asarray(v).reshape(-1, P).T

    def halves(w):
        w = np.asarray(w)
        return w.reshape(-1, P, w.shape[1]).transpose(1, 0, 2)

    def const(v):
        return np.full((P, 1), v, f32)

    patches = np.asarray(x).reshape(B, 3, 11, 16, 13, 16).transpose(0, 3, 5, 1, 2, 4).reshape(B, KT, P, NPATCH)
    patches = np.pad(patches, ((0, 0), (0, 0), (0, 0), (1, 0)))
    tok_cols = np.zeros((3, TI), f32)
    tok_cols[0] = np.asarray(L0_tok_pos_emb).reshape(-1)
    tok_cols[1, 0] = 1
    tok_cols[2, 1:] = 1
    xpb = np.asarray(L0_attn_xp_b)
    sel = np.zeros((3, 32, 32, P), f32)
    for j in range(32):
        sel[:, j, j] = 0.5 if j < NS else 1
    q = np.arange(P)
    same = q[:, None] // B == q[None] // B
    bits = (1 << np.arange(NBITS - 1, -1, -1)).astype(np.int32)
    place = np.zeros((P, E, KB, B, SETS), f32)
    place[..., 0] = q[:, None, None, None]
    place[..., 1] = T * np.arange(B)
    place[..., 2] = P * np.arange(KB)[:, None]
    arrays = {
        "patches": patches.transpose(0, 2, 1, 3),
        "txt": np.asarray(txt).transpose(2, 0, 1),
        "tokw": halves(np.asarray(L0_tok_W).T),
        "tok_rows": np.stack([np.ones(P, f32), np.asarray(L0_tok_cls_token).reshape(-1), np.asarray(L0_tok_b)]),
        "tok_cols": tok_cols,
        "vecs": np.concatenate([
            cols(L0_attn_in_b), cols(L0_attn_conv_b), cols(xpb[2 * NS:]), cols(L0_attn_dt_b), cols(L0_attn_D_skip),
            cols(L0_attn_out_b), cols(L0_attn_ln_g), cols(L0_attn_ln_b), const(1e-5), const(LOG_EPS_HALF),
            cols(L0_ffn_b1)], axis=1),
        "inw": np.asarray(L0_attn_in_w).T,
        "convw": np.asarray(L0_attn_conv_w).reshape(NH, P, KC).transpose(1, 0, 2).reshape(P, NH * KC),
        "xpw": halves(np.asarray(L0_attn_xp_w).T),
        "xpb": xpb[:2 * NS].reshape(-1, 1),
        "dtw": halves(np.asarray(L0_attn_dt_w).T),
        "alog": halves(L0_attn_A_log),
        "outw": halves(np.asarray(L0_attn_out_w).T),
        "wr": np.asarray(L0_ffn_Wr),
        "w1": np.asarray(L0_ffn_W1).transpose(1, 0, 2),
        "w2": np.asarray(L0_ffn_W2).reshape(E, FT, P, P).transpose(2, 0, 1, 3).reshape(P, E, FT * P),
        "b2": np.broadcast_to(np.asarray(L0_ffn_b2).reshape(1, E * P), (P, E * P)),
        "ident_c": np.eye(P, dtype=f32),
        "sel_c": sel.reshape(96, 32, P).astype(ml_dtypes.bfloat16),
        "group_c": same.astype(f32),
        "below_c": (same & (q[:, None] < q[None])).astype(f32),
        "mean_c": np.full((P, P), 1 / P, f32),
        "iota_c": np.tile(np.arange(P), (P, 1)).astype(ml_dtypes.bfloat16),
        "place_c": place.reshape(P, -1).astype(ml_dtypes.bfloat16),
        "bits_i": np.tile(bits, (P, 1)),
        "bits_f": np.tile(bits.astype(f32), (P, 1)),
    }
    nc = bacc.Bacc("TRN2", target_bir_lowering=False, num_devices=1)
    ins, aps = {}, {}
    for name, a in arrays.items():
        ins[name + "_in"] = np.ascontiguousarray(a)
        aps[name] = nc.dram_tensor(name + "_in", a.shape, mybir.dt.from_np(a.dtype), kind="ExternalInput").ap()
    out = nc.dram_tensor("out", (B * T, P), F32, kind="ExternalOutput").ap()
    build_program(nc, **aps, out=out)
    r = run_bass_kernel_spmd(nc, [ins], core_ids=[0])
    return r.results[0]["out"].reshape(B, T, P)
```

```python
from contextlib import ExitStack

import concourse.bass as bass
from concourse import mybir

ALU = mybir.AluOpType
ACT = mybir.ActivationFunctionType
AX = mybir.AxisListType
F32 = mybir.dt.float32
BF16 = mybir.dt.bfloat16
I32 = mybir.dt.int32

P = 128
B = 16
NPATCH = 143
TI = NPATCH + 1
T = TI + 128
KT = 6
NH = 2
NS = 16
KC = 4
E = 8
FT = 4
CAP = 1024
UNIT = 512
UNITS = E * CAP // UNIT
TPU = UNIT // P
NG = B * T // UNIT
SETS = 6
LOG_FLOOR = -13.815510557964274
LOG_EPS_HALF = 9.210340371976184
SERIES_BELOW = 1.0 / 128
KB = -(-T // P)
NBITS = 30
WAYS = 4
NSTEP = NBITS // 2

S_GONE = -104.0

RANGES = [(0, 16, 16), (16, 48, 8), (64, T - 64, 2)]

V_INB, V_CB, V_DTIN, V_DTB, V_D, V_OUTB, V_LNG, V_LNB, V_EPS, V_LE, V_B1 = 0, 4, 6, 8, 10, 12, 13, 14, 15, 16, 17
NV = V_B1 + E * FT


def each_batch(eng, body):
    body(0, 0, True)
    body(1, 1, True)
    with eng.Fori(1, B // 2) as i:
        for s in range(2):
            body(i * 2 + s, s, False)


def skewed(eng, head, tail):
    head(0, 0, True)
    head(1, 1, True)
    tail(0, 0, True)
    head(2, 0, False)
    tail(1, 1, True)
    with eng.Fori(1, B // 2 - 1) as i:
        for s in range(2):
            head(i * 2 + s + 1, 1 - s, False)
            tail(i * 2 + s, s, False)
    head(B - 1, 1, False)
    tail(B - 2, 0, False)
    tail(B - 1, 1, False)


def pipelined(eng, *steps):
    lag = max(g for _, g in steps)
    start = lag + 2 + lag % 2

    def turn(i):
        for body, g in steps:
            if 0 <= i - g < B:
                body(i - g, (i - g) % 2)
    for i in range(start):
        turn(i)
    with eng.Fori(start // 2, B // 2) as k:
        for p in range(2):
            for body, g in steps:
                body(k * 2 + (p - g), (p - g) % 2)
    for i in range(B, B + lag):
        turn(i)


def freed(eng, sem, b, back, per=1):
    if not isinstance(b, int):
        eng.wait_ge(sem, b * per + (1 - back) * per)
    elif b >= back:
        eng.wait_ge(sem, min(b + 1 - back, B) * per)


def nothing(*_):
    pass


def build_program(nc, patches, txt, tokw, tok_rows, tok_cols, vecs, inw, convw, xpw, xprow, xpb, dtw, alog, outw, wr,
                  w1, w2, b2, ident_c, sel_c, group_c, below_c, mean_c, steps_c, iota_c, place_c, out):
    h_save = nc.dram_tensor("h_save", [P, B, T], F32, kind="Internal").ap()
    x_rows = nc.dram_tensor("x_rows", [B * T, P], F32, kind="Internal").ap()
    with ExitStack() as ctx:
        def sb(name, shape, dt=F32):
            return ctx.enter_context(nc.sbuf_tensor(name, shape, dt))

        def sem(name):
            return ctx.enter_context(nc.semaphore(name))

        bank = [ctx.enter_context(nc.psum_tensor(f"bank{i}", [P, 512], F32)) for i in range(8)]

        WORK = 10952
        first = sb("first", [P, 2 * KT * TI + KT * P + 2 * NH * T])
        work = sb("work", [P, WORK])
        xn = sb("xn", [P, B, T])
        xs = sb("xs", [P, B, NH, T])
        dt = sb("dt", [P, B, NH, T])
        dtx = sb("dtx", [P, B, NH, T])
        bc = sb("bc", [96, B, T], BF16)
        vec = sb("vec", [P, NV])
        nvec = sb("nvec", [P, 2 * NH])
        ident = sb("ident", [P, P])
        sel = sb("sel", [96, 32, P], BF16)
        meanm = sb("meanm", [P, P])
        xpb_s = sb("xpb_s", [32, 1])
        inw_s = sb("inw_s", [P, 2 * NH * P])
        xpw_s = sb("xpw_s", [P, NH, 32])
        xprow_s = sb("xprow_s", [P, NH, NH * P])
        wdt = sb("wdt", [P, NH, NH * P])
        dt_bias = sb("dt_bias", [P, NH])
        dtw_s = sb("dtw_s", [P, NH, NH * P])
        outw_s = sb("outw_s", [P, NH, P])
        convw_s = sb("convw_s", [P, NH * KC])
        negA = sb("negA", [P, NH, NS])
        wr_s = sb("wr_s", [P, E])
        group = sb("group", [P, P])
        below = sb("below", [P, P])
        steps = sb("steps", [P, NSTEP, WAYS - 1], I32)
        lowx = sb("lowx", [P, P], BF16)

        def view(arr, off, *shape, rows=P, dtype=F32):
            size = 1
            for d in shape:
                size *= d
            v = arr[0:rows, off:off + (size if dtype != BF16 else size // 2)]
            if dtype != F32:
                v = v.bitcast(dtype)
            names = "abcd"[:len(shape)]
            return v if len(shape) == 1 else v.rearrange(
                f"p ({' '.join(names)}) -> p {' '.join(names)}", **dict(zip(names, shape)))

        hT = view(work, 0, B, T)
        oT = dt[:, :, :, :].rearrange("p b h t -> p (b h t)")[:, 0:B * T].rearrange("p (b t) -> p b t", b=B)

        class Scratch:
            def __init__(self, off=B * T):
                self.off = off

            def take(self, *shape, **kw):
                size = 1
                for d in shape:
                    size *= d
                v = view(work, self.off, *shape, **kw)
                self.off += size if kw.get("dtype") != BF16 else size // 2
                assert self.off <= WORK, self.off
                return v

            def two(self, *shape, **kw):
                return [self.take(*shape, **kw) for _ in range(2)]

        def row(arr, b):
            return arr[:, bass.ds(b, 1), :].rearrange("p o t -> p (o t)")

        def both(arr, b):
            return arr[:, bass.ds(b, 1), :, :].rearrange("p o h t -> p (o h) t")

        stage_done = [sem(f"stage{k}_done") for k in range(3)]

        def fence(eng, k):
            eng.drain().then_inc(stage_done[k], 1)
            eng.wait_ge(stage_done[k], 4)

        passed = sem("passed")

        def apart(eng):
            eng.sem_inc(passed, 1)

        block = ctx.enter_context(nc.Block())

        class Norm:

            def __init__(self, name, src, dst, src_ok, m):
                self.src, self.dst, self.src_ok, self.turn = src, dst, src_ok, (self, 1)
                self.mean, self.cent, self.sq, self.var, self.log, self.rstd, self.out = (
                    sem(f"{name}_{n}") for n in ("mean", "cent", "sq", "var", "log", "rstd", "out"))
                self.sqb, self.logb, self.rsb = m.two(T), m.two(T), m.two(T)

            def pe_mean(self, b, s):
                pe = nc.tensor
                pe.wait_ge(self.src_ok, b + 1)
                freed(pe, self.turn[0].cent, b, self.turn[1])
                pe.matmul(bank[5][:, 0:T], meanm[:, :], row(self.src, b), start=True, stop=True).then_inc(self.mean, 1)

            def pe_var(self, b, s):
                pe = nc.tensor
                pe.wait_ge(self.sq, b + 1)
                freed(pe, self.turn[0].log, b, self.turn[1])
                pe.matmul(bank[6][:, 0:T], meanm[:, :], self.sqb[s], start=True, stop=True).then_inc(self.var, 1)

            def act_square(self, b, s):
                act = nc.scalar
                act.wait_ge(self.cent, b + 1)
                freed(act, self.var, b, 2)
                act.activation(self.sqb[s], row(self.dst, b), ACT.Square).then_inc(self.sq, 1)

            def act_rstd(self, b, s):
                act = nc.scalar
                act.wait_ge(self.var, b + 1)
                act.activation(self.logb[s], bank[6][:, 0:T], ACT.Ln, bias=vec[:, V_EPS:V_EPS + 1]).then_inc(
                    self.log, 1)
                act.wait_ge(self.log, b + 1)
                freed(act, self.out, b, 2)
                act.activation(self.rsb[s], self.logb[s], ACT.Exp, scale=-0.5).then_inc(self.rstd, 1)

            def dve_center(self, b, s):
                dve = nc.vector
                dve.wait_ge(self.mean, b + 1)
                dve.tensor_tensor(row(self.dst, b), row(self.src, b), bank[5][:, 0:T], ALU.subtract).then_inc(
                    self.cent, 1)

            def dve_scale(self, b, s):
                dve = nc.vector
                dve.wait_ge(self.rstd, b + 1)
                dve.tensor_tensor(row(self.dst, b), row(self.dst, b), self.rsb[s], ALU.mult).then_inc(self.out, 1)

        (consts_in, late_in, tok_mm, tok_ev, in_mm, in_ev, conv_tap, conv_ok, c_exp, c_log, c_sig, x_ok, pads_ok,
         nvec_ok, negA_exp, negA_ok, h_saved) = (
            sem(n) for n in ("consts_in", "late_in", "tok_mm", "tok_ev", "in_mm", "in_ev", "conv_tap", "conv_ok",
                             "c_exp", "c_log", "c_sig", "x_ok", "pads_ok", "nvec_ok", "negA_exp", "negA_ok",
                             "h_saved"))
        batch_in = [sem(f"batch_in{s}") for s in range(2)]
        m = Scratch()
        pat = [view(first, i * KT * TI, KT, TI) for i in range(2)]
        tokw_s = view(first, 2 * KT * TI, KT, P)
        dlog = [view(first, 2 * KT * TI + KT * P + i * NH * T, NH, T) for i in range(2)]
        tokr_s = m.take(P, rows=3)
        tokc_s = m.take(TI, rows=3)
        xpad = m.two(NH, T + KC - 1)
        norm_in = Norm("norm_in", hT, xn, tok_ev, m)
        EARLY = [(vec[:, :], vecs), (tokw_s, tokw), (tokr_s, tok_rows), (tokc_s, tok_cols), (meanm[:, :], mean_c),
                 (inw_s[:, :], inw), (convw_s[:, :], convw)]
        LATE = [(ident[:, :], ident_c), (xpw_s[:, :, :], xpw), (xprow_s[:, :, :], xprow), (xpb_s[:, :], xpb), (dtw_s[:, :, :], dtw),
                (negA[:, :, :], alog), (outw_s[:, :, :], outw), (wr_s[:, :], wr), (sel[:, :, :], sel_c), (group[:, :], group_c), (below[:, :], below_c),
                (steps[:, :, :], steps_c), (lowx[:, :], iota_c)]

        (w_mm, w_ev, bias_ok, xp_mm, bcf_ev, dt_mm, dt_abs, dt_exp, dt_log, dt_relu, dt_ser, dt_mask, dt_sel, dt_ok,
         dtx_ok, bc_rest, bc_q, bc_mid, bc_low, y_ok) = (sem(n) for n in (
             "w_mm", "w_ev", "bias_ok", "xp_mm", "bcf_ev", "dt_mm", "dt_abs", "dt_exp", "dt_log", "dt_relu",
             "dt_ser", "dt_mask", "dt_sel", "dt_ok", "dtx_ok", "bc_rest", "bc_q", "bc_mid", "bc_low", "y_ok"))
        drel = m.two(NH, T)
        dser, dmask = m.take(NH, T), m.take(NH, T, dtype=I32)
        bcf, bcr = m.two(T, rows=32), m.take(T, rows=32)
        bcq = m.two(T, rows=32, dtype=BF16)

        def steps_pe(pe):
            def setup():
                pe.wait_ge(late_in, 16 * len(LATE))
                for a in range(NH):
                    for k in range(NH):
                        mm = nc.tensor.matmul(bank[(4, 7)[a]][:, 0:NH * P], xprow_s[:, k, a * P:(a + 1) * P],
                                              dtw_s[:, k, :], start=(k == 0), stop=(k == NH - 1))
                    mm.then_inc(w_mm, 1)
                for h in range(NH):
                    for k in range(NH):
                        mm = nc.tensor.matmul(bank[1][:, h:h + 1], dtw_s[:, k, h * P:(h + 1) * P],
                                              vec[:, V_DTIN + k:V_DTIN + k + 1], start=(k == 0), stop=(k == NH - 1))
                mm.then_inc(w_mm, 1)
                pe.wait_ge(w_ev, NH)
                pe.wait_ge(bias_ok, 1)

            def rows(b, s):
                freed(pe, bcf_ev, b, 1)
                apart(pe)
                for k in range(NH):
                    mm = nc.tensor.matmul(bank[1][0:32, 0:T], xpw_s[:, k, :], both(xs, b)[:, k, :],
                                          start=(k == 0), stop=(k == NH - 1))
                mm.then_inc(xp_mm, 1)

            def steps(b, s):
                if isinstance(b, int) and b == 0:
                    setup()
                pe.wait_ge(x_ok, b + 1)
                freed(pe, dt_relu, b, 1, NH)
                for h in range(NH):
                    for k in range(NH):
                        mm = nc.tensor.matmul(bank[(4, 7)[h]][:, 0:T], wdt[:, k, h * P:(h + 1) * P],
                                              both(xs, b)[:, k, :], start=(k == 0), stop=(k == NH - 1))
                mm.then_inc(dt_mm, 1)
            return steps, rows

        def steps_act(act):
            def setup(b, s):
                if not (isinstance(b, int) and b == 0):
                    return
                act.wait_ge(late_in, 16 * len(LATE))
                nc.scalar.activation(negA[:, :, :], negA[:, :, :], ACT.Exp).then_inc(negA_exp, 1)
                for a in range(NH):
                    act.wait_ge(w_mm, a + 1)
                    nc.scalar.copy(wdt[:, a, :], bank[(4, 7)[a]][:, 0:NH * P]).then_inc(w_ev, 1)
                act.wait_ge(bias_ok, 1)

            def sp_a(b, s):
                act.wait_ge(dt_mm, b + 1)
                apart(act)
                for h in range(NH):
                    a = nc.scalar.activation(both(dt, b)[:, h, :], bank[(4, 7)[h]][:, 0:T], ACT.Abs,
                                             bias=dt_bias[:, h:h + 1])
                a.then_inc(dt_abs, 1)

            def sp_e(b, s):
                act.wait_ge(dt_abs, b + 1)
                apart(act)
                nc.scalar.activation(both(dt, b), both(dt, b), ACT.Exp, scale=-1.0).then_inc(dt_exp, 1)

            def sp_l(b, s):
                act.wait_ge(dt_exp, b + 1)
                freed(act, dt_ok, b, 2)
                apart(act)
                nc.scalar.activation(dlog[s], both(dt, b), ACT.Ln, bias=1.0).then_inc(dt_log, 1)

            def rows(b, s):
                act.wait_ge(xp_mm, b + 1)
                freed(act, bc_rest, b, 2)
                nc.scalar.activation(bcf[s], bank[1][0:32, 0:T], ACT.Identity, bias=xpb_s[:, :])
                nc.scalar.activation(row(bc, b)[0:32, :], bank[1][0:32, 0:T], ACT.Identity,
                                     bias=xpb_s[:, :]).then_inc(bcf_ev, 1)

            def middle(b, s):
                act.wait_ge(bc_q, b + 1)
                nc.scalar.copy(row(bc, b)[32:64, :], bcq[s]).then_inc(bc_mid, 1)

            def skip(b, s):
                act.wait_ge(dtx_ok, b + 1)
                for h in range(NH):
                    nc.scalar.activation(both(xs, b)[:, h, :], both(xs, b)[:, h, :], ACT.Copy,
                                         scale=vec[:, V_D + h:V_D + h + 1]).then_inc(y_ok, 1)
            return setup, sp_a, sp_e, sp_l, rows, middle, skip

        def steps_dve(dve):
            def setup(b, s):
                if not (isinstance(b, int) and b == 0):
                    return
                dve.wait_ge(w_mm, NH + 1)
                nc.vector.tensor_tensor(dt_bias[:, :], bank[1][:, 0:NH], vec[:, V_DTB:V_DTB + NH],
                                        ALU.add).then_inc(bias_ok, 1)
                dve.wait_ge(negA_exp, 1)
                nc.vector.tensor_scalar(negA[:, :, :], negA[:, :, :], -1.0, None, ALU.mult).then_inc(negA_ok, 1)

            def relu(b, s):
                dve.wait_ge(dt_abs, b + 1)
                freed(dve, dt_ok, b, 2)
                for h in range(NH):
                    nc.vector.tensor_scalar(drel[s][:, h, :], bank[(4, 7)[h]][:, 0:T], dt_bias[:, h:h + 1], 0.0,
                                            ALU.add, ALU.max).then_inc(dt_relu, 1)

            def series(b, s):
                freed(dve, dt_sel, b, 1)
                dve.wait_ge(dt_exp, b + 1)
                nc.vector.tensor_scalar(dser, both(dt, b), 1.0 / 3, -0.5, ALU.mult, ALU.add).then_inc(dt_ser, 1)
                nc.vector.tensor_scalar(dmask, both(dt, b), SERIES_BELOW, None, ALU.is_lt).then_inc(dt_mask, 1)

            def series_end(b, s):
                dve.wait_ge(dt_ser, 3 * b + 1)
                nc.vector.tensor_tensor(dser, dser, both(dt, b), ALU.mult).then_inc(dt_ser, 1)
                dve.wait_ge(dt_ser, 3 * b + 2)
                nc.vector.scalar_tensor_tensor(dser, dser, 1.0, both(dt, b), ALU.add, ALU.mult).then_inc(dt_ser, 1)
                dve.wait_ge(dt_ser, 3 * b + 3)
                dve.wait_ge(dt_mask, b + 1)
                dve.wait_ge(dt_log, b + 1)
                apart(dve)
                nc.vector.copy_predicated(dlog[s], dmask, dser).then_inc(dt_sel, 1)

            return setup, relu, series, series_end

        def steps_pool(pool):
            def rests(b, s):
                pool.wait_ge(bcf_ev, b + 1)
                apart(pool)
                nc.gpsimd.tensor_tensor(bcr, bcf[s], row(bc, b)[0:32, :], ALU.subtract).then_inc(bc_rest, 1)
                pool.wait_ge(bc_rest, b + 1)
                freed(pool, bc_mid, b, 2)
                apart(pool)
                nc.gpsimd.tensor_copy(bcq[s], bcr).then_inc(bc_q, 1)
                pool.wait_ge(bc_q, b + 1)
                apart(pool)
                nc.gpsimd.tensor_tensor(row(bc, b)[64:96, :], bcr, bcq[s], ALU.subtract).then_inc(bc_low, 1)
                pool.wait_ge(bc_low, b + 1)

            def total(b, s):
                pool.wait_ge(dt_sel, b + 1)
                pool.wait_ge(dt_relu, NH * b + NH)
                apart(pool)
                nc.gpsimd.tensor_tensor(both(dt, b), dlog[s], drel[s], ALU.add).then_inc(dt_ok, 1)

            def times_x(b, s):
                pool.wait_ge(dt_ok, b + 1)
                apart(pool)
                nc.gpsimd.tensor_tensor(both(dtx, b), both(dt, b), both(xs, b), ALU.mult).then_inc(dtx_ok, 1)
            return rests, total, times_x

        def start_sync(sp):
            def load(b, s, first):
                if not first:
                    sp.wait_ge(tok_mm, b - 1)
                sp.dma_start(pat[s], patches[bass.ds(b, 1)].rearrange("o p k n -> (o p) k n")).then_inc(
                    batch_in[s], 16)
                sp.dma_start(row(hT, b)[:, TI:T], txt[:, bass.ds(b, 1), :].rearrange("p o t -> p (o t)")).then_inc(
                    batch_in[s], 16)
            each_batch(sp, load)

        def start_pe(pe):
            pe.wait_ge(consts_in, 16 * len(EARLY))

            def tok(b, s):
                freed(pe, tok_ev, b, 1)
                nc.tensor.matmul(bank[0][:, 0:TI], tokr_s, tokc_s, start=True, stop=False)
                pe.wait_ge(batch_in[s], b * 16 + (32 - 16 * s))
                for k in range(KT):
                    mm = nc.tensor.matmul(bank[0][:, 0:TI], tokw_s[:, k, :], pat[s][:, k, :], start=False,
                                          stop=(k == KT - 1))
                mm.then_inc(tok_mm, 1)

            def inproj(b, s):
                pe.wait_ge(norm_in.out, b + 1)
                freed(pe, in_ev, b, 1)
                for h in range(NH):
                    mm = nc.tensor.matmul(bank[2 + h][:, 0:T],
                                          inw_s[:, h * P:(h + 1) * P], row(xn, b), start=True, stop=True)
                mm.then_inc(in_mm, 1)
            steps, rows = steps_pe(pe)
            pipelined(pe, (norm_in.pe_mean, 1), (tok, 0), (inproj, 3), (norm_in.pe_var, 1), (steps, 6), (rows, 6))

        def start_act(act):
            for dst, src in EARLY:
                act.dma_start(dst, src).then_inc(consts_in, 16)
            nc.scalar.preload_act_table_set("natural_log_exp_and_others")
            act.wait_ge(consts_in, 16 * len(EARLY))
            act.wait_ge(nvec_ok, 1)

            def evict(b, s):
                act.wait_ge(tok_mm, b + 1)
                nc.scalar.copy(row(hT, b)[:, 0:TI], bank[0][:, 0:TI]).then_inc(tok_ev, 1)

            def pad(b, s):
                act.wait_ge(in_mm, b + 1)
                freed(act, conv_ok, b, 2)
                for h in range(NH):
                    a = nc.scalar.activation(xpad[s][:, h, KC - 1:], bank[2 + h][:, 0:T], ACT.Identity, bias=vec[:, V_INB + h:V_INB + h + 1])
                a.then_inc(in_ev, 1)

            def c_e(b, s):
                act.wait_ge(conv_ok, b + 1)
                apart(act)
                nc.scalar.activation(both(dtx, b), both(xs, b), ACT.Exp, scale=-1.0).then_inc(c_exp, 1)

            def c_l(b, s):
                act.wait_ge(c_exp, b + 1)
                apart(act)
                nc.scalar.activation(both(dtx, b), both(dtx, b), ACT.Ln, bias=1.0).then_inc(c_log, 1)

            def c_s(b, s):
                act.wait_ge(c_log, b + 1)
                apart(act)
                nc.scalar.activation(both(dtx, b), both(dtx, b), ACT.Exp, scale=-1.0).then_inc(c_sig, 1)
            setup, sp_a, sp_e, sp_l, rows, middle, skip = steps_act(act)
            pipelined(act, (c_e, 5), (norm_in.act_square, 1), (c_l, 5), (evict, 0), (c_s, 5), (pad, 3), (norm_in.act_rstd, 1), (setup, 6), (sp_a, 6), (rows, 6), (sp_e, 6), (middle, 8), (sp_l, 6), (skip, 9))

        def start_dve(dve):
            for s in range(2):
                nc.vector.memset(xpad[s][:, :, 0:KC - 1], 0.0).then_inc(pads_ok, 1)
            dve.wait_ge(consts_in, 16 * len(EARLY))
            nc.vector.tensor_scalar(nvec[:, :], vec[:, V_INB:V_INB + 2 * NH], -1.0, None, ALU.mult).then_inc(nvec_ok, 1)
            dve.wait_ge(pads_ok, 2)

            def conv(b, s):
                dve.wait_ge(in_ev, b + 1)
                for k in range(KC):
                    for h in range(NH):
                        tap = convw_s[:, h * KC + k:h * KC + k + 1]
                        x_k, to = xpad[s][:, h, k:k + T], both(xs, b)[:, h, :]
                        if k == 0:
                            a = nc.vector.tensor_scalar(to, x_k, tap, vec[:, V_CB + h:V_CB + h + 1], ALU.mult,
                                                        ALU.add)
                        else:
                            dve.wait_ge(conv_tap, b * 7 + (NH * k + h - 1))
                            a = nc.vector.scalar_tensor_tensor(to, x_k, tap, to, ALU.mult, ALU.add)
                        a.then_inc(conv_ok if k == KC - 1 and h == NH - 1 else conv_tap, 1)
            setup, relu, series, series_end = steps_dve(dve)
            pipelined(dve, (relu, 7), (norm_in.dve_scale, 3), (series, 7), (norm_in.dve_center, 1), (series_end, 7), (conv, 4), (setup, 6))

        def start_pool(pool):
            for dst, src in LATE:
                pool.dma_start(dst, src).then_inc(late_in, 16)

            def silu(b, s):
                pool.wait_ge(c_sig, b + 1)
                apart(pool)
                nc.gpsimd.tensor_tensor(both(xs, b), both(xs, b), both(dtx, b), ALU.mult).then_inc(x_ok, 1)
            rests, total, times_x = steps_pool(pool)
            pipelined(pool, (total, 8), (rests, 7), (times_x, 8), (silu, 5))

        TILE = max(NH * g * (1 + tl) for _, tl, g in RANGES)
        m = Scratch(0)
        s_mask, s_u = m.take(TILE), m.take(TILE)
        s_a, s_L, s_w = m.two(TILE), m.two(TILE), m.two(TILE)
        s_c = m.two(512)
        carryL, carryH = m.take(NS, B * NH), m.take(NS, B * NH)
        s_max, s_dead, ones_c = m.take(NS), m.take(NS), m.take(1)
        alive = [m.take(NS, rows=1, dtype=I32) for _ in RANGES]
        alive4 = [m.take(NS // 4, rows=1, dtype=I32) for _ in RANGES]
        S = {n: sem(f"scan_{n}") for n in ("bmm", "cmm", "ccopy", "clip", "logsum", "logtail", "decay", "gate", "src",
                                           "inp", "state", "tail", "out", "added")}
        OF = {"pe": ("bmm", "cmm"), "act": ("ccopy", "decay", "gate"), "pool": ("out", "added"),
              "dve": ("clip", "logsum", "logtail", "src", "inp", "state", "tail")}
        s_zero, s_pads, s_skip, s_flag, s_count = (
            sem(n) for n in ("scan_zero", "scan_pads", "scan_skip", "scan_flag", "scan_count"))
        LAST = len(RANGES) - 1

        def tiles_before(r):
            return sum(B // gb * NS for _, _, gb in RANGES[:r])

        def scan_starts(eng, who):
            for n in OF[who]:
                eng.sem_inc(S[n], 2)

        def until(eng, name, k):
            eng.wait_ge(S[name], k + 3)

        class Tile:

            def __init__(self, r, n, g, s):
                self.t0, self.tl, self.gb = RANGES[r]
                self.carried, self.carries = r > 0, r < LAST
                self.k = tiles_before(r) + n * (B // self.gb) + g
                self.g, self.n, self.s = g, n, s
                self.segs = self.gb * NH

            def flat(self, buf):
                return buf[:, 0:self.segs * (1 + self.tl)]

            def seg(self, buf):
                return self.flat(buf).rearrange("p (s t) -> p s t", s=self.segs)

            def body(self, buf):
                return self.seg(buf)[:, :, 1:]

            def body_bh(self, buf):
                return self.seg(buf).rearrange("p (b h) t -> p b h t", h=NH)[:, :, :, 1:]

            def array(self, arr):
                return arr[:, bass.ds(self.g * self.gb, self.gb), :, self.t0:self.t0 + self.tl]

            def rows_bc(self):
                return bc[:, bass.ds(self.g * self.gb, self.gb), self.t0:self.t0 + self.tl]

            def per_token(self, ap):
                return ap[:, 0:self.gb * self.tl].rearrange("p (b o t) -> p b o t", b=self.gb, o=1).to_broadcast(
                    [P, self.gb, NH, self.tl])

            def carry(self, arr):
                return arr[:, bass.ds(self.n, 1), bass.ds(self.g * self.segs, self.segs)].rearrange("p o s -> p (o s)")

        def tiles(eng, who, before_range, turn):
            def run(r, tile, count):
                turn(tile(0, 0), None)
                if count > 2:
                    with eng.Fori(0, count // 2 - 1) as i:
                        for s in range(2):
                            turn(tile(i * 2 + s + 1, 1 - s), tile(i * 2 + s, s))
                turn(tile(count - 1, 1), tile(count - 2, 0))
                turn(None, tile(count - 1, 1))

            before_range(0)
            run(0, lambda n, s: Tile(0, n, 0, s), NS)
            for r in range(1, len(RANGES)):
                before_range(r)
                eng.wait_ge(s_flag, 2 * r)
                groups = B // RANGES[r][2]

                def skip(states):
                    eng.drain().then_inc(s_skip, 1)
                    for name in OF[who]:
                        eng.sem_inc(S[name], states * groups)

                with eng.Fori(0, NS // 4) as q:
                    with eng.If(eng.value_load(alive4[r][0:1, bass.ds(q, 1)], min_val=0, max_val=P) != 0):
                        with eng.Fori(0, 4) as j:
                            n = eng.snap(q * 4 + j)
                            with eng.If(eng.value_load(alive[r][0:1, bass.ds(n, 1)], min_val=0, max_val=P) != 0):
                                run(r, lambda g, s: Tile(r, n, g, s), groups)
                            with eng.Else():
                                skip(1)
                    with eng.Else():
                        skip(4)

        def scan_pe(pe):
            scan_starts(pe, "pe")

            def count_dead(r):
                if r:
                    pe.wait_ge(s_count, 2 * r - 1)
                    nc.tensor.matmul(bank[4][0:1, 0:NS], ones_c, s_dead, start=True, stop=True).then_inc(s_count, 1)

            def spread(x):
                n = x.gb * x.tl
                until(pe, "src", x.k - 2)
                nc.tensor.matmul(bank[x.s][:, 0:n], sel[:, bass.ds(x.n, 1), :].rearrange("p o m -> p (o m)"),
                                 x.rows_bc(), start=True, stop=True).then_inc(S["bmm"], 1)
                until(pe, "ccopy", x.k - 2)
                nc.tensor.matmul(bank[2 + x.s][:, 0:n],
                                 sel[:, bass.ds(x.n + NS, 1), :].rearrange("p o m -> p (o m)"),
                                 x.rows_bc(), start=True, stop=True).then_inc(S["cmm"], 1)
            tiles(pe, "pe", count_dead, lambda h, t: h and spread(h))

        def scan_act(act):
            scan_starts(act, "act")
            act.wait_ge(h_saved, 16)

            def head(x):
                until(act, "clip", x.k)
                until(act, "state", x.k - 2)
                nc.scalar.activation(x.body(s_a[x.s]), x.body(s_u), ACT.Exp).then_inc(S["decay"], 1)
                until(act, "logtail" if x.carries else "logsum", x.k)
                nc.scalar.activation(x.flat(s_L[x.s]), x.flat(s_L[x.s]), ACT.Tanh, scale=0.5,
                                     bias=vec[:, V_LE:V_LE + 1]).then_inc(S["gate"], 1)
                until(act, "cmm", x.k)
                until(act, "out", x.k - 2)
                nc.scalar.copy(s_c[x.s][:, 0:x.gb * x.tl], bank[2 + x.s][:, 0:x.gb * x.tl]).then_inc(S["ccopy"], 1)
            tiles(act, "act", nothing, lambda h, t: h and head(h))

        def scan_dve(dve):
            scan_starts(dve, "dve")
            dve.wait_ge(h_saved, 16)

            def before_range(r):
                t = Tile(r, 0, 0, 0)
                if r:
                    until(dve, "added", t.k - 1)
                    nc.vector.tensor_reduce(s_max, carryL, AX.X, ALU.max).then_inc(s_zero, 1)
                    dve.wait_ge(s_zero, 8 * r + 1)
                    nc.vector.tensor_scalar(s_dead, s_max, S_GONE, None, ALU.is_le).then_inc(s_count, 1)
                    dve.wait_ge(s_count, 2 * r)
                    nc.vector.tensor_scalar(alive[r], bank[4][0:1, 0:NS], -1.0, float(P), ALU.mult,
                                            ALU.add).then_inc(s_flag, 1)
                    dve.wait_ge(s_flag, 2 * r - 1)
                    nc.vector.tensor_reduce(alive4[r], alive[r].rearrange("p (q j) -> p q j", j=4), AX.X,
                                            ALU.max).then_inc(s_flag, 1)
                nc.vector.memset(t.flat(s_mask), 1.0).then_inc(s_zero, 1)
                dve.wait_ge(s_zero, 8 * r + (2 if r else 1))
                for buf in (s_mask, *s_a, s_u, *s_w):
                    nc.vector.memset(t.seg(buf)[:, :, 0:1], 0.0).then_inc(s_zero, 1)
                if not r:
                    nc.vector.memset(ones_c, 1.0).then_inc(s_zero, 1)
                dve.wait_ge(s_zero, 8 * r + 8)

            def clip(x):
                until(dve, "decay", x.k - 1)
                until(dve, "logsum", x.k - 1)
                if x.carried:
                    nc.vector.tensor_scalar(x.seg(s_u)[:, :, 0:1], x.carry(carryL).rearrange(
                        "p (s o) -> p s o", o=1), 1.0, None, ALU.mult).then_inc(s_pads, 1)
                for h in range(NH):
                    a = nc.vector.tensor_scalar(x.body_bh(s_u)[:, :, h, :], x.array(dt)[:, :, h, :],
                                                negA[:, h, bass.ds(x.n, 1)], LOG_FLOOR, ALU.mult, ALU.max)
                a.then_inc(S["clip"], 1)

            def log_sum(x):
                until(dve, "clip", x.k)
                until(dve, "inp", x.k - 2)
                nc.vector.tensor_tensor_scan(x.flat(s_L[x.s]), x.flat(s_mask), x.flat(s_u), 0.0, ALU.mult,
                                             ALU.add).then_inc(S["logsum"], 1)

            def log_carry(x):
                if x.carries:
                    until(dve, "logsum", x.k)
                    nc.vector.tensor_scalar(x.carry(carryL), x.seg(s_L[x.s])[:, :, x.tl:].rearrange(
                        "p s o -> p (s o)"), 1.0, None, ALU.mult).then_inc(S["logtail"], 1)

            def source(x):
                until(dve, "bmm", x.k)
                until(dve, "added", x.k - 2)
                nc.vector.tensor_tensor(x.body_bh(s_w[x.s]), x.array(dtx), x.per_token(bank[x.s]),
                                        ALU.mult).then_inc(S["src"], 1)
                if x.carried:
                    nc.vector.tensor_scalar(x.seg(s_w[x.s])[:, :, 0:1], x.carry(carryH).rearrange(
                        "p (s o) -> p s o", o=1), 1.0, None, ALU.mult).then_inc(s_pads, 1)

            def gated(x):
                until(dve, "gate", x.k)
                until(dve, "src", x.k)
                nc.vector.scalar_tensor_tensor(x.body(s_w[x.s]), x.body(s_L[x.s]), 1.0, x.body(s_w[x.s]), ALU.add,
                                               ALU.mult).then_inc(S["inp"], 1)

            def state(x):
                until(dve, "decay", x.k)
                until(dve, "inp", x.k)
                nc.vector.tensor_tensor_scan(x.flat(s_w[x.s]), x.flat(s_a[x.s]), x.flat(s_w[x.s]), 0.0, ALU.mult,
                                             ALU.add).then_inc(S["state"], 1)

            def state_carry(x):
                if x.carries:
                    until(dve, "state", x.k)
                    nc.vector.tensor_scalar(x.carry(carryH), x.seg(s_w[x.s])[:, :, x.tl:].rearrange(
                        "p s o -> p (s o)"), 1.0, None, ALU.mult).then_inc(S["tail"], 1)

            def turn(h, t):
                for of_h, of_t in ((clip, source), (log_sum, gated), (log_carry, state)):
                    if h:
                        of_h(h)
                    if t:
                        of_t(t)
                if t:
                    state_carry(t)
            tiles(dve, "dve", before_range, turn)

        def scan_pool(pool):
            scan_starts(pool, "pool")

            def sum_up(x):
                until(pool, "tail" if x.carries else "state", x.k)
                until(pool, "ccopy", x.k)
                apart(pool)
                nc.gpsimd.tensor_tensor(x.body_bh(s_w[x.s]), x.body_bh(s_w[x.s]), x.per_token(s_c[x.s]),
                                        ALU.mult).then_inc(S["out"], 1)
                until(pool, "out", x.k)
                until(pool, "added", x.k - 1)
                apart(pool)
                nc.gpsimd.tensor_tensor(x.array(xs), x.array(xs), x.body_bh(s_w[x.s]), ALU.add).then_inc(S["added"], 1)
            tiles(pool, "pool", nothing, lambda h, t: t and sum_up(t))

        (z_mm, z_exp, z_log, z_sig, z_gate, yz_ok, o_mm, o_ok, aff_ok, h2_ok, lg_mm, lg_ev, h_back) = (
            sem(n) for n in ("z_mm", "z_exp", "z_log", "z_sig", "z_gate", "yz_ok", "o_mm", "o_ok", "aff_ok", "h2_ok",
                             "lg_mm", "lg_ev", "h_back"))
        m = Scratch()
        zsig = m.two(NH, T)
        lg = view(dt[:, :, :, :].rearrange("p b h t -> p (b h t)"), B * T, B, T, rows=E)

        norm1, norm2 = Norm("norm_blk", oT, oT, o_ok, m), Norm("norm_moe", hT, xn, h2_ok, m)
        norm1.turn, norm2.turn = (norm2, 2), (norm1, -1)

        def block_pe(pe):
            def z(b, s):
                freed(pe, z_gate, b, 2)
                for h in range(NH):
                    mm = nc.tensor.matmul(bank[2 * s + h][:, 0:T], inw_s[:, (NH + h) * P:(NH + h + 1) * P],
                                          row(xn, b), start=True, stop=True)
                mm.then_inc(z_mm, 1)

            def outproj(b, s):
                pe.wait_ge(yz_ok, b + 1)
                freed(pe, o_ok, b, 1)
                for k in range(NH):
                    mm = nc.tensor.matmul(bank[4][:, 0:T], outw_s[:, k, :], both(dtx, b)[:, k, :],
                                          start=(k == 0), stop=(k == NH - 1))
                mm.then_inc(o_mm, 1)

            def logits(b, s):
                pe.wait_ge(norm2.out, b + 1)
                freed(pe, lg_ev, b, 1)
                nc.tensor.matmul(bank[7][0:E, 0:T], wr_s[:, :], row(xn, b), start=True, stop=True).then_inc(lg_mm, 1)
            pipelined(pe, (norm1.pe_mean, 5), (outproj, 4), (z, 0), (norm2.pe_mean, 6), (norm1.pe_var, 5), (logits, 7), (norm2.pe_var, 6))

        def block_act(act):
            nc.scalar.preload_act_table_set("natural_log_exp_and_others")

            def z_e(b, s):
                act.wait_ge(z_mm, b + 1)
                freed(act, z_gate, b, 2)
                for h in range(NH):
                    a = nc.scalar.activation(zsig[s][:, h, :], bank[2 * s + h][:, 0:T], ACT.Exp, scale=-1.0,
                                             bias=nvec[:, NH + h:NH + h + 1])
                a.then_inc(z_exp, 1)

            def z_l(b, s):
                act.wait_ge(z_exp, b + 1)
                nc.scalar.activation(zsig[s], zsig[s], ACT.Ln, bias=1.0).then_inc(z_log, 1)

            def z_s(b, s):
                act.wait_ge(z_log, b + 1)
                nc.scalar.activation(zsig[s], zsig[s], ACT.Exp, scale=-1.0).then_inc(z_sig, 1)

            def logits(b, s):
                act.wait_ge(lg_mm, b + 1)
                nc.scalar.copy(row(lg, b), bank[7][0:E, 0:T]).then_inc(lg_ev, 1)
            pipelined(act, (norm1.act_square, 5), (z_s, 1), (z_e, 0), (norm2.act_square, 6), (norm1.act_rstd, 5), (z_l, 0), (logits, 7), (norm2.act_rstd, 6))

        def block_dve(dve):
            def gate(b, s):
                dve.wait_ge(z_sig, b + 1)
                for h in range(NH):
                    a = nc.vector.scalar_tensor_tensor(both(dtx, b)[:, h, :], bank[2 * s + h][:, 0:T],
                                                       vec[:, V_INB + NH + h:V_INB + NH + h + 1], zsig[s][:, h, :],
                                                       ALU.add, ALU.mult)
                a.then_inc(z_gate, 1)

            def affine(b, s):
                dve.wait_ge(norm1.out, b + 1)
                nc.vector.tensor_scalar(row(oT, b), row(oT, b), vec[:, V_LNG:V_LNG + 1], vec[:, V_LNB:V_LNB + 1],
                                        ALU.mult, ALU.add).then_inc(aff_ok, 1)

            def residual(b, s):
                dve.wait_ge(o_mm, b + 1)
                nc.vector.scalar_tensor_tensor(row(oT, b), bank[4][:, 0:T], vec[:, V_OUTB:V_OUTB + 1],
                                               row(xn, b), ALU.add, ALU.add).then_inc(o_ok, 1)
            pipelined(dve, (norm1.dve_scale, 6), (affine, 6), (gate, 2), (norm1.dve_center, 5), (residual, 4), (norm2.dve_center, 6), (norm2.dve_scale, 7))

        def block_pool(pool):
            def add(b, s):
                pool.wait_ge(aff_ok, b + 1)
                apart(pool)
                nc.gpsimd.tensor_tensor(row(hT, b), row(hT, b), row(oT, b), ALU.add).then_inc(h2_ok, 1)

            def gate_y(b, s):
                pool.wait_ge(z_gate, b + 1)
                apart(pool)
                nc.gpsimd.tensor_tensor(both(dtx, b), both(dtx, b), both(xs, b), ALU.mult).then_inc(yz_ok, 1)
            pool.wait_ge(h_back, 16)
            pipelined(pool, (add, 6), (gate_y, 2))

        bigx = xs[:, :, :, :].rearrange("p b h t -> p (b h t)")
        bigd = dt[:, :, :, :].rearrange("p b h t -> p (b h t)")
        bigy = dtx[:, :, :, :].rearrange("p b h t -> p (b h t)")
        lg_moved, rt_thr, rt_pe, rt_dve, rt_act, place_in, place_ok, b2_in, w_in = (
            sem(n) for n in ("lg_moved", "rt_thr", "rt_pe", "rt_dve", "rt_act",
                             "place_in", "place_ok", "b2_in", "w_in"))
        lgr = view(bigx, 0, T)
        prob, flag, pick, ones_t = (view(bigx, T * i, T) for i in (1, 2, 3, 4))
        slotI = view(bigx, T * 5, T, dtype=I32)
        sm = view(bigx, T * 6, 32)
        smi = sm.bitcast(I32)
        rowe = view(bigx, T * 6 + 32, E, rows=1)
        rowx = view(bigx, T * 6 + 32 + E, P, rows=1)
        C_MAX, C_NEG, C_SUM, C_INV, C_CNT, C_GT, C_EQ = range(7)
        C_CAND, C_COUNTS, C_THR = 8, 12, 19

        m = Scratch()
        tin = {"x": m.take(UNIT), "h": m.take(UNIT)}
        trow = {"x": m.take(TPU, P), "h": m.take(TPU, P)}
        gath = [m.take(TPU, P), *trow.values()]
        xe = m.two(UNIT)
        place = m.take(E, KB * B, SETS, dtype=BF16)
        tokT = {n: m.take(KB, P) for n in ("lo", "hi", "w")}
        hot_hi = m.take(KB * B, E, dtype=BF16)
        found = m.take(P, rows=SETS * E)
        chosen = m.take(2, CAP // P)
        idx = m.take(E, CAP // P, dtype=I32)
        hot_lo = [view(bigy, i * KB * B * P // 2, KB * B, P, dtype=BF16) for i in range(2)]
        told = [view(bigy, KB * B * P + i * KB * B * SETS * 4, KB * B, SETS, 8, dtype=BF16) for i in range(2)]
        hid = [view(bigx, 2600 + i * FT * UNIT, FT, UNIT) for i in range(2)]
        oute = [view(bigx, 2600 + (2 * FT + i) * UNIT, TPU, P) for i in range(2)]
        weight = view(bigx, 2600 + (2 * FT + 2) * UNIT, E, CAP // P)
        b2_s = view(xn[:, :, :].rearrange("p b t -> p (b t)"), 0, E, P)
        w1_s = view(bigd, 0, E, FT * P)
        w2_s = view(bigd, E * FT * P, E, FT * P)
        assert CAP // P == 8 and B * T % UNIT == 256

        def col(c):
            return sm[:, c:c + 1]

        def coli(c):
            return smi[:, c:c + 1]

        def route_sync(sp):
            for e in range(E):
                sp.dma_start(lgr[e * B:(e + 1) * B, :], lg[e:e + 1, :, :]).then_inc(lg_moved, 16)

        NGA = NG + 1
        EARLY_G = 1
        t_cp, t_mm, t_ev, t_st = ({n: sem(f"rows_{w}_{n}") for n in "xh"} for w in ("cp", "mm", "ev", "st"))
        source = {"x": xn[:, :, :].rearrange("p b t -> p (b t)"), "h": work[:, 0:B * T]}
        target = {"x": x_rows, "h": out}

        def group_cp(pool, i, n=UNIT):
            for a in "xh":
                if not (isinstance(i, int) and i == 0):
                    pool.wait_ge(t_mm[a], i)
                    apart(pool)
                nc.gpsimd.tensor_copy(tin[a][:, 0:n], source[a][:, bass.ds(i * UNIT, n)]).then_inc(t_cp[a], 1)

        def group_mm(pe, a, i, n=UNIT):
            pe.wait_ge(t_cp[a], i + 1)
            if not (isinstance(i, int) and i == 0):
                pe.wait_ge(t_ev[a], i)
            bk = bank[2 if a == "x" else 3]
            for j in range(n // P):
                t = nc.tensor.transpose(bk[:, j * P:(j + 1) * P], tin[a][:, j * P:(j + 1) * P], ident[:, :])
            t.then_inc(t_mm[a], 1)

        def group_ev(act, i, n=UNIT):
            for a in "xh":
                act.wait_ge(t_mm[a], i + 1)
                if not (isinstance(i, int) and i == 0):
                    act.wait_ge(t_st[a], 16 * i)
                bk = bank[2 if a == "x" else 3]
                nc.scalar.copy(trow[a][:, 0:n // P, :], bk[:, 0:n].rearrange("p (j c) -> p j c", c=P)).then_inc(
                    t_ev[a], 1)

        def group_store(sp, i, n=UNIT):
            for a in "xh":
                sp.wait_ge(t_ev[a], i + 1)
                sp.dma_start(target[a][bass.ds(i * UNIT, n), :].rearrange("(j p) c -> p j c", p=P),
                             trow[a][:, 0:n // P, :]).then_inc(t_st[a], 16)

        def rows_pool(pool):
            with pool.Fori(0, NG) as i:
                group_cp(pool, i)
            group_cp(pool, NG, B * T - NG * UNIT)

        def rows_sync(sp):
            with sp.Fori(0, NG) as i:
                group_store(sp, i)
            group_store(sp, NG, B * T - NG * UNIT)

        R_BITS = 8
        R_END = R_BITS + 5 * NSTEP

        def route_pe(pe):
            n = [0]

            def mm(out_, lhsT, rhs, ve, ac=0):
                pe.wait_ge(rt_dve, ve)
                if ac:
                    pe.wait_ge(rt_act, ac)
                n[0] += 1
                nc.tensor.matmul(out_, lhsT, rhs, start=True, stop=True).then_inc(rt_pe, 1)
            for i in range(EARLY_G):
                for a in "xh":
                    group_mm(pe, a, i)
            pe.wait_ge(rt_dve, 2)
            nc.tensor.transpose(bank[4][0:1, 0:P], col(C_MAX), ident[:, :]).then_inc(rt_pe, 1)
            mm(bank[5][:, 0:1], rowx[:, :], ident[0:1, 0:1], 4)
            mm(bank[6][:, 0:1], group[:, :], col(C_SUM), 5, 1)

            def count(i):
                pe.wait_ge(rt_dve, i * 5 + (R_BITS + 4))
                nc.tensor.matmul(bank[7][:, 0:WAYS - 1], group[:, :], sm[:, C_COUNTS:C_COUNTS + WAYS - 1], start=True,
                                 stop=True).then_inc(rt_pe, 1)
            assert NSTEP == 2 * (NG - EARLY_G) + 1
            with pe.Fori(0, NG - EARLY_G) as i:
                count(i * 2)
                group_mm(pe, "x", i + EARLY_G)
                count(i * 2 + 1)
                group_mm(pe, "h", i + EARLY_G)
            for a in "xh":
                group_mm(pe, a, NG, B * T - NG * UNIT)
            count(NSTEP - 1)
            mm(bank[4][:, 0:1], group[:, :], col(C_GT), R_END + 2)
            mm(bank[5][:, 0:1], below[:, :], col(C_EQ), R_END + 4)
            mm(bank[6][:, 0:1], below[:, :], col(C_CNT), R_END + 10)
            pe.wait_ge(t_ev["x"], NGA)
            pe.wait_ge(t_ev["h"], NGA)
            for j, (src, ve) in enumerate(((prob, R_END + 10), (pick, R_END + 15), (flag, R_END + 17))):
                pe.wait_ge(rt_dve, ve)
                for k in range(KB):
                    w = min(P, T - k * P)
                    t = nc.tensor.transpose(bank[j][0:w, k * P:(k + 1) * P], src[:, k * P:k * P + w], ident[:, :])
                t.then_inc(rt_pe, 1)

        RT_SLOTS = 3 + NSTEP + 3

        def route_act(act):
            for i in range(EARLY_G):
                group_ev(act, i)
            act.wait_ge(rt_dve, 5)
            nc.scalar.activation(prob, lgr, ACT.Exp, bias=col(C_NEG), accum_out=col(C_SUM)).then_inc(rt_act, 1)
            nc.scalar.preload_act_table_set("gelu_and_others")
            with act.Fori(EARLY_G, NG) as i:
                group_ev(act, i)
            group_ev(act, NG, B * T - NG * UNIT)

        def route_dve(dve):
            n = [0]

            def did(ins):
                n[0] += 1
                ins.then_inc(rt_dve, 1)
                dve.wait_ge(rt_dve, n[0])
            did(nc.vector.memset(ones_t, 1.0))
            dve.wait_ge(lg_moved, 16 * E)
            did(nc.vector.tensor_reduce(col(C_MAX), lgr, AX.X, ALU.max))
            dve.wait_ge(rt_pe, 1)
            did(nc.vector.tensor_reduce(rowe, bank[4][0:1, 0:P].rearrange("p (e b) -> p e b", e=E), AX.X,
                                        ALU.max))
            did(nc.vector.tensor_copy(rowx.rearrange("p (e b) -> p e b", e=E),
                                      rowe.rearrange("p (e o) -> p e o", o=1).to_broadcast([1, E, B])))
            dve.wait_ge(rt_pe, 2)
            did(nc.vector.tensor_scalar(col(C_NEG), bank[5][:, 0:1], -1.0, None, ALU.mult))
            dve.wait_ge(rt_pe, 3)
            did(nc.vector.reciprocal(col(C_INV), bank[6][:, 0:1]))
            did(nc.vector.tensor_scalar(prob, prob, col(C_INV), None, ALU.mult))
            did(nc.vector.memset(coli(C_THR), 0))
            assert n[0] == R_BITS
            PER = 5

            def step(i):
                at = i * 5 + R_BITS
                nc.vector.tensor_tensor(smi[:, C_CAND:C_CAND + 3], coli(C_THR).to_broadcast([P, 3]),
                                        steps[:, bass.ds(i, 1), :].rearrange("p o w -> p (o w)"),
                                        ALU.bitwise_or).then_inc(rt_dve, 1)
                dve.wait_ge(rt_dve, at + 1)
                for w in range(3):
                    nc.vector.tensor_scalar((flag, pick, lgr)[w], prob, col(C_CAND + w), None, ALU.is_ge, ALU.add,
                                            accum_out=col(C_COUNTS + w)).then_inc(rt_dve, 1)
                dve.wait_ge(rt_pe, i + 4)
                nc.vector.scalar_tensor_tensor(sm[:, C_THR - 3:C_THR], bank[7][:, 0:3], float(CAP),
                                               sm[:, C_CAND:C_CAND + 3], ALU.is_ge, ALU.mult).then_inc(rt_dve, 1)
                dve.wait_ge(rt_dve, at + 5)
                nc.vector.tensor_reduce(col(C_THR), sm[:, C_THR - 3:C_THR + 1], AX.X, ALU.max).then_inc(rt_thr, 1)
                dve.wait_ge(rt_thr, i + 1)
            with dve.Fori(0, NSTEP // PER) as i:
                for j in range(PER):
                    step(i * PER + j)
            n[0] += 5 * NSTEP
            did(nc.vector.tensor_scalar(flag, prob, col(C_THR), None, ALU.is_gt))
            did(nc.vector.tensor_reduce(col(C_GT), flag, AX.X, ALU.add))
            did(nc.vector.tensor_scalar(lgr, prob, col(C_THR), None, ALU.is_equal))
            did(nc.vector.tensor_reduce(col(C_EQ), lgr, AX.X, ALU.add))
            did(nc.vector.tensor_tensor_scan(pick, ones_t, lgr, 0.0, ALU.mult, ALU.add))
            dve.wait_ge(rt_pe, 3 + NSTEP + 2)
            did(nc.vector.tensor_scalar(pick, pick, bank[5][:, 0:1], bank[4][:, 0:1], ALU.add, ALU.add))
            did(nc.vector.tensor_scalar(pick, pick, float(CAP), None, ALU.is_le))
            did(nc.vector.tensor_tensor(pick, pick, lgr, ALU.mult))
            did(nc.vector.tensor_tensor(pick, pick, flag, ALU.add))
            did(nc.vector.tensor_reduce(col(C_CNT), pick, AX.X, ALU.add))
            did(nc.vector.tensor_tensor_scan(flag, ones_t, pick, 0.0, ALU.mult, ALU.add))
            did(nc.vector.scalar_tensor_tensor(flag, pick, -2.0 * CAP, flag, ALU.mult, ALU.add))
            dve.wait_ge(rt_pe, RT_SLOTS)
            did(nc.vector.tensor_scalar(slotI, flag, bank[6][:, 0:1], 2.0 * CAP - 1, ALU.add, ALU.add))
            did(nc.vector.tensor_scalar(lgr.bitcast(I32), slotI, P - 1, None, ALU.bitwise_and))
            did(nc.vector.tensor_copy(pick, lgr.bitcast(I32)))
            did(nc.vector.tensor_scalar(slotI, slotI, 7, None, ALU.logical_shift_right))
            did(nc.vector.tensor_copy(flag, slotI))
            assert n[0] == R_END + 17
            assert len(tokT) == 3
            for name, a in tokT.items():
                did(nc.vector.memset(a[:, KB - 1, :], 2.0 * CAP / P if name == "hi" else 0.0))
            w = T - (KB - 1) * P
            for j, a in enumerate((tokT["w"], tokT["lo"], tokT["hi"])):
                dve.wait_ge(rt_pe, RT_SLOTS + 1 + j)
                did(nc.vector.tensor_copy(a[:, 0:KB - 1, :], bank[j][:, 0:(KB - 1) * P].rearrange(
                    "p (k c) -> p k c", c=P)))
                did(nc.vector.tensor_copy(a[0:w, KB - 1, :], bank[j][0:w, (KB - 1) * P:KB * P]))

        def weights_pool(pool):
            wT = tokT["w"]
            pool.wait_ge(place_in, 16)
            pool.wait_ge(rt_dve, R_END + 22)
            n = 0
            for i in range(3):
                for k in range(KB):
                    nc.gpsimd.tensor_copy(
                        place[:, :, k * B:(k + 1) * B, 3 + i:4 + i].rearrange("p e b o -> p e (b o)"),
                        wT[:, k, :].rearrange("p (e b) -> p e b", e=E)).then_inc(place_ok, 1)
                if i < 2:
                    pool.wait_ge(place_ok, n + KB)
                    for k in range(KB):
                        part = place[:, :, k * B:(k + 1) * B, 3 + i:4 + i].rearrange("p e b o -> p e (b o)")
                        nc.gpsimd.tensor_tensor(wT[:, k, :].rearrange("p (e b) -> p e b", e=E),
                                                wT[:, k, :].rearrange("p (e b) -> p e b", e=E), part,
                                                ALU.subtract).then_inc(place_ok, 1)
                    n += 2 * KB
                    pool.wait_ge(place_ok, n)

        C = {n: sem(f"slot_{n}") for n in ("hi", "lo", "told", "mm", "cp", "tr", "sum", "idx")}
        M = {n: sem(f"moe_{n}") for n in ("tr", "xe", "hid", "gelu", "out", "bias", "scaled")}
        gathered = [sem(f"gathered{i}") for i in range(3)]
        scattered = [sem(f"scattered{i}") for i in range(2)]

        def hot_dve(dve, e):
            s = e % 2
            if e >= 2:
                dve.wait_ge(C["mm"], e - 1)
            if e:
                dve.wait_ge(C["told"], e)

            def per_tile(a, w):
                return a[:, :, e * B:(e + 1) * B].rearrange("p k (b o) -> p k b o", o=1).to_broadcast([P, KB, B, w])

            def over_tiles(w):
                return lowx[:, 0:w].rearrange("p (k b w) -> p k b w", k=1, b=1).to_broadcast([P, KB, B, w])
            nc.vector.tensor_tensor(hot_hi.rearrange("p (k b) w -> p k b w", k=KB), per_tile(tokT["hi"], 8),
                                    over_tiles(8), ALU.is_equal).then_inc(C["hi"], 1)
            for k in range(KB):
                nc.vector.tensor_tensor(hot_lo[s][:, k * B:(k + 1) * B, :], per_tile(tokT["lo"], P)[:, k, :, :],
                                        over_tiles(P)[:, k, :, :], ALU.is_equal).then_inc(C["lo"], 1)
            dve.wait_ge(C["hi"], e + 1)
            dve.wait_ge(place_ok, 5 * KB)
            nc.vector.tensor_tensor(
                told[s],
                hot_hi.rearrange("p t (o w) -> p t o w", o=1).to_broadcast([P, KB * B, SETS, 8]),
                place[:, e, :, :].rearrange("p t (s o) -> p t s o", o=1).to_broadcast([P, KB * B, SETS, 8]),
                ALU.mult).then_inc(C["told"], 1)

        def slots_pe(pe, e):
            s = e % 2
            pe.wait_ge(C["lo"], KB * (e + 1))
            pe.wait_ge(C["told"], e + 1)
            if e:
                pe.wait_ge(C["sum"], e)
            for t in range(KB * B):
                mm = nc.tensor.matmul(bank[7][0:SETS * 8, 0:P], told[s][:, t, :, :].rearrange("p s w -> p (s w)"),
                                      hot_lo[s][:, t, :], start=(t == 0), stop=(t == KB * B - 1))
            mm.then_inc(C["mm"], 1)

        def slots_tr(pe, e):
            pe.wait_ge(C["cp"], e + 1)
            nc.tensor.transpose(bank[7][:, P:P + SETS * 8], found, ident[0:SETS * 8, 0:SETS * 8]).then_inc(C["tr"], 1)

        def slots_act(act, e):
            act.wait_ge(C["mm"], e + 1)
            if e:
                act.wait_ge(C["tr"], e)
            nc.scalar.copy(found, bank[7][0:SETS * 8, 0:P]).then_inc(C["cp"], 1)

        def slots_dve(dve, e):
            dve.wait_ge(C["tr"], e + 1)
            parts = bank[7][:, P:P + SETS * 8].rearrange("p (v s w) -> p v w s", v=2, s=3)
            nc.vector.tensor_reduce(chosen, parts, AX.X, ALU.add).then_inc(C["sum"], 1)
            dve.wait_ge(C["sum"], e + 1)
            nc.vector.tensor_copy(idx[:, e, :], chosen[:, 0, :]).then_inc(C["idx"], 1)
            nc.vector.tensor_copy(weight[:, e, :], chosen[:, 1, :]).then_inc(C["idx"], 1)
            dve.wait_ge(C["idx"], 2 * e + 2)

        def tile_of(u, j):
            return u // 2, u % 2 * TPU + j

        def moe_pool(pool):
            def gather(u):
                if u % 2 == 0:
                    pool.wait_ge(C["idx"], u + 2)
                if u >= 3:
                    pool.wait_ge(M["tr"], u - 2)
                for j in range(TPU):
                    e, g = tile_of(u, j)
                    pool.indirect_dma_start(gath[u % 3][:, j, :], None, x_rows, bass.IndirectOffsetOnAxis(
                        ap=idx[:, e, g:g + 1], axis=0)).then_inc(gathered[u % 3], 16)

            def scatter(u):
                pool.wait_ge(M["scaled"], u + 1)
                if u % 2 == 0 and u:
                    for i in range(2):
                        pool.wait_ge(scattered[i], 16 * TPU * (u // 2))
                for j in range(TPU):
                    e, g = tile_of(u, j)
                    pool.indirect_dma_start(out, bass.IndirectOffsetOnAxis(ap=idx[:, e, g:g + 1], axis=0),
                                            oute[u % 2][:, j, :], None, compute_op=ALU.add).then_inc(
                                                scattered[u % 2], 16)
            pool.wait_ge(t_st["x"], 16 * NGA)
            pool.wait_ge(t_st["h"], 16 * NGA)
            gather(0)
            gather(1)
            for u in range(UNITS):
                if u + 2 < UNITS:
                    gather(u + 2)
                scatter(u)
            for i in range(2):
                pool.wait_ge(scattered[i], 16 * TPU * (UNITS // 2))

        def moe_pe(pe):
            def rows_to_channels(u):
                pe.wait_ge(gathered[u % 3], 16 * TPU * (u // 3 + 1))
                if u:
                    pe.wait_ge(M["xe"], u)
                for j in range(TPU):
                    t = nc.tensor.transpose(bank[4][:, j * P:(j + 1) * P], gath[u % 3][:, j, :], ident[:, :])
                t.then_inc(M["tr"], 1)

            def hidden(u):
                pe.wait_ge(M["xe"], u + 1)
                for f in range(FT):
                    if u:
                        pe.wait_ge(M["gelu"], FT * (u - 1) + f + 1)
                    nc.tensor.matmul(bank[f][:, 0:UNIT], w1_s[:, u // 2, f * P:(f + 1) * P], xe[u % 2], start=True,
                                     stop=True).then_inc(M["hid"], 1)

            def outputs(u):
                if u >= 2:
                    pe.wait_ge(M["bias"], u - 1)
                for j in range(TPU):
                    for f in range(FT):
                        if j == 0:
                            pe.wait_ge(M["gelu"], FT * u + f + 1)
                        mm = nc.tensor.matmul(bank[5 + u % 2][:, j * P:(j + 1) * P],
                                              hid[u % 2][:, f, j * P:(j + 1) * P],
                                              w2_s[:, u // 2, f * P:(f + 1) * P], start=(f == 0), stop=(f == FT - 1))
                mm.then_inc(M["out"], 1)
            slots_pe(pe, 0)
            slots_tr(pe, 0)
            pe.wait_ge(w_in, 32)
            rows_to_channels(0)
            for u in range(UNITS):
                e = (u + 3) // 2
                finds = (u % 2 == 1 or u == 0) and e < E
                hidden(u)
                if u + 1 < UNITS:
                    rows_to_channels(u + 1)
                if finds:
                    slots_pe(pe, e)
                    if u == 0:
                        slots_tr(pe, e)
                outputs(u)
                if finds and u:
                    slots_tr(pe, e)

        def moe_act(act):
            def channels(u):
                act.wait_ge(M["tr"], u + 1)
                if u >= 2:
                    act.wait_ge(M["hid"], FT * (u - 1))
                nc.scalar.copy(xe[u % 2], bank[4][:, 0:UNIT]).then_inc(M["xe"], 1)

            def gelu(u):
                if u >= 2:
                    act.wait_ge(M["out"], u - 1)
                for f in range(FT):
                    act.wait_ge(M["hid"], FT * u + f + 1)
                    nc.scalar.activation(hid[u % 2][:, f, :], bank[f][:, 0:UNIT], ACT.Gelu,
                                         bias=vec[:, V_B1 + u // 2 * FT + f:V_B1 + u // 2 * FT + f + 1]).then_inc(
                                             M["gelu"], 1)
            slots_act(act, 0)
            channels(0)
            for u in range(UNITS):
                e = (u + 3) // 2
                gelu(u)
                if u + 1 < UNITS:
                    channels(u + 1)
                if (u % 2 == 1 or u == 0) and e < E:
                    slots_act(act, e)

        def moe_dve(dve):
            def weigh(u):
                dve.wait_ge(M["out"], u + 1)
                if u >= 2:
                    dve.wait_ge(scattered[u % 2], 16 * TPU * (u // 2))
                nc.vector.tensor_tensor(
                    oute[u % 2], bank[5 + u % 2][:, 0:UNIT].rearrange("p (j c) -> p j c", c=P),
                    b2_s[:, u // 2:u // 2 + 1, :].to_broadcast([P, TPU, P]), ALU.add).then_inc(M["bias"], 1)
                dve.wait_ge(M["bias"], u + 1)
                for j in range(TPU):
                    e, g = tile_of(u, j)
                    ins = nc.vector.tensor_scalar(oute[u % 2][:, j, :], oute[u % 2][:, j, :],
                                                  weight[:, e, g:g + 1], None, ALU.mult)
                ins.then_inc(M["scaled"], 1)
            hot_dve(dve, 0)
            slots_dve(dve, 0)
            hot_dve(dve, 1)
            slots_dve(dve, 1)
            hot_dve(dve, 2)
            dve.wait_ge(b2_in, 16)
            for u in range(UNITS):
                if u % 2 == 0 and u and u // 2 + 2 < E:
                    hot_dve(dve, u // 2 + 2)
                weigh(u)
                if u % 2 == 1 and (u + 3) // 2 < E:
                    slots_dve(dve, (u + 3) // 2)

        @block.sync
        def _(sp):
            start_sync(sp)
            sp.wait_ge(tok_ev, B)
            sp.dma_start(h_save, hT).then_inc(h_saved, 16)
            sp.wait_ge(stage_done[1], 4)
            sp.dma_start(hT, h_save).then_inc(h_back, 16)
            sp.wait_ge(stage_done[2], 4)
            route_sync(sp)
            sp.dma_start(w1_s, w1).then_inc(w_in, 16)
            sp.wait_ge(lg_moved, 16 * E)
            sp.dma_start(w2_s, w2).then_inc(w_in, 16)
            sp.dma_start(place.rearrange("p e t s -> p (e t s)"), place_c).then_inc(place_in, 16)
            rows_sync(sp)
            sp.wait_ge(t_cp["x"], NGA)
            sp.dma_start(b2_s.rearrange("p e c -> p (e c)"), b2).then_inc(b2_in, 16)

        @block.tensor
        def _(pe):
            for k, stage in enumerate((start_pe, scan_pe, block_pe)):
                stage(pe)
                fence(pe, k)
            route_pe(pe)
            moe_pe(pe)

        @block.scalar
        def _(act):
            for k, stage in enumerate((start_act, scan_act, block_act)):
                stage(act)
                fence(act, k)
            route_act(act)
            moe_act(act)

        @block.vector
        def _(dve):
            for k, stage in enumerate((start_dve,
                                       scan_dve, block_dve)):
                stage(dve)
                fence(dve, k)
            route_dve(dve)
            moe_dve(dve)

        @block.gpsimd
        def _(pool):
            for k, stage in enumerate((start_pool, lambda e: (e.wait_ge(h_saved, 16), scan_pool(e)),
                                       block_pool)):
                stage(pool)
                fence(pool, k)
            rows_pool(pool)
            weights_pool(pool)
            moe_pool(pool)


def kernel(x, txt, L0_tok_W, L0_tok_b, L0_tok_cls_token, L0_tok_pos_emb, L0_attn_in_w, L0_attn_in_b, L0_attn_conv_w,
           L0_attn_conv_b, L0_attn_xp_w, L0_attn_xp_b, L0_attn_dt_w, L0_attn_dt_b, L0_attn_A_log, L0_attn_D_skip,
           L0_attn_out_w, L0_attn_out_b, L0_attn_ln_g, L0_attn_ln_b, L0_ffn_Wr, L0_ffn_W1, L0_ffn_b1, L0_ffn_W2,
           L0_ffn_b2):
    import ml_dtypes
    import numpy as np
    import concourse.bacc as bacc
    from concourse.bass_utils import run_bass_kernel_spmd

    f32 = np.float32

    def cols(v):
        return np.asarray(v).reshape(-1, P).T

    def halves(w):
        w = np.asarray(w)
        return w.reshape(-1, P, w.shape[1]).transpose(1, 0, 2)

    def const(v):
        return np.full((P, 1), v, f32)

    patches = np.asarray(x).reshape(B, 3, 11, 16, 13, 16).transpose(0, 3, 5, 1, 2, 4).reshape(B, KT, P, NPATCH)
    patches = np.pad(patches, ((0, 0), (0, 0), (0, 0), (1, 0)))
    tok_cols = np.zeros((3, TI), f32)
    tok_cols[0] = np.asarray(L0_tok_pos_emb).reshape(-1)
    tok_cols[1, 0] = 1
    tok_cols[2, 1:] = 1
    xpb = np.asarray(L0_attn_xp_b)
    sel = np.zeros((3, 32, 32, P), f32)
    for j in range(32):
        sel[:, j, j] = 0.5 if j < NS else 1
    q = np.arange(P)
    same = q[:, None] // B == q[None] // B
    bits = (1 << np.arange(NBITS - 1, -1, -1)).astype(np.int32)
    place = np.zeros((P, E, KB, B, SETS), f32)
    place[..., 0] = q[:, None, None, None]
    place[..., 1] = T * np.arange(B)
    place[..., 2] = P * np.arange(KB)[:, None]
    arrays = {
        "patches": patches.transpose(0, 2, 1, 3),
        "txt": np.asarray(txt).transpose(2, 0, 1),
        "tokw": halves(np.asarray(L0_tok_W).T),
        "tok_rows": np.stack([np.ones(P, f32), np.asarray(L0_tok_cls_token).reshape(-1), np.asarray(L0_tok_b)]),
        "tok_cols": tok_cols,
        "vecs": np.concatenate([
            cols(L0_attn_in_b), cols(L0_attn_conv_b), cols(xpb[2 * NS:]), cols(L0_attn_dt_b), cols(L0_attn_D_skip),
            cols(L0_attn_out_b), cols(L0_attn_ln_g), cols(L0_attn_ln_b), const(1e-5), const(LOG_EPS_HALF),
            cols(L0_ffn_b1)], axis=1),
        "inw": np.asarray(L0_attn_in_w).T,
        "convw": np.asarray(L0_attn_conv_w).reshape(NH, P, KC).transpose(1, 0, 2).reshape(P, NH * KC),
        "xpw": halves(np.asarray(L0_attn_xp_w)[:2 * NS].T),
        "xprow": halves(np.asarray(L0_attn_xp_w)[2 * NS:]),
        "xpb": xpb[:2 * NS].reshape(-1, 1),
        "dtw": halves(np.asarray(L0_attn_dt_w).T),
        "alog": halves(L0_attn_A_log),
        "outw": halves(np.asarray(L0_attn_out_w).T),
        "wr": np.asarray(L0_ffn_Wr),
        "w1": np.asarray(L0_ffn_W1).transpose(1, 0, 2),
        "w2": np.asarray(L0_ffn_W2).reshape(E, FT, P, P).transpose(2, 0, 1, 3).reshape(P, E, FT * P),
        "b2": np.broadcast_to(np.asarray(L0_ffn_b2).reshape(1, E * P), (P, E * P)),
        "ident_c": np.eye(P, dtype=f32),
        "sel_c": sel.reshape(96, 32, P).astype(ml_dtypes.bfloat16),
        "group_c": same.astype(f32),
        "below_c": (same & (q[:, None] < q[None])).astype(f32),
        "mean_c": np.full((P, P), 1 / P, f32),
        "iota_c": np.tile(np.arange(P), (P, 1)).astype(ml_dtypes.bfloat16),
        "place_c": place.reshape(P, -1).astype(ml_dtypes.bfloat16),
        "steps_c": np.tile(bits[1::2, None] * np.arange(1, WAYS, dtype=np.int32), (P, 1, 1)),
    }
    nc = bacc.Bacc("TRN2", target_bir_lowering=False, num_devices=1)
    ins, aps = {}, {}
    for name, a in arrays.items():
        ins[name + "_in"] = np.ascontiguousarray(a)
        aps[name] = nc.dram_tensor(name + "_in", a.shape, mybir.dt.from_np(a.dtype), kind="ExternalInput").ap()
    out = nc.dram_tensor("out", (B * T, P), F32, kind="ExternalOutput").ap()
    build_program(nc, **aps, out=out)
    r = run_bass_kernel_spmd(nc, [ins], core_ids=[0])
    return r.results[0]["out"].reshape(B, T, P)
```
